# Optimizing a Trainium2 kernel written in Bass

```python
import numpy as np
import jax
import jax.numpy as jnp

def _softmax(x, axis=-1):
    return jax.nn.softmax(x, axis=axis)

def _gelu(x):
    return jax.nn.gelu(x, approximate=True)

def _silu(x):
    return jax.nn.silu(x)

def _sigmoid(x):
    return jax.nn.sigmoid(x)

def _layernorm(x, axis=-1, eps=1e-05):
    m = jnp.mean(x, axis=axis, keepdims=True)
    v = jnp.var(x, axis=axis, keepdims=True)
    return (x - m) / jnp.sqrt(v + eps)

def _scatter_add(tgt, idx, src, axis=0):
    return tgt.at[idx].add(src)

def _segment_sum(src, seg, n):
    return jax.ops.segment_sum(src, seg, n)
kernel_name = 'mk_xattn_seq_d2_seqx_r8_2ecdf2'

def setup_inputs(seed: int=0):
    np.random.seed(seed)
    _w = jnp.asarray

    def _rec_inputs():
        import jax
        import jax.numpy as jnp
        _rk = jax.random.key(seed)
        x = -0.0002928 + 1 * jax.random.normal(jax.random.fold_in(_rk, 1), (64, 128, 128), jnp.float32)
        _lenS = 128 - jax.random.randint(jax.random.fold_in(_rk, 7), (64,), 0, max(1, 128 // 4) + 1, jnp.int32)
        _lenS2 = 77 - jax.random.randint(jax.random.fold_in(_rk, 8), (64,), 0, max(1, 77 // 4) + 1, jnp.int32)
        _ctx_1024P = jax.random.normal(jax.random.fold_in(_rk, 11), (64, 16, 128), jnp.float32)
        _ctx_1024c = jax.random.dirichlet(jax.random.fold_in(_rk, 511), 0.3 * jnp.ones((16,), jnp.float32), (64, 77))
        _ctx_1024t = jnp.einsum('bsk,bkd->bsd', _ctx_1024c, _ctx_1024P)
        _ctx_1024t = _ctx_1024t * jax.lax.rsqrt(jnp.mean(jnp.square(_ctx_1024t)) + 1e-12) * 0.953939
        ctx_1024 = -1.39393e-06 + 0.999914 * (_ctx_1024t + 0.3 * jax.random.normal(jax.random.fold_in(_rk, 611), (64, 77, 128), jnp.float32))
        _validS = jnp.arange(128)[None, :] < _lenS[:, None]
        _validS2 = jnp.arange(77)[None, :] < _lenS2[:, None]
        _causal = jnp.tril(jnp.ones((128, 128), dtype=bool))
        mask_Bx1xSxS2_ff0 = jnp.where(jnp.ones((64, 1, 128, 77), dtype=bool), 0.0, -1000000000.0).astype(jnp.float32)
        mask_1x1xSxS2_ff0 = jnp.where(jnp.ones((1, 1, 128, 77), dtype=bool), 0.0, -1000000000.0).astype(jnp.float32)
        mask_1xSxS2_bk1 = jnp.broadcast_to(_validS2[0:1, None, :], (1, 128, 77))
        return (x, ctx_1024, mask_Bx1xSxS2_ff0, mask_1x1xSxS2_ff0, mask_1xSxS2_bk1)
    x, ctx_1024, mask_Bx1xSxS2_ff0, mask_1x1xSxS2_ff0, mask_1xSxS2_bk1 = _rec_inputs()

    def _L0_xattn_setup():
        import jax, jax.numpy as jnp
        import numpy as np
        import math
        H, NH, NKV, HD, FF = (128, 16, 4, 64, 512)
        B, S = (2, 256)
        EPS, THETA = (1e-06, 10000.0)

        def _rmsnorm(x, w, eps=EPS):
            v = jnp.mean(x.astype(jnp.float32) ** 2, axis=-1, keepdims=True)
            return (x.astype(jnp.float32) * jax.lax.rsqrt(v + eps)).astype(x.dtype) * w

        def _rope_tables(seq_len, head_dim, theta=THETA):
            inv_freq = 1.0 / theta ** (jnp.arange(0, head_dim, 2, dtype=jnp.float32) / head_dim)
            freqs = jnp.arange(seq_len, dtype=jnp.float32)[:, None] * inv_freq[None, :]
            emb = jnp.concatenate([freqs, freqs], axis=-1)
            return (jnp.cos(emb), jnp.sin(emb))

        def _rotate_half(x):
            x1, x2 = jnp.split(x, 2, axis=-1)
            return jnp.concatenate([-x2, x1], axis=-1)

        def _apply_rope(x, cos, sin):
            return x * cos[None, None] + _rotate_half(x) * sin[None, None]
        key = jax.random.key(seed)
        ks = jax.random.split(key, 12)
        std = 0.02
        return {'hidden_states': jax.random.normal(ks[0], (B, S, H), jnp.float32), 'kv_states': jax.random.normal(ks[1], (B, S, H), jnp.float32), 'attention_mask': jnp.zeros((B, 1, S, S), jnp.float32), 'ln1_w': jnp.ones((H,), jnp.float32), 'ln2_w': jnp.ones((H,), jnp.float32), 'Wq': jax.random.normal(ks[2], (H, NH * HD), jnp.float32) * std, 'Wk': jax.random.normal(ks[3], (H, NKV * HD), jnp.float32) * std, 'Wv': jax.random.normal(ks[4], (H, NKV * HD), jnp.float32) * std, 'Wo': jax.random.normal(ks[5], (NH * HD, H), jnp.float32) * std, 'Wgate': jax.random.normal(ks[6], (H, FF), jnp.float32) * std, 'Wup': jax.random.normal(ks[7], (H, FF), jnp.float32) * std, 'Wdown': jax.random.normal(ks[8], (FF, H), jnp.float32) * std}
    _L0_xattn_all = _L0_xattn_setup()
    _L0_xattn_in = {k: v for k, v in _L0_xattn_all.items() if k in ('ln1_w', 'ln2_w', 'Wq', 'Wk', 'Wv', 'Wo', 'Wgate', 'Wup', 'Wdown')}
    del _L0_xattn_all

    def _L1_xattn_setup():
        import jax, jax.numpy as jnp
        import numpy as np
        B, Q, C, H, N, D, F = (1, 256, 256, 128, 16, 64, 512)
        R = Q + C
        EPS = 1e-12
        NEG = 1e+30

        def _layernorm(x, g, b):
            m = jnp.mean(x, axis=-1, keepdims=True)
            v = jnp.mean(jnp.square(x - m), axis=-1, keepdims=True)
            return (x - m) * jax.lax.rsqrt(v + EPS) * g + b

        def _rel_shift(x, klen):
            b, n, q, r = x.shape
            x = x.reshape(b, n, r, q)[:, :, 1:, :].reshape(b, n, q, r - 1)
            return x[:, :, :, :klen]
        key = jax.random.key(seed)
        ks = jax.random.split(key, 16)
        s = 0.02
        return dict(content_stream=jax.random.normal(ks[0], (B, Q, H), jnp.float32), content_mask=jnp.zeros((B, 1, Q, C), jnp.float32), context=jax.random.normal(ks[1], (B, C, H), jnp.float32), position_encoding=jax.random.normal(ks[2], (B, R, H), jnp.float32), content_bias=jax.random.normal(ks[3], (N, D), jnp.float32) * s, position_bias=jax.random.normal(ks[4], (N, D), jnp.float32) * s, segment_encoding=jax.random.normal(ks[5], (2, N, D), jnp.float32) * s, segment_matrix=jax.random.randint(ks[6], (B, Q, C), 0, 2).astype(bool), segment_bias=jax.random.normal(ks[7], (N, D), jnp.float32) * s, Wq=jax.random.normal(ks[8], (H, N, D), jnp.float32) * s, Wk=jax.random.normal(ks[9], (H, N, D), jnp.float32) * s, Wv=jax.random.normal(ks[10], (H, N, D), jnp.float32) * s, Wr=jax.random.normal(ks[11], (H, N, D), jnp.float32) * s, Wo=jax.random.normal(ks[12], (H, N, D), jnp.float32) * s, ln1_gamma=jnp.ones((H,), jnp.float32), ln1_beta=jnp.zeros((H,), jnp.float32), W1=jax.random.normal(ks[13], (H, F), jnp.float32) * s, b1=jnp.zeros((F,), jnp.float32), W2=jax.random.normal(ks[14], (F, H), jnp.float32) * s, b2=jnp.zeros((H,), jnp.float32), ln2_gamma=jnp.ones((H,), jnp.float32), ln2_beta=jnp.zeros((H,), jnp.float32))
    _L1_xattn_all = _L1_xattn_setup()
    _L1_xattn_in = {k: v for k, v in _L1_xattn_all.items() if k in ('position_encoding', 'content_bias', 'position_bias', 'segment_encoding', 'segment_bias', 'Wq', 'Wk', 'Wv', 'Wr', 'Wo', 'ln1_gamma', 'ln1_beta', 'W1', 'b1', 'W2', 'b2', 'ln2_gamma', 'ln2_beta')}
    del _L1_xattn_all
    return {'x': x, 'ctx_1024': ctx_1024, 'mask_Bx1xSxS2_ff0': mask_Bx1xSxS2_ff0, 'mask_1x1xSxS2_ff0': mask_1x1xSxS2_ff0, 'mask_1xSxS2_bk1': mask_1xSxS2_bk1, 'L0_xattn_ln1_w': _L0_xattn_in['ln1_w'], 'L0_xattn_ln2_w': _L0_xattn_in['ln2_w'], 'L0_xattn_Wq': _L0_xattn_in['Wq'], 'L0_xattn_Wk': _L0_xattn_in['Wk'], 'L0_xattn_Wv': _L0_xattn_in['Wv'], 'L0_xattn_Wo': _L0_xattn_in['Wo'], 'L0_xattn_Wgate': _L0_xattn_in['Wgate'], 'L0_xattn_Wup': _L0_xattn_in['Wup'], 'L0_xattn_Wdown': _L0_xattn_in['Wdown'], 'L1_xattn_position_encoding': _L1_xattn_in['position_encoding'], 'L1_xattn_content_bias': _L1_xattn_in['content_bias'], 'L1_xattn_position_bias': _L1_xattn_in['position_bias'], 'L1_xattn_segment_encoding': _L1_xattn_in['segment_encoding'], 'L1_xattn_segment_bias': _L1_xattn_in['segment_bias'], 'L1_xattn_Wq': _L1_xattn_in['Wq'], 'L1_xattn_Wk': _L1_xattn_in['Wk'], 'L1_xattn_Wv': _L1_xattn_in['Wv'], 'L1_xattn_Wr': _L1_xattn_in['Wr'], 'L1_xattn_Wo': _L1_xattn_in['Wo'], 'L1_xattn_ln1_gamma': _L1_xattn_in['ln1_gamma'], 'L1_xattn_ln1_beta': _L1_xattn_in['ln1_beta'], 'L1_xattn_W1': _L1_xattn_in['W1'], 'L1_xattn_b1': _L1_xattn_in['b1'], 'L1_xattn_W2': _L1_xattn_in['W2'], 'L1_xattn_b2': _L1_xattn_in['b2'], 'L1_xattn_ln2_gamma': _L1_xattn_in['ln2_gamma'], 'L1_xattn_ln2_beta': _L1_xattn_in['ln2_beta']}

def reference(x, ctx_1024, mask_Bx1xSxS2_ff0, mask_1x1xSxS2_ff0, mask_1xSxS2_bk1, L0_xattn_ln1_w, L0_xattn_ln2_w, L0_xattn_Wq, L0_xattn_Wk, L0_xattn_Wv, L0_xattn_Wo, L0_xattn_Wgate, L0_xattn_Wup, L0_xattn_Wdown, L1_xattn_position_encoding, L1_xattn_content_bias, L1_xattn_position_bias, L1_xattn_segment_encoding, L1_xattn_segment_bias, L1_xattn_Wq, L1_xattn_Wk, L1_xattn_Wv, L1_xattn_Wr, L1_xattn_Wo, L1_xattn_ln1_gamma, L1_xattn_ln1_beta, L1_xattn_W1, L1_xattn_b1, L1_xattn_W2, L1_xattn_b2, L1_xattn_ln2_gamma, L1_xattn_ln2_beta):
    import jax
    import jax.numpy as jnp

    def _L0_xattn_ref(hidden_states, kv_states, attention_mask, ln1_w, ln2_w, Wq, Wk, Wv, Wo, Wgate, Wup, Wdown):
        import jax, jax.numpy as jnp
        import numpy as np
        import math
        H, NH, NKV, HD, FF = (128, 16, 4, 64, 512)
        B, S = (2, 256)
        EPS, THETA = (1e-06, 10000.0)

        def _rmsnorm(x, w, eps=EPS):
            v = jnp.mean(x.astype(jnp.float32) ** 2, axis=-1, keepdims=True)
            return (x.astype(jnp.float32) * jax.lax.rsqrt(v + eps)).astype(x.dtype) * w

        def _rope_tables(seq_len, head_dim, theta=THETA):
            inv_freq = 1.0 / theta ** (jnp.arange(0, head_dim, 2, dtype=jnp.float32) / head_dim)
            freqs = jnp.arange(seq_len, dtype=jnp.float32)[:, None] * inv_freq[None, :]
            emb = jnp.concatenate([freqs, freqs], axis=-1)
            return (jnp.cos(emb), jnp.sin(emb))

        def _rotate_half(x):
            x1, x2 = jnp.split(x, 2, axis=-1)
            return jnp.concatenate([-x2, x1], axis=-1)

        def _apply_rope(x, cos, sin):
            return x * cos[None, None] + _rotate_half(x) * sin[None, None]
        bsz, q_len, _ = hidden_states.shape
        k_len = kv_states.shape[1]
        residual = hidden_states
        h = _rmsnorm(hidden_states, ln1_w)
        kv = _rmsnorm(kv_states, ln1_w)
        q = (h @ Wq).reshape(bsz, q_len, NH, HD).transpose(0, 2, 1, 3)
        k = (kv @ Wk).reshape(bsz, k_len, NKV, HD).transpose(0, 2, 1, 3)
        v = (kv @ Wv).reshape(bsz, k_len, NKV, HD).transpose(0, 2, 1, 3)
        cos_q, sin_q = _rope_tables(q_len, HD)
        cos_k, sin_k = _rope_tables(k_len, HD)
        q = _apply_rope(q, cos_q, sin_q)
        k = _apply_rope(k, cos_k, sin_k)
        groups = NH // NKV
        k = jnp.repeat(k, groups, axis=1)
        v = jnp.repeat(v, groups, axis=1)
        scores = jnp.einsum('bhqd,bhkd->bhqk', q, k) / math.sqrt(HD)
        scores = scores + attention_mask
        probs = jax.nn.softmax(scores.astype(jnp.float32), axis=-1).astype(q.dtype)
        attn = jnp.einsum('bhqk,bhkd->bhqd', probs, v)
        attn = attn.transpose(0, 2, 1, 3).reshape(bsz, q_len, NH * HD)
        attn = attn @ Wo
        hidden = residual + attn
        residual = hidden
        x = _rmsnorm(hidden, ln2_w)
        x = jax.nn.silu(x @ Wgate) * (x @ Wup) @ Wdown
        return residual + x

    def _L1_xattn_ref(content_stream, content_mask, context, position_encoding, content_bias, position_bias, segment_encoding, segment_matrix, segment_bias, Wq, Wk, Wv, Wr, Wo, ln1_gamma, ln1_beta, W1, b1, W2, b2, ln2_gamma, ln2_beta):
        import jax, jax.numpy as jnp
        import numpy as np
        B, Q, C, H, N, D, F = (1, 256, 256, 128, 16, 64, 512)
        R = Q + C
        EPS = 1e-12
        NEG = 1e+30

        def _layernorm(x, g, b):
            m = jnp.mean(x, axis=-1, keepdims=True)
            v = jnp.mean(jnp.square(x - m), axis=-1, keepdims=True)
            return (x - m) * jax.lax.rsqrt(v + EPS) * g + b

        def _rel_shift(x, klen):
            b, n, q, r = x.shape
            x = x.reshape(b, n, r, q)[:, :, 1:, :].reshape(b, n, q, r - 1)
            return x[:, :, :, :klen]
        q = jnp.einsum('bqh,hnd->bqnd', content_stream, Wq)
        k = jnp.einsum('bch,hnd->bcnd', context, Wk)
        v = jnp.einsum('bch,hnd->bcnd', context, Wv)
        r = jnp.einsum('brh,hnd->brnd', position_encoding, Wr)
        ac = jnp.einsum('bqnd,bcnd->bnqc', q + content_bias, k)
        bd = _rel_shift(jnp.einsum('bqnd,brnd->bnqr', q + position_bias, r), k.shape[1])
        ef = jnp.einsum('bqnd,snd->bnqs', q + segment_bias, segment_encoding)
        ef = jnp.where(segment_matrix[:, None], ef[..., 1:], ef[..., :1])
        scores = (ac + bd + ef) / jnp.sqrt(jnp.float32(D))
        scores = scores - NEG * content_mask
        probs = jax.nn.softmax(scores, axis=-1)
        attn = jnp.einsum('bnqc,bcnd->bqnd', probs, v)
        attn_out = jnp.einsum('bqnd,hnd->bqh', attn, Wo)
        ffn_in = _layernorm(attn_out + content_stream, ln1_gamma, ln1_beta)
        ffn_out = jax.nn.relu(ffn_in @ W1 + b1) @ W2 + b2
        return _layernorm(ffn_out + ffn_in, ln2_gamma, ln2_beta)
    x = _L0_xattn_ref(x, ctx_1024, mask_Bx1xSxS2_ff0, L0_xattn_ln1_w, L0_xattn_ln2_w, L0_xattn_Wq, L0_xattn_Wk, L0_xattn_Wv, L0_xattn_Wo, L0_xattn_Wgate, L0_xattn_Wup, L0_xattn_Wdown)
    x = _L1_xattn_ref(x, mask_1x1xSxS2_ff0, ctx_1024, L1_xattn_position_encoding, L1_xattn_content_bias, L1_xattn_position_bias, L1_xattn_segment_encoding, mask_1xSxS2_bk1, L1_xattn_segment_bias, L1_xattn_Wq, L1_xattn_Wk, L1_xattn_Wv, L1_xattn_Wr, L1_xattn_Wo, L1_xattn_ln1_gamma, L1_xattn_ln1_beta, L1_xattn_W1, L1_xattn_b1, L1_xattn_W2, L1_xattn_b2, L1_xattn_ln2_gamma, L1_xattn_ln2_beta)
    return x

_drawn_inputs = setup_inputs


def setup_inputs(seed=0):
    import zlib

    import numpy as np

    out = dict(_drawn_inputs(seed))
    spreads = {'L0_xattn_ln1_w': (1.0, 0.6),
     'L0_xattn_ln2_w': (1.0, 0.6),
     'L1_xattn_ln1_gamma': (1.0, 0.2),
     'L1_xattn_ln1_beta': (0.0, 0.1),
     'L1_xattn_b1': (0.0, 0.289),
     'L1_xattn_b2': (0.0, 0.1),
     'L1_xattn_ln2_gamma': (1.0, 0.2),
     'L1_xattn_ln2_beta': (0.0, 0.1)}
    factors = {'L0_xattn_Wq': 8.0,
     'L0_xattn_Wk': 8.0,
     'L0_xattn_Wgate': 4.912,
     'L0_xattn_Wup': 4.884,
     'L0_xattn_Wdown': 4.866,
     'L1_xattn_position_encoding': 8.0,
     'L1_xattn_content_bias': 200.0,
     'L1_xattn_position_bias': 48.808,
     'L1_xattn_segment_encoding': 200.0,
     'L1_xattn_segment_bias': 200.0,
     'L1_xattn_Wq': 8.0,
     'L1_xattn_Wk': 23.025,
     'L1_xattn_Wr': 8.0}
    for name, (base, spread) in spreads.items():
        noise = np.random.default_rng([zlib.crc32(name.encode()), seed]).standard_normal(out[name].shape)
        drawn = base * np.exp(spread * noise) if base else spread * noise
        out[name] = jnp.asarray(drawn.astype(out[name].dtype))
    for name, factor in factors.items():
        out[name] = (out[name] * factor).astype(out[name].dtype)
    return out
```

```python
from contextlib import ExitStack

import concourse.bass as bass
from concourse import mybir

F32 = mybir.dt.float32
U8 = mybir.dt.uint8
ALU = mybir.AluOpType
ACT = mybir.ActivationFunctionType
AX = mybir.AxisListType

B, S, C, H = 64, 128, 77, 128
NH, D = 16, 64
CC = NH // 2
GKV = 4
FF = 512
FC = FF // 128
J = S + C - 1
CW1 = C + 1
VW = D + 1
BANKS = [(0, 6), (6, 11), (11, 16)]
BANK = 512
S_BANKS = (0, 1, 6, 7)
SCALE = 1.0 / 8.0
EPS0, EPS1 = 1e-6, 1e-12


def at_least(eng, sem, value):
    if isinstance(value, int) and value <= 0:
        return
    eng.wait_ge(sem, value)


def upto_last(count):
    return min(count, B) if isinstance(count, int) else count


def dma_after(sp, sem, value):
    if isinstance(value, int):
        at_least(sp, sem, value)
    else:
        sp.wait_ge(sem, value)
        sp.nop(nofuse=True)


def by_pairs(eng, first, end, step):
    with eng.Fori(first // 2, end // 2) as half:
        for k in range(2):
            step(2 * half + (first % 2 + k), (first + k) % 2)


def bcast_mid(ap, n):
    return ap.unsqueeze(1).to_broadcast([ap.shape[0], n, ap.shape[1]])


def bcast_last(ap, n):
    return ap.unsqueeze(2).to_broadcast([ap.shape[0], ap.shape[1], n])


def layer0(nc, d, x1T, ident, ps, halfneg):
    with ExitStack() as ctx:
        def sb(name, shape, dt=F32):
            return ctx.enter_context(nc.sbuf_tensor("l0_" + name, shape, dt))

        def sem(name):
            return ctx.enter_context(nc.semaphore("l0_" + name))

        wq = sb("wq", [128, NH * D])
        wkv = sb("wkv", [128, 2 * GKV * D])
        wo = sb("wo", [128, CC, H])
        wgu = sb("wgu", [128, 2 * FF])
        wd = sb("wd", [128, FC, H])
        lns = sb("lns", [128, 2])
        rope_q = sb("rope_q", [128, 2 * D])
        rope_k = sb("rope_k", [C, 2 * D])
        XC = [sb(f"XC{p}", [128, 2, H]) for p in range(2)]
        XT = [sb(f"XT{p}", [128, S]) for p in range(2)]
        CT = [sb(f"CT{p}", [128, C]) for p in range(2)]
        MK = [sb(f"MK{p}", [128, C]) for p in range(2)]
        XR = [sb(f"XR{p}", [128, H]) for p in range(2)]
        sq = sb("sq", [128, 2, H])
        ss = sb("ss", [128, 2])
        ms = sb("ms", [128, 2])
        rstd = [sb(f"rstd{p}", [128, 2]) for p in range(2)]
        rope_s = sb("rope_s", [128, 2 * D])
        KS = sb("KS", [C, GKV * D])
        KA = sb("KA", [C, GKV * D])
        KB = sb("KB", [C, GKV * D])
        VA = [sb(f"VA{p}", [C, GKV, VW]) for p in range(2)]
        QA = sb("QA", [128, NH, D])
        QB = sb("QB", [128, NH, D])
        QT = sb("QT", [128, CC, S])
        KT = sb("KT", [128, 2, C])
        P = sb("P", [128, NH, C])
        MX = sb("MX", [128, NH])
        PT = sb("PT", [C, NH, S])
        RS = sb("RS", [128, NH])
        A = sb("A", [128, NH * D])
        AT = sb("AT", [128, CC, S])
        XP = sb("XP", [128, H])
        sq2 = sb("sq2", [128, H])
        ss2 = sb("ss2", [128, 1])
        ms2 = sb("ms2", [128, 1])
        rs2 = sb("rs2", [128, 1])
        HN = sb("HN", [128, H])
        HNT = sb("HNT", [128, S])
        TH = sb("TH", [128, FF])
        SG = sb("SG", [128, FF])
        HT = sb("HT", [128, FC, S])

        w_in = sem("w_in")
        x_in = [sem(f"x_in{p}") for p in range(2)]
        xr_in = [sem(f"xr_in{p}") for p in range(2)]
        w_scaled = sem("w_scaled")
        pads = sem("pads")
        squared, summed, mean_ready = sem("squared"), sem("summed"), sem("mean_ready")
        rstd_ready, rope_s_ready = sem("rstd_ready"), sem("rope_s_ready")
        q_ready, kv_ready, kv_out = sem("q_ready"), sem("kv_ready"), sem("kv_out")
        q_parts, q_roped, k_parts, k_roped = sem("q_parts"), sem("q_roped"), sem("k_parts"), sem("k_roped")
        qt_ready, kt_ready, qt_out, kt_out = sem("qt_ready"), sem("kt_ready"), sem("qt_out"), sem("kt_out")
        s_ready, s_masked, s_max, s_centred, p_ready = (sem(n) for n in ("s_ready", "s_masked", "s_max", "s_centred", "p_ready"))
        pt_ready, pt_out, pt_out_v = sem("pt_ready"), sem("pt_out"), sem("pt_out_v")
        pv_ready, sum_inv, a_ready = sem("pv_ready"), sem("sum_inv"), sem("a_ready")
        at_ready, at_out, wo_ready, xp_ready = sem("at_ready"), sem("at_out"), sem("wo_ready"), sem("xp_ready")
        sq2_ready, mean2_ready, rstd2_ready, hn_ready = (sem(n) for n in ("sq2_ready", "mean2_ready", "rstd2_ready", "hn_ready"))
        hnt_ready, hnt_out, gate_ready, up_ready = (sem(n) for n in ("hnt_ready", "hnt_out", "gate_ready", "up_ready"))
        tanh_ready, silu_ready, ht_ready = sem("tanh_ready"), sem("silu_ready"), sem("ht_ready")
        down_ready, x1t_out = sem("down_ready"), sem("x1t_out")
        NW = 8
        block = ctx.enter_context(nc.Block())

        @block.sync
        def _(sp):
            def load(b, p):
                dma_after(sp, rope_s_ready, b - 1)
                dma_after(sp, q_ready, b - 1)
                dma_after(sp, kv_ready, b - 1)
                dma_after(sp, s_masked, 2 * (b - 1))
                sp.dma_start(XC[p][:, 0, :], d["x"][b, :, :]).then_inc(x_in[p], 16)
                sp.dma_start(XC[p][0:C, 1, :], d["ctx"][b, :, :]).then_inc(x_in[p], 16)
                sp.dma_start(XT[p][:, :], d["xT"][b, :, :]).then_inc(x_in[p], 16)
                sp.dma_start(CT[p][:, :], d["ctxT"][:, b, :]).then_inc(x_in[p], 16)
                sp.dma_start(MK[p][:, :], d["mask"][b, :, :]).then_inc(x_in[p], 16)

            def load_residual(b, p):
                dma_after(sp, xp_ready, b - 1)
                sp.dma_start(XR[p][:, :], d["x"][b, :, :]).then_inc(xr_in[p], 16)

            sp.wait_ge(pads, 1)
            load(0, 0)
            for t, n in ((wq, "wq0"), (wkv, "wkv0"), (wgu, "wgu"), (lns, "lns")):
                sp.dma_start(t[:, :], d[n]).then_inc(w_in, 16)
            sp.dma_start(rope_q[:, :], d["rope"][:, 0, :]).then_inc(w_in, 16)
            sp.dma_start(rope_k[:, :], d["rope"][0:C, 1, :]).then_inc(w_in, 16)
            sp.dma_start(wo[:, :, :], d["wo0"]).then_inc(w_in, 16)
            sp.dma_start(wd[:, :, :], d["wd"]).then_inc(w_in, 16)
            load(1, 1)
            load_residual(0, 0)
            load_residual(1, 1)

            def both(b, p):
                load(b, p)
                load_residual(b, p)
            by_pairs(sp, 2, B, both)

        @block.tensor
        def _(pe):
            def project(f, p):
                at_least(pe, x_in[p], 40 * (f - p) + 80)
                at_least(pe, s_masked, 2 * f)
                for k in range(2):
                    mm = nc.tensor.matmul(ps[:, k, :], XT[p][:, :], wq[:, k * 512:(k + 1) * 512], start=True, stop=True)
                mm.then_inc(q_ready, 1)

            def project_kv(f, p):
                at_least(pe, xp_ready, f - 1)
                nc.tensor.matmul(ps[0:C, 2, :], CT[p][:, :], wkv[:, :], start=True, stop=True).then_inc(kv_ready, 1)

            def transpose_probs(m):
                at_least(pe, at_out, 2 * m)
                at_least(pe, x1t_out, m - 1)
                at_least(pe, a_ready, 3 * m)
                at_least(pe, s_masked, 2 * (m + 1))
                pe.wait_ge(p_ready, 2 * (m + 1))
                for g, bank in enumerate((3, 4, 5, 7)):
                    for n in range(4 * g, 4 * g + 4):
                        mm = nc.tensor.transpose(ps[0:C, bank, (n % 4) * S:(n % 4 + 1) * S], P[:, n, :], ident[:, :])
                    mm.then_inc(pt_ready, 1)

            def transpose_normed(e):
                pe.wait_ge(hn_ready, e + 1)
                nc.tensor.transpose(ps[:, 6, 0:S], HN[:, :], ident[:, :]).then_inc(hnt_ready, 1)

            def gate_up(e):
                pe.wait_ge(hnt_out, e + 1)
                for k in range(FC):
                    mm = nc.tensor.matmul(ps[:, 6, k * S:(k + 1) * S], wgu[:, k * 128:(k + 1) * 128], HNT[:, :],
                                          start=True, stop=True)
                mm.then_inc(gate_ready, 1)
                at_least(pe, pt_out_v, upto_last(e + 2))
                for k in range(FC):
                    mm = nc.tensor.matmul(ps[:, 7, k * S:(k + 1) * S], wgu[:, FF + k * 128:FF + (k + 1) * 128], HNT[:, :],
                                          start=True, stop=True)
                mm.then_inc(up_ready, 1)

            def weigh_values(m, p):
                pe.wait_ge(pt_out, 3 * (m + 1))
                pe.wait_ge(pt_out_v, m + 1)
                for k, (a, z) in enumerate(BANKS):
                    for n in range(a, z):
                        g = n // 4
                        mm = nc.tensor.matmul(ps[:, 3 + k, (n - a) * VW:(n - a + 1) * VW], PT[:, n, :], VA[p][:, g, :],
                                              start=True, stop=True)
                mm.then_inc(pv_ready, 1)

            def transpose_qk(f):
                at_least(pe, silu_ready, f - 1)
                at_least(pe, ht_ready, f - 1)
                if isinstance(f, int) and f < 2:
                    at_least(pe, pt_out_v, f)
                    at_least(pe, xp_ready, f - 1)
                pe.wait_ge(q_roped, f + 1)
                for k in range(2):
                    for c in range(4 * k, 4 * k + 4):
                        mm = nc.tensor.transpose(ps[:, 6 + k, (c % 4) * S:(c % 4 + 1) * S],
                                                 QA[:, 2 * c:2 * c + 2, :].rearrange("q u d -> q (u d)"), ident[:, :])
                    mm.then_inc(qt_ready, 1)
                pe.wait_ge(kv_out, f + 1)
                pe.wait_ge(k_roped, f + 1)
                for a in range(2):
                    mm = nc.tensor.transpose(ps[:, 2, a * C:(a + 1) * C], KA[:, a * 128:(a + 1) * 128], ident[0:C, 0:C])
                mm.then_inc(kt_ready, 1)

            def scores(f):
                pe.wait_ge(qt_out, 2 * (f + 1))
                pe.wait_ge(kt_out, f + 1)
                pe.wait_ge(q_parts, f + 1)
                for k in range(2):
                    for i in range(4):
                        for u in range(2):
                            mm = nc.tensor.matmul(ps[:, S_BANKS[2 * k + u], i * C:(i + 1) * C], QT[64 * u:64 * u + 64, 4 * k + i, :],
                                                  KT[64 * u:64 * u + 64, k, :], start=True, stop=True)
                    mm.then_inc(s_ready, 1)

            def transpose_attn(m):
                pe.wait_ge(a_ready, 3 * (m + 1))
                for k in range(2):
                    for c in range(4 * k, 4 * k + 4):
                        mm = nc.tensor.transpose(ps[:, 3 + k, (c % 4) * S:(c % 4 + 1) * S],
                                                 A[:, c * 128:(c + 1) * 128], ident[:, :])
                    mm.then_inc(at_ready, 1)

            def down(e):
                pe.wait_ge(ht_ready, e + 1)
                for k in range(FC):
                    nc.tensor.matmul(ps[:, 5, 0:S], wd[:, k, :], HT[:, k, :], start=(k == 0), stop=False)
                nc.tensor.matmul(ps[:, 5, 0:S], XP[:, :], ident[:, :], start=False, stop=True).then_inc(down_ready, 1)

            def project_out(m):
                pe.wait_ge(at_out, 2 * (m + 1))
                for c in range(CC):
                    mm = nc.tensor.matmul(ps[:, 2, 0:H], AT[:, c, :], wo[:, c, :], start=(c == 0), stop=(c == CC - 1))
                mm.then_inc(wo_ready, 1)

            def step(t, p, front=True, mid=True, end=True):
                if front:
                    project(t + 1, 1 - p)
                    project_kv(t + 1, 1 - p)
                if mid:
                    transpose_probs(t)
                if end:
                    transpose_normed(t - 1)
                    gate_up(t - 1)
                if mid:
                    weigh_values(t, p)
                if front:
                    transpose_qk(t + 1)
                    scores(t + 1)
                if mid:
                    transpose_attn(t)
                if end:
                    if mid:
                        pe.wait_ge(a_ready, 3 * (t + 1))
                    down(t - 1)
                if mid:
                    project_out(t)

            pe.wait_ge(w_in, 16 * NW)
            pe.wait_ge(w_scaled, 3)
            step(-1, 1, mid=False, end=False)
            step(0, 0, end=False)
            step(1, 1)
            step(2, 0)
            by_pairs(pe, 3, B - 1, step)
            step(B - 1, 1, front=False)
            step(B, 0, front=False, mid=False)

        @block.scalar
        def _(act):
            def kv_evict(f, p):
                act.wait_ge(rstd_ready, f + 1)
                act.wait_ge(kv_ready, f + 1)
                at_least(act, k_parts, f)
                at_least(act, pv_ready, f - 1)
                nc.scalar.activation(KS[:, :], ps[0:C, 2, 0:GKV * D], ACT.Copy, scale=rstd[p][0:C, 1:2])
                nc.scalar.activation(VA[p][:, :, 0:D], ps[0:C, 2, GKV * D:].rearrange("c (g d) -> c g d", g=GKV),
                                     ACT.Copy, scale=rstd[p][0:C, 1:2]).then_inc(kv_out, 1)

            def probs_evict(m):
                for g, bank in enumerate((3, 4, 5)):
                    act.wait_ge(pt_ready, 4 * m + g + 1)
                    if g == 0:
                        at_least(act, pv_ready, m)
                    nc.scalar.copy(PT[:, 4 * g:4 * g + 4, :], ps[0:C, bank, :].rearrange("c (n q) -> c n q", n=4)).then_inc(pt_out, 1)

            def normed_evict(e):
                act.wait_ge(hnt_ready, e + 1)
                at_least(act, up_ready, e)
                nc.scalar.copy(HNT[:, :], ps[:, 6, 0:S]).then_inc(hnt_out, 1)

            def tanh(e):
                act.wait_ge(gate_ready, e + 1)
                at_least(act, silu_ready, e)
                nc.scalar.activation(TH[:, :], ps[:, 6, :], ACT.Tanh, scale=0.5).then_inc(tanh_ready, 1)

            def qk_evict(f):
                at_least(act, s_ready, 2 * f)
                for k in range(2):
                    act.wait_ge(qt_ready, 2 * f + k + 1)
                    nc.scalar.copy(QT[:, 4 * k:4 * k + 4, :], ps[:, 6 + k, :].rearrange("c (n q) -> c n q", n=4)).then_inc(qt_out, 1)
                act.wait_ge(kt_ready, f + 1)
                nc.scalar.copy(KT[:, :, :], ps[:, 2, 0:2 * C].rearrange("p (a c) -> p a c", a=2)).then_inc(kt_out, 1)

            def exps(f):
                for k in range(2):
                    act.wait_ge(s_centred, 2 * f + k + 1)
                    nc.scalar.activation(P[:, 8 * k:8 * k + 8, :], P[:, 8 * k:8 * k + 8, :], ACT.Exp).then_inc(p_ready, 1)

            def attn_evict(m):
                at_least(act, wo_ready, m)
                for k in range(2):
                    act.wait_ge(at_ready, 2 * m + k + 1)
                    nc.scalar.copy(AT[:, 4 * k:4 * k + 4, :], ps[:, 3 + k, :].rearrange("c (n q) -> c n q", n=4)).then_inc(at_out, 1)

            def x1_evict(e):
                act.wait_ge(down_ready, e + 1)
                nc.scalar.copy(x1T[:, e, :], ps[:, 5, 0:S]).then_inc(x1t_out, 1)

            def step(t, p, front=True, mid=True, end=True):
                if front:
                    kv_evict(t + 1, 1 - p)
                if mid:
                    probs_evict(t)
                if end:
                    normed_evict(t - 1)
                    tanh(t - 1)
                if front:
                    qk_evict(t + 1)
                if mid:
                    attn_evict(t)
                if end:
                    x1_evict(t - 1)
                if front:
                    exps(t + 1)

            act.wait_ge(pads, 2)
            step(-1, 1, mid=False, end=False)
            step(0, 0, end=False)
            step(1, 1)
            step(2, 0)
            by_pairs(act, 3, B - 1, step)
            step(B - 1, 1, front=False)
            step(B, 0, front=False, mid=False)

        @block.vector
        def _(dve):
            def mean_squares(f, p):
                at_least(dve, x_in[p], 40 * (f - p) + 80)
                at_least(dve, summed, f)
                nc.vector.tensor_tensor(sq[:, :, :], XC[p][:, :, :], XC[p][:, :, :], ALU.mult).then_inc(squared, 1)
                dve.wait_ge(squared, f + 1)
                nc.vector.tensor_reduce(ss[:, :], sq[:, :, :], AX.X, ALU.add).then_inc(summed, 1)
                dve.wait_ge(summed, f + 1)
                at_least(dve, rstd_ready, f)
                nc.vector.tensor_scalar(ms[:, :], ss[:, :], 1.0 / H, EPS0, ALU.mult, ALU.add).then_inc(mean_ready, 1)

            def scaled_rope(f, p):
                dve.wait_ge(rstd_ready, f + 1)
                at_least(dve, q_parts, f)
                nc.vector.tensor_scalar(rope_s[:, :], rope_q[:, :], rstd[p][:, 0:1], None, ALU.mult).then_inc(rope_s_ready, 1)

            def rope(f):
                dve.wait_ge(q_ready, f + 1)
                dve.wait_ge(rope_s_ready, f + 1)
                at_least(dve, qt_ready, 2 * f)
                at_least(dve, q_roped, f)
                q = ps[:, 0:2, :].rearrange("p k (n d) -> p (k n) d", d=D)
                nc.vector.tensor_tensor(QA[:, :, :], q, bcast_mid(rope_s[:, 0:D], NH), ALU.mult)
                nc.vector.tensor_tensor(QB[:, :, 0:D // 2], q[:, :, D // 2:], bcast_mid(rope_s[:, D:D + D // 2], NH), ALU.mult)
                nc.vector.tensor_tensor(QB[:, :, D // 2:], q[:, :, 0:D // 2], bcast_mid(rope_s[:, D + D // 2:], NH),
                                        ALU.mult).then_inc(q_parts, 1)

            def probs_evict(m):
                dve.wait_ge(pt_ready, 4 * (m + 1))
                at_least(dve, pv_ready, m)
                nc.vector.tensor_copy(PT[:, 12:16, :], ps[0:C, 7, :].rearrange("c (n q) -> c n q", n=4)).then_inc(pt_out_v, 1)

            def silu(e):
                dve.wait_ge(tanh_ready, e + 1)
                at_least(dve, ht_ready, e)
                nc.vector.scalar_tensor_tensor(SG[:, :], TH[:, :], 1.0, ps[:, 6, :], ALU.add, ALU.mult).then_inc(silu_ready, 1)
                dve.wait_ge(silu_ready, e + 1)
                dve.wait_ge(up_ready, e + 1)
                at_least(dve, down_ready, e)
                nc.vector.tensor_tensor(HT[:, :, :].rearrange("p k q -> p (k q)"), SG[:, :], ps[:, 7, :], ALU.mult).then_inc(ht_ready, 1)

            def normalise(m):
                dve.wait_ge(pv_ready, m + 1)
                at_least(dve, a_ready, 3 * m)
                for k, (a, z) in enumerate(BANKS):
                    o = ps[:, 3 + k, 0:(z - a) * VW].rearrange("p (n d) -> p n d", d=VW)
                    nc.vector.reciprocal(RS[:, a:z].unsqueeze(2), o[:, :, D:VW]).then_inc(sum_inv, 1)
                at_least(dve, at_ready, 2 * m)
                for k, (a, z) in enumerate(BANKS):
                    o = ps[:, 3 + k, 0:(z - a) * VW].rearrange("p (n d) -> p n d", d=VW)
                    dve.wait_ge(sum_inv, 3 * m + k + 1)
                    nc.vector.tensor_tensor(A[:, a * D:z * D].rearrange("p (n d) -> p n d", d=D), o[:, :, 0:D],
                                            bcast_last(RS[:, a:z], D), ALU.mult).then_inc(a_ready, 1)

            def mask_max(f, p):
                at_least(dve, pt_ready, 4 * f)
                at_least(dve, s_centred, 2 * f)
                for k in range(2):
                    dve.wait_ge(s_ready, 2 * f + k + 1)
                    b0, b1 = S_BANKS[2 * k:2 * k + 2]
                    sc = ps[:, b0:b1 + 1, 0:4 * C].rearrange("p k (n c) -> p k n c", c=C)
                    mk = MK[p][:, :].unsqueeze(1).unsqueeze(1).to_broadcast([128, 2, 4, C])
                    nc.vector.tensor_tensor(P[:, 8 * k:8 * k + 8, :].rearrange("p (k n) c -> p k n c", k=2), sc, mk,
                                            ALU.add).then_inc(s_masked, 1)
                for k in range(2):
                    dve.wait_ge(s_masked, 2 * f + k + 1)
                    nc.vector.tensor_reduce(MX[:, 8 * k:8 * k + 8], P[:, 8 * k:8 * k + 8, :], AX.X, ALU.max).then_inc(s_max, 1)

            def residual_norm(m, p):
                dve.wait_ge(wo_ready, m + 1)
                at_least(dve, xr_in[p], 8 * (m - p) + 16)
                at_least(dve, down_ready, m)
                nc.vector.tensor_tensor(XP[:, :], ps[:, 2, 0:H], XR[p][:, :], ALU.add).then_inc(xp_ready, 1)
                dve.wait_ge(xp_ready, m + 1)
                nc.vector.tensor_tensor(sq2[:, :], XP[:, :], XP[:, :], ALU.mult).then_inc(sq2_ready, 1)
                dve.wait_ge(sq2_ready, 2 * m + 1)
                nc.vector.tensor_reduce(ss2[:, :], sq2[:, :], AX.X, ALU.add).then_inc(sq2_ready, 1)
                dve.wait_ge(sq2_ready, 2 * m + 2)
                nc.vector.tensor_scalar(ms2[:, :], ss2[:, :], 1.0 / H, EPS0, ALU.mult, ALU.add).then_inc(mean2_ready, 1)
                dve.wait_ge(rstd2_ready, m + 1)
                at_least(dve, hnt_ready, m)
                nc.vector.tensor_scalar(HN[:, :], XP[:, :], rs2[:, 0:1], None, ALU.mult).then_inc(hn_ready, 1)

            def step(t, p, front=True, mid=True, end=True, more=True):
                if front:
                    rope(t + 1)
                if mid:
                    probs_evict(t)
                if end:
                    silu(t - 1)
                if mid:
                    normalise(t)
                if front:
                    mask_max(t + 1, 1 - p)
                    if more:
                        mean_squares(t + 2, p)
                if mid:
                    residual_norm(t, p)
                if front and more:
                    scaled_rope(t + 2, p)

            for p in range(2):
                last = nc.vector.memset(XC[p][:, :, :], 0.0)
            last.then_inc(pads, 1)
            for p in range(2):
                last = nc.vector.memset(VA[p][:, :, :], 1.0)
            last.then_inc(pads, 1)
            dve.wait_ge(w_in, 16 * NW)
            nc.vector.tensor_scalar(wq[:, :], wq[:, :], lns[:, 0:1], None, ALU.mult)
            nc.vector.tensor_scalar(wkv[:, :], wkv[:, :], lns[:, 0:1], None, ALU.mult)
            nc.vector.tensor_scalar(wgu[:, :], wgu[:, :], lns[:, 1:2], None, ALU.mult).then_inc(w_scaled, 1)
            nc.vector.tensor_scalar(wd[:, :, :], wd[:, :, :], 0.5, None, ALU.mult).then_inc(w_scaled, 1)
            nc.vector.tensor_scalar(rope_q[:, :], rope_q[:, :], SCALE, None, ALU.mult).then_inc(w_scaled, 1)
            dve.wait_ge(w_scaled, 3)
            mean_squares(0, 0)
            scaled_rope(0, 0)
            step(-1, 1, mid=False, end=False)
            step(0, 0, end=False)
            step(1, 1)
            step(2, 0)
            by_pairs(dve, 3, B - 3, step)
            step(B - 3, 1)
            step(B - 2, 0, more=False)
            step(B - 1, 1, front=False)
            step(B, 0, front=False, mid=False)

        @block.gpsimd
        def _(pool):
            def rstd_x(f, p):
                pool.wait_ge(mean_ready, f + 1)
                at_least(pool, kv_out, f - 1)
                nc.gpsimd.tensor_tensor(rstd[p][:, :], ms[:, :], halfneg[:, 0:2], ALU.pow).then_inc(rstd_ready, 1)

            def rope_sum(f):
                pool.wait_ge(q_parts, f + 1)
                nc.gpsimd.tensor_tensor(QA[:, :, :], QA[:, :, :], QB[:, :, :], ALU.add).then_inc(q_roped, 1)

            def rope_keys(f):
                pool.wait_ge(kv_out, f + 1)
                at_least(pool, kt_ready, f)
                at_least(pool, k_roped, f)
                k = KS[:, :].rearrange("c (g d) -> c g d", d=D)
                ka = KA[:, :].rearrange("c (g d) -> c g d", d=D)
                kb = KB[:, :].rearrange("c (g d) -> c g d", d=D)
                h = D // 2
                nc.gpsimd.tensor_tensor(ka, k, bcast_mid(rope_k[:, 0:D], GKV), ALU.mult)
                nc.gpsimd.tensor_tensor(kb[:, :, 0:h], k[:, :, h:], bcast_mid(rope_k[:, D:D + h], GKV), ALU.mult)
                nc.gpsimd.tensor_tensor(kb[:, :, h:], k[:, :, 0:h], bcast_mid(rope_k[:, D + h:], GKV), ALU.mult).then_inc(k_parts, 1)
                pool.wait_ge(k_parts, f + 1)
                nc.gpsimd.tensor_tensor(KA[:, :], KA[:, :], KB[:, :], ALU.add).then_inc(k_roped, 1)

            def centre(f):
                for k in range(2):
                    pool.wait_ge(s_max, 2 * f + k + 1)
                    nc.gpsimd.tensor_tensor(P[:, 8 * k:8 * k + 8, :], P[:, 8 * k:8 * k + 8, :],
                                            bcast_last(MX[:, 8 * k:8 * k + 8], C), ALU.subtract).then_inc(s_centred, 1)

            def rstd_mlp(m):
                pool.wait_ge(mean2_ready, m + 1)
                at_least(pool, hn_ready, m)
                nc.gpsimd.tensor_tensor(rs2[:, :], ms2[:, :], halfneg[:, 0:1], ALU.pow).then_inc(rstd2_ready, 1)

            def step(t, p, front=True, mid=True, more=True):
                if front:
                    rope_keys(t + 1)
                    rope_sum(t + 1)
                    centre(t + 1)
                    if more:
                        rstd_x(t + 2, p)
                if mid:
                    rstd_mlp(t)

            pool.wait_ge(w_in, 16 * NW)
            rstd_x(0, 0)
            step(-1, 1, mid=False)
            step(0, 0)
            step(1, 1)
            step(2, 0)
            by_pairs(pool, 3, B - 3, step)
            step(B - 3, 1)
            step(B - 2, 0, more=False)
            step(B - 1, 1, front=False)


def prepare1(nc, d, t, ident, ones, ps):
    MT, GM, WT, U, DW, DC, ctxT = t["MT"], t["GM"], t["WT"], t["U"], t["DW"], t["DC"], t["ctxT"]
    with ExitStack() as ctx:
        def sb(name, shape, dt=F32):
            return ctx.enter_context(nc.sbuf_tensor("pr_" + name, shape, dt))

        def sem(name):
            return ctx.enter_context(nc.semaphore("pr_" + name))

        wqT = sb("wqT", [128, CC, H])
        wkT = sb("wkT", [128, CC, H])
        wr = sb("wr", [128, NH * D])
        pos = sb("pos", [128, J])
        small = sb("small", [128, 5, CC])
        rT = sb("rT", [128, CC, J])
        rS = sb("rS", [128, CC, J])
        dse = sb("dse", [128, CC])
        pr = sb("pr", [128, 2, CC])
        bc = sb("bc", [128, NH])
        cw = sb("cw", [128, NH])
        cb, pb, sbias, se0, se1 = (small[:, k, :] for k in range(5))
        w_in, r_ready, r_out, rs_out, small_out = (sem(n) for n in ("w_in", "r_ready", "r_out", "rs_out", "small_out"))
        step_ready, step_out, dse_out, u_ready, u_out, consts = (sem(n) for n in ("step_ready", "step_out", "dse_out", "u_ready", "u_out", "consts"))
        block = ctx.enter_context(nc.Block())

        @block.sync
        def _(sp):
            sp.dma_start(wr[:, :], d["wr1"]).then_inc(w_in, 16)
            sp.dma_start(pos[:, :], d["pos"]).then_inc(w_in, 16)
            sp.dma_start(small[:, :, :], d["small"]).then_inc(w_in, 16)
            sp.dma_start(wqT[:, :, :], d["wqT"]).then_inc(w_in, 16)
            sp.dma_start(wkT[:, :, :], d["wkT"]).then_inc(w_in, 16)
            sp.dma_start(ctxT[:, :, :], d["ctxT"]).then_inc(w_in, 16)

        @block.tensor
        def _(pe):
            pe.wait_ge(w_in, 96)
            for c in range(CC):
                nc.tensor.matmul(ps[:, c, 0:J], wr[:, c * 128:(c + 1) * 128], pos[:, :], start=True, stop=True).then_inc(r_ready, 1)
            pe.wait_ge(small_out, 1)
            s = 0
            for n in range(NH):
                if s < 8:
                    pe.wait_ge(rs_out, s + 1)
                    pe.wait_ge(r_out, s + 1)
                else:
                    pe.wait_ge(step_out, s - 7)
                o = 64 * (n % 2)
                nc.tensor.matmul(ps[:, s % 8, 0:J], wqT[o:o + 64, n // 2, :], rS[o:o + 64, n // 2, :],
                                 start=True, stop=True).then_inc(step_ready, 1)
                s += 1
            pe.wait_ge(r_out, 2 * CC)
            for n in range(NH):
                pe.wait_ge(step_out, s - 7)
                o = 64 * (n % 2)
                nc.tensor.matmul(ps[:, s % 8, 0:J], ones[o:o + 64, :], rT[o:o + 64, n // 2, :],
                                 start=True, stop=True).then_inc(step_ready, 1)
                s += 1
            for g in range(4):
                pe.wait_ge(step_out, s - 7)
                for k in range(4):
                    o, c = 64 * (g % 2), 4 * (g // 2) + k
                    mm = nc.tensor.matmul(ps[:, s % 8, k * H:(k + 1) * H], wkT[o:o + 64, c, :], wqT[o:o + 64, c, :],
                                          start=True, stop=True)
                mm.then_inc(step_ready, 1)
                s += 1
            pe.wait_ge(small_out, 2)
            for u in range(2):
                o = 64 * u
                pe.wait_ge(step_out, s - 7)
                for c in range(CC):
                    mm = nc.tensor.matmul(ps[:, s % 8, c:c + 1], wkT[o:o + 64, c, :], cb[o:o + 64, c:c + 1], start=True, stop=True)
                mm.then_inc(step_ready, 1)
                s += 1
            for u in range(2):
                o = 64 * u
                pe.wait_ge(step_out, s - 7)
                for c in range(CC):
                    mm = nc.tensor.matmul(ps[:, s % 8, c:c + 1], wqT[o:o + 64, c, :], dse[o:o + 64, c:c + 1], start=True, stop=True)
                mm.then_inc(step_ready, 1)
                s += 1
            for u in range(2):
                o = 64 * u
                pe.wait_ge(step_out, s - 7)
                for k in range(2):
                    mm = nc.tensor.matmul(ps[:, s % 8, k * CC:(k + 1) * CC], ones[o:o + 64, :], pr[o:o + 64, k, :],
                                          start=True, stop=True)
                mm.then_inc(step_ready, 1)
                s += 1
            pe.wait_ge(step_out, s)
            for c in range(CW1):
                o = ps[:, c // 26, (c % 26) * NH:(c % 26 + 1) * NH]
                if c > 0:
                    mm = nc.tensor.matmul(o[0:64, :], ctxT[:, :, c - 1], cw[:, :], start=True, stop=True)
                if c < C:
                    nc.tensor.matmul(o[64:128, :], ctxT[:, :, c], cw[:, :], start=True, stop=True)
            mm.then_inc(u_ready, 1)

        @block.vector
        def _(dve):
            dve.wait_ge(w_in, 96)
            nc.vector.memset(U[:, :, :], 0.0).then_inc(dse_out, 0 + 1)
            nc.vector.tensor_tensor(dse[:, :], se1, se0, ALU.subtract).then_inc(small_out, 1)
            dve.wait_ge(small_out, 1)
            nc.vector.tensor_tensor(pr[:, 0, :], sbias, se0, ALU.mult)
            nc.vector.tensor_tensor(pr[:, 1, :], sbias, dse[:, :], ALU.mult).then_inc(small_out, 1)
            for c in range(CC):
                dve.wait_ge(r_ready, c + 1)
                nc.vector.tensor_scalar(rS[:, c, :], ps[:, c, 0:J], se0[:, c:c + 1], None, ALU.add).then_inc(rs_out, 1)
                nc.vector.tensor_copy(rT[:, c, :], ps[:, c, 0:J]).then_inc(r_out, 1)
            for c in range(CC):
                dve.wait_ge(r_out, c + 1)
                nc.vector.tensor_scalar(rT[:, c, :], rT[:, c, :], pb[:, c:c + 1], None, ALU.mult).then_inc(r_out, 1)
            s = 0
            for table in (GM, WT):
                for n in range(NH):
                    dve.wait_ge(step_ready, s + 1)
                    nc.vector.tensor_scalar(table[:, n, :], ps[:, s % 8, 0:J], SCALE, None, ALU.mult).then_inc(step_out, 1)
                    s += 1
            for g in range(4):
                dve.wait_ge(step_ready, s + 1)
                first = 8 * (g // 2) + g % 2
                nc.vector.tensor_scalar(MT[:, first:first + 7:2, :], ps[:, s % 8, :].rearrange("p (n h) -> p n h", n=4), SCALE, None,
                                        ALU.mult).then_inc(step_out, 1)
                s += 1
            for table in (cw, DW):
                for u in range(2):
                    dve.wait_ge(step_ready, s + 1)
                    nc.vector.tensor_scalar(table[:, u:NH:2], ps[:, s % 8, 0:CC], SCALE, None, ALU.mult).then_inc(step_out, 1)
                    s += 1
            for u in range(2):
                dve.wait_ge(step_ready, s + 1)
                nc.vector.tensor_scalar(bc[:, u:NH:2], ps[:, s % 8, 0:CC], SCALE, None, ALU.mult)
                nc.vector.tensor_scalar(DC[:, u:NH:2], ps[:, s % 8, CC:2 * CC], SCALE, None, ALU.mult).then_inc(step_out, 1)
                s += 1
            dve.wait_ge(step_out, s)
            nc.vector.tensor_tensor(WT[:, :, :], WT[:, :, :], bcast_last(bc[:, :], J), ALU.add).then_inc(consts, 1)
            dve.wait_ge(u_ready, 1)
            dve.wait_ge(dse_out, 1)
            for lo, hi, first, last in ((64, 128, 0, C), (0, 64, 1, CW1)):
                for k in range(3):
                    a, z = max(first, 26 * k), min(last, 26 * k + 26)
                    nc.vector.tensor_copy(U[lo:hi, :, a:z], ps[lo:hi, k, (a - 26 * k) * NH:(z - 26 * k) * NH]
                                          .rearrange("p (c n) -> p n c", n=NH)).then_inc(u_out, 1)


def position_terms(nc, t, bd, x1T, ps):
    GM, WT, U = t["GM"], t["WT"], t["U"]
    with ExitStack() as ctx:
        def sb(name, shape, dt=F32):
            return ctx.enter_context(nc.sbuf_tensor("pt_" + name, shape, dt))

        def sem(name):
            return ctx.enter_context(nc.semaphore("pt_" + name))

        xq = [sb(f"xq{p}", [128, 2, B]) for p in range(2)]
        ev = [sb(f"ev{p}", [128, NH, CW1]) for p in range(2)]
        xq_ready, g_ready, w_added, u_added = sem("xq_ready"), sem("g_ready"), sem("w_added"), sem("u_added")
        stored = [sem(f"stored{p}") for p in range(2)]
        block = ctx.enter_context(nc.Block())

        def loop(eng, step):
            step(0, 0)
            step(1, 1)
            by_pairs(eng, 2, S // 2, step)

        @block.scalar
        def _(act):
            def step(k, p):
                at_least(act, g_ready, 3 * (k - 1))
                nc.scalar.copy(xq[p][:, :, :], x1T[:, :, bass.ds(2 * k, 2)].rearrange("p b s -> p s b")).then_inc(xq_ready, 1)
            loop(act, step)

        @block.tensor
        def _(pe):
            def step(k, p):
                pe.wait_ge(xq_ready, k + 1)
                at_least(pe, w_added, 3 * (k - 1))
                for g, (a, z) in enumerate(BANKS):
                    nc.tensor.matmul(ps[:, 3 * p + g, 0:(z - a) * CW1], xq[p][:, :, :].rearrange("p s b -> p (s b)"),
                                     GM[:, a:z, bass.ds(S - 2 - 2 * k, CW1)], start=True, stop=True).then_inc(g_ready, 1)
            loop(pe, step)

        @block.vector
        def _(dve):
            def step(k, p):
                at_least(dve, stored[p], 16 * (k - p))
                for g, (a, z) in enumerate(BANKS):
                    dve.wait_ge(g_ready, 3 * k + g + 1)
                    nc.vector.tensor_tensor(ev[p][:, a:z, :], ps[:, 3 * p + g, 0:(z - a) * CW1].rearrange("p (n c) -> p n c", c=CW1),
                                            WT[:, a:z, bass.ds(S - 2 - 2 * k, CW1)], ALU.add).then_inc(w_added, 1)
            loop(dve, step)

        @block.gpsimd
        def _(pool):
            def step(k, p):
                pool.wait_ge(w_added, 3 * k + 3)
                nc.gpsimd.tensor_tensor(ev[p][:, :, :], ev[p][:, :, :], U[:, :, :], ALU.add).then_inc(u_added, 1)
            loop(pool, step)

        @block.sync
        def _(sp):
            def step(k, p):
                dma_after(sp, u_added, k + 1)
                for s in range(2):
                    sp.dma_start(bd[:, 2 * k + s, :], ev[p][64 * s:64 * s + 64, :, :].rearrange("b n c -> b (n c)")).then_inc(stored[p], 16)
            loop(sp, step)
            for p in range(2):
                sp.wait_ge(stored[p], 32 * (S // 4))


def layer1(nc, d, t, bd, out, x1T, ident, ps, halfneg):
    MT, DW, DC, ctxT = t["MT"], t["DW"], t["DC"], t["ctxT"]
    with ExitStack() as ctx:
        def sb(name, shape, dt=F32):
            return ctx.enter_context(nc.sbuf_tensor("l1_" + name, shape, dt))

        def sem(name):
            return ctx.enter_context(nc.semaphore("l1_" + name))

        wv = sb("wv", [128, NH * D])
        wo = sb("wo", [128, CC, H])
        w1 = sb("w1", [128, FF])
        w2 = sb("w2", [128, FC, H])
        b1 = sb("b1", [128, FC])
        rows = sb("rows", [128, 5, H])
        seg8 = sb("seg8", [128, C], U8)
        seg = sb("seg", [128, C])
        nm = sb("nm", [128, C])
        XT = [sb(f"XT{p}", [128, S]) for p in range(2)]
        CT = [sb(f"CT{p}", [128, C]) for p in range(2)]
        BD = [sb(f"BD{p}", [128, NH, CW1]) for p in range(2)]
        DS = sb("DS", [128, NH])
        T = sb("T", [128, NH, C])
        Z = sb("Z", [128, NH, C])
        VA = [sb(f"VA{p}", [C, NH, VW]) for p in range(2)]
        P = sb("P", [128, NH, C])
        MX = sb("MX", [128, NH])
        PT = sb("PT", [C, NH, S])
        RS = sb("RS", [128, NH])
        A = sb("A", [128, NH * D])
        AT = sb("AT", [128, CC, S])
        Y = sb("Y", [128, 2, H])
        st = sb("st", [128, 2, 6])
        mv = sb("mv", [128, 2, 2])
        ve = sb("ve", [128, 2])
        rs = sb("rs", [128, 2])
        NRM = sb("NRM", [128, 2, H])
        Z1 = sb("Z1", [128, H])
        ZB = sb("ZB", [128, H])
        ZT = sb("ZT", [128, S])
        HT = sb("HT", [128, FC, S])
        OUT = [sb(f"OUT{p}", [128, H]) for p in range(2)]

        w_in, pads = sem("w_in"), sem("pads")
        bd_in = [sem(f"bd_in{p}") for p in range(2)]
        stored = [sem(f"stored{p}") for p in range(2)]
        names = ("seg_ready xt_ready dd_ready ds_ready t_seg t_mask t_ready z_ready z_out v_ready v_out s_ready s_added s_max "
                 "s_centred p_ready pt_ready pt_out pt_out_v pv_ready sum_inv a_ready at_ready at_out wo_ready "
                 "y_ready stat1 var1 rstd1 nrm1 gam1 z1_ready zb_ready zt_ready zt_out h_ready ht_out down_ready "
                 "w_ready stat2 var2 rstd2 nrm2 gam2 out_ready").split()
        e = {n: sem(n) for n in names}
        NW = 8
        block = ctx.enter_context(nc.Block())

        @block.sync
        def _(sp):
            def load(b, p):
                dma_after(sp, e["t_ready"], b - 1)
                v = bd[b, :, :].rearrange("(k s) e -> s k e", s=2)
                for s in range(2):
                    w = NH * CW1 - 1
                    sp.dma_start(BD[p][s:128:2, :, :].rearrange("q n c -> q (n c)")[:, 0:w], v[s, :, 1 - s:1 - s + w]).then_inc(bd_in[p], 16)

            load(0, 0)
            load(1, 1)
            for tile, n in ((wv, "wv1"), (w1, "w1"), (b1, "b1"), (seg8, "seg"), (nm, "cmask")):
                sp.dma_start(tile[:, :], d[n]).then_inc(w_in, 16)
            sp.dma_start(wo[:, :, :], d["wo1"]).then_inc(w_in, 16)
            sp.dma_start(w2[:, :, :], d["w2"]).then_inc(w_in, 16)
            sp.dma_start(rows[:, :, :], d["rows"].partition_broadcast(128)).then_inc(w_in, 16)

            def step(b, p):
                load(b, p)
                store(b - 2, p)

            def store(b, p):
                dma_after(sp, e["out_ready"], b + 1)
                sp.dma_start(out[b, :, :], OUT[p][:, :]).then_inc(stored[p], 16)
            by_pairs(sp, 2, B, step)
            store(B - 2, 0)
            store(B - 1, 1)
            for p in range(2):
                sp.wait_ge(stored[p], 16 * (B // 2))

        @block.tensor
        def _(pe):
            def front1(f, p):
                pe.wait_ge(e["xt_ready"], f + 1)
                at_least(pe, e["v_out"], 2 * f)
                nc.tensor.matmul(ps[:, 7, 0:NH], XT[p][:, :], DW[:, :], start=True, stop=True).then_inc(e["dd_ready"], 1)
                at_least(pe, e["s_added"], 3 * f)
                for k, (a, z) in enumerate(BANKS):
                    for n in range(a, z):
                        mm = nc.tensor.matmul(ps[:, k, (n - a) * C:(n - a + 1) * C], MT[:, n, :], ctxT[:, f, :],
                                              start=True, stop=True)
                    mm.then_inc(e["z_ready"], 1)

            def transpose_probs(m):
                at_least(pe, e["at_out"], 2 * m)
                at_least(pe, e["a_ready"], 3 * m)
                at_least(pe, e["w_ready"], m - 1)
                pe.wait_ge(e["ds_ready"], upto_last(m + 2))
                pe.wait_ge(e["p_ready"], 3 * (m + 1))
                for g, bank in enumerate((3, 4, 5, 7)):
                    for n in range(4 * g, 4 * g + 4):
                        mm = nc.tensor.transpose(ps[0:C, bank, (n % 4) * S:(n % 4 + 1) * S], P[:, n, :], ident[:, :])
                    mm.then_inc(e["pt_ready"], 1)

            def transpose_normed(b):
                pe.wait_ge(e["z1_ready"], b + 1)
                nc.tensor.transpose(ps[:, 6, 0:S], Z1[:, :], ident[:, :]).then_inc(e["zt_ready"], 1)

            def up(b):
                pe.wait_ge(e["zt_out"], b + 1)
                for k in range(FC):
                    mm = nc.tensor.matmul(ps[:, 6, k * S:(k + 1) * S], w1[:, k * 128:(k + 1) * 128], ZT[:, :], start=True, stop=True)
                mm.then_inc(e["h_ready"], 1)

            def weigh_values(m, p):
                pe.wait_ge(e["pt_out"], 3 * (m + 1))
                pe.wait_ge(e["pt_out_v"], m + 1)
                for k, (a, z) in enumerate(BANKS):
                    for n in range(a, z):
                        mm = nc.tensor.matmul(ps[:, 3 + k, (n - a) * VW:(n - a + 1) * VW], PT[:, n, :], VA[p][:, n, :],
                                              start=True, stop=True)
                mm.then_inc(e["pv_ready"], 1)

            def values(f, p):
                at_least(pe, e["ht_out"], f - 1)
                at_least(pe, e["pt_out_v"], f)
                if isinstance(f, int):
                    pe.wait_ge(e["ds_ready"], f + 1)
                    at_least(pe, e["y_ready"], f - 1)
                for k in range(2):
                    nc.tensor.matmul(ps[0:C, 6 + k, :], CT[p][:, :], wv[:, k * 512:(k + 1) * 512], start=True, stop=True) \
                        .then_inc(e["v_ready"], 1)

            def scores(f, p):
                for k, (a, z) in enumerate(BANKS):
                    pe.wait_ge(e["z_out"], 3 * f + k + 1)
                    nc.tensor.matmul(ps[:, k, 0:(z - a) * C], XT[p][:, :], Z[:, a:z, :].rearrange("p n c -> p (n c)"),
                                     start=True, stop=True).then_inc(e["s_ready"], 1)

            def transpose_attn(m):
                pe.wait_ge(e["a_ready"], 3 * (m + 1))
                for k in range(2):
                    for c in range(4 * k, 4 * k + 4):
                        mm = nc.tensor.transpose(ps[:, 3 + k, (c % 4) * S:(c % 4 + 1) * S], A[:, c * 128:(c + 1) * 128], ident[:, :])
                    mm.then_inc(e["at_ready"], 1)

            def down(b):
                pe.wait_ge(e["ht_out"], b + 1)
                for k in range(FC):
                    mm = nc.tensor.matmul(ps[:, 5, 0:H], HT[:, k, :], w2[:, k, :], start=(k == 0), stop=(k == FC - 1))
                mm.then_inc(e["down_ready"], 1)

            def project_out(m, p):
                pe.wait_ge(e["at_out"], 2 * (m + 1))
                pe.wait_ge(e["v_out"], 2 * upto_last(m + 2))
                for c in range(CC):
                    nc.tensor.matmul(ps[:, 6, 0:H], AT[:, c, :], wo[:, c, :], start=(c == 0), stop=False)
                nc.tensor.matmul(ps[:, 6, 0:H], XT[p][:, :], ident[:, :], start=False, stop=True).then_inc(e["wo_ready"], 1)

            def step(t, p, front=True, mid=True, end=True):
                if front:
                    front1(t + 1, 1 - p)
                if mid:
                    transpose_probs(t)
                if end:
                    transpose_normed(t - 1)
                    up(t - 1)
                if mid:
                    weigh_values(t, p)
                if front:
                    values(t + 1, 1 - p)
                    scores(t + 1, 1 - p)
                if mid:
                    transpose_attn(t)
                if end:
                    down(t - 1)
                if mid:
                    project_out(t, p)

            pe.wait_ge(w_in, 16 * NW)
            step(-1, 1, mid=False, end=False)
            step(0, 0, end=False)
            step(1, 1)
            step(2, 0)
            by_pairs(pe, 3, B - 1, step)
            step(B - 1, 1, front=False)
            step(B, 0, front=False, mid=False)

        @block.scalar
        def _(act):
            def z_evict(f):
                at_least(act, e["s_ready"], 3 * f)
                for k, (a, z) in enumerate(BANKS[:2]):
                    act.wait_ge(e["z_ready"], 3 * f + k + 1)
                    nc.scalar.copy(Z[:, a:z, :], ps[:, k, 0:(z - a) * C].rearrange("p (n c) -> p n c", c=C)).then_inc(e["z_out"], 1)
                a, z = BANKS[2]
                act.wait_ge(e["z_ready"], 3 * f + 3)
                nc.scalar.copy(Z[:, a:z, :], ps[:, 2, 0:(z - a) * C].rearrange("p (n c) -> p n c", c=C)).then_inc(e["z_out"], 1)

            def probs_evict(m):
                for g, bank in enumerate((3, 4, 5)):
                    act.wait_ge(e["pt_ready"], 4 * m + g + 1)
                    if g == 0:
                        at_least(act, e["pv_ready"], m)
                    nc.scalar.copy(PT[:, 4 * g:4 * g + 4, :], ps[0:C, bank, :].rearrange("c (n q) -> c n q", n=4)).then_inc(e["pt_out"], 1)

            def normed_evict(b):
                act.wait_ge(e["zt_ready"], b + 1)
                at_least(act, e["h_ready"], b)
                nc.scalar.copy(ZT[:, :], ps[:, 6, 0:S]).then_inc(e["zt_out"], 1)

            def relu(b):
                act.wait_ge(e["h_ready"], b + 1)
                at_least(act, e["down_ready"], b)
                for k in range(FC):
                    last = nc.scalar.activation(HT[:, k, :], ps[:, 6, k * S:(k + 1) * S], ACT.Relu, bias=b1[:, k:k + 1])
                last.then_inc(e["ht_out"], 1)

            def values_evict(f, p):
                at_least(act, e["pv_ready"], f - 1)
                for k in range(2):
                    act.wait_ge(e["v_ready"], 2 * f + k + 1)
                    nc.scalar.copy(VA[p][:, 8 * k:8 * k + 8, 0:D], ps[0:C, 6 + k, :].rearrange("c (n d) -> c n d", d=D)).then_inc(e["v_out"], 1)

            def exps(f):
                for k, (a, z) in enumerate(BANKS):
                    act.wait_ge(e["s_centred"], 3 * f + k + 1)
                    nc.scalar.activation(P[:, a:z, :], P[:, a:z, :], ACT.Exp).then_inc(e["p_ready"], 1)

            def attn_evict(m):
                at_least(act, e["wo_ready"], m)
                for k in range(2):
                    act.wait_ge(e["at_ready"], 2 * m + k + 1)
                    nc.scalar.copy(AT[:, 4 * k:4 * k + 4, :], ps[:, 3 + k, :].rearrange("c (n q) -> c n q", n=4)).then_inc(e["at_out"], 1)

            def step(t, p, front=True, mid=True, end=True):
                if front:
                    z_evict(t + 1)
                if mid:
                    probs_evict(t)
                if end:
                    normed_evict(t - 1)
                    relu(t - 1)
                if front:
                    values_evict(t + 1, 1 - p)
                if mid:
                    attn_evict(t)
                if front:
                    exps(t + 1)

            act.wait_ge(pads, 1)
            act.wait_ge(w_in, 16 * NW)
            step(-1, 1, mid=False, end=False)
            step(0, 0, end=False)
            step(1, 1)
            step(2, 0)
            by_pairs(act, 3, B - 1, step)
            step(B - 1, 1, front=False)
            step(B, 0, front=False, mid=False)

        @block.vector
        def _(dve):
            def segment_diff(f):
                dve.wait_ge(e["dd_ready"], f + 1)
                at_least(dve, e["t_seg"], f)
                nc.vector.tensor_tensor(DS[:, :], ps[:, 7, 0:NH], DC[:, :], ALU.add).then_inc(e["ds_ready"], 1)

            def probs_evict(m):
                dve.wait_ge(e["pt_ready"], 4 * (m + 1))
                at_least(dve, e["pv_ready"], m)
                nc.vector.tensor_copy(PT[:, 12:16, :], ps[0:C, 7, :].rearrange("c (n q) -> c n q", n=4)).then_inc(e["pt_out_v"], 1)

            def normalise(m):
                dve.wait_ge(e["pv_ready"], m + 1)
                at_least(dve, e["a_ready"], 3 * m)
                for k, (a, z) in enumerate(BANKS):
                    o = ps[:, 3 + k, 0:(z - a) * VW].rearrange("p (n d) -> p n d", d=VW)
                    nc.vector.reciprocal(RS[:, a:z].unsqueeze(2), o[:, :, D:VW]).then_inc(e["sum_inv"], 1)
                at_least(dve, e["at_ready"], 2 * m)
                for k, (a, z) in enumerate(BANKS):
                    o = ps[:, 3 + k, 0:(z - a) * VW].rearrange("p (n d) -> p n d", d=VW)
                    dve.wait_ge(e["sum_inv"], 3 * m + k + 1)
                    nc.vector.tensor_tensor(A[:, a * D:z * D].rearrange("p (n d) -> p n d", d=D), o[:, :, 0:D],
                                            bcast_last(RS[:, a:z], D), ALU.mult).then_inc(e["a_ready"], 1)

            def add_max(f):
                at_least(dve, e["pt_ready"], 4 * f)
                at_least(dve, e["s_centred"], 3 * f)
                dve.wait_ge(e["t_ready"], f + 1)
                for k, (a, z) in enumerate(BANKS):
                    dve.wait_ge(e["s_ready"], 3 * f + k + 1)
                    nc.vector.tensor_tensor(P[:, a:z, :], ps[:, k, 0:(z - a) * C].rearrange("p (n c) -> p n c", c=C),
                                            T[:, a:z, :], ALU.add).then_inc(e["s_added"], 1)
                for k, (a, z) in enumerate(BANKS):
                    dve.wait_ge(e["s_added"], 3 * f + k + 1)
                    nc.vector.tensor_reduce(MX[:, a:z], P[:, a:z, :], AX.X, ALU.max).then_inc(e["s_max"], 1)
                    dve.wait_ge(e["s_max"], 3 * f + k + 1)
                    nc.vector.tensor_tensor(P[:, a:z, :], P[:, a:z, :], bcast_last(MX[:, a:z], C), ALU.subtract) \
                        .then_inc(e["s_centred"], 1)

            def layer_norm(k, b, source_ready):
                stat, var, rstd, nrm = (e[n + str(k + 1)] for n in ("stat", "var", "rstd", "nrm"))
                dve.wait_ge(source_ready, b + 1)
                at_least(dve, stat, 2 * b)
                nc.vector.bn_stats(st[:, k, :], Y[:, k, :]).then_inc(stat, 1)
                dve.wait_ge(stat, 2 * b + 1)
                dve.nop(nofuse=True)
                nc.vector.bn_aggr(mv[:, k, :], st[:, k, :]).then_inc(stat, 1)
                dve.wait_ge(stat, 2 * b + 2)
                nc.vector.tensor_scalar(ve[:, k:k + 1], mv[:, k, 1:2], EPS1, None, ALU.add).then_inc(var, 1)
                dve.wait_ge(rstd, b + 1)
                at_least(dve, e["gam" + str(k + 1)], b)
                nc.vector.tensor_scalar(NRM[:, k, :], Y[:, k, :], mv[:, k, 0:1], rs[:, k:k + 1], ALU.subtract, ALU.mult).then_inc(nrm, 1)

            def norm1(m):
                dve.wait_ge(e["wo_ready"], m + 1)
                at_least(dve, e["nrm1"], m)
                nc.vector.tensor_copy(Y[:, 0, :], ps[:, 6, 0:H]).then_inc(e["y_ready"], 1)
                layer_norm(0, m, e["y_ready"])

            def norm2(b):
                dve.wait_ge(e["down_ready"], b + 1)
                dve.wait_ge(e["zb_ready"], b + 1)
                at_least(dve, e["nrm2"], b)
                nc.vector.tensor_tensor(Y[:, 1, :], ps[:, 5, 0:H], ZB[:, :], ALU.add).then_inc(e["w_ready"], 1)
                layer_norm(1, b, e["w_ready"])

            def step(t, p, front=True, mid=True, end=True):
                if front:
                    segment_diff(t + 1)
                if mid:
                    probs_evict(t)
                    normalise(t)
                if front:
                    add_max(t + 1)
                if end:
                    norm2(t - 1)
                if mid:
                    norm1(t)

            for p in range(2):
                last = nc.vector.memset(VA[p][:, :, :], 1.0)
            last.then_inc(pads, 1)
            dve.wait_ge(w_in, 16 * NW)
            nc.vector.tensor_copy(seg[:, :], seg8[:, :])
            nc.vector.tensor_scalar(nm[:, :], nm[:, :], -1e30, None, ALU.mult).then_inc(e["seg_ready"], 1)
            step(-1, 1, mid=False, end=False)
            step(0, 0, end=False)
            step(1, 1)
            step(2, 0)
            by_pairs(dve, 3, B - 1, step)
            step(B - 1, 1, front=False)
            step(B, 0, front=False, mid=False)

        @block.gpsimd
        def _(pool):
            def fetch(f, p):
                at_least(pool, e["wo_ready"], f - 1)
                nc.gpsimd.tensor_copy(XT[p][:, :], x1T[:, f, :])
                nc.gpsimd.tensor_copy(CT[p][:, :], ctxT[:, f, :]).then_inc(e["xt_ready"], 1)

            def terms(f, p):
                pool.wait_ge(e["ds_ready"], f + 1)
                at_least(pool, e["s_added"], 3 * f)
                nc.gpsimd.tensor_tensor(T[:, :, :], bcast_mid(seg[:, :], NH), bcast_last(DS[:, :], C), ALU.mult).then_inc(e["t_seg"], 1)
                pool.wait_ge(e["t_seg"], f + 1)
                nc.gpsimd.tensor_tensor(T[:, :, :], T[:, :, :], bcast_mid(nm[:, :], NH), ALU.add).then_inc(e["t_mask"], 1)
                pool.wait_ge(e["t_mask"], f + 1)
                at_least(pool, bd_in[p], 16 * (f - p) + 32)
                nc.gpsimd.tensor_tensor(T[:, :, :], T[:, :, :], BD[p][:, :, 0:C], ALU.add).then_inc(e["t_ready"], 1)

            def weigh_norm(k, b, scale_row, shift_row, outp, done):
                var, rstd, nrm, gam = (e[n + str(k + 1)] for n in ("var", "rstd", "nrm", "gam"))
                pool.wait_ge(var, b + 1)
                at_least(pool, nrm, b)
                nc.gpsimd.tensor_tensor(rs[:, k:k + 1], ve[:, k:k + 1], halfneg[:, 0:1], ALU.pow).then_inc(rstd, 1)
                pool.wait_ge(nrm, b + 1)
                nc.gpsimd.tensor_tensor(NRM[:, k, :], NRM[:, k, :], rows[:, scale_row, :], ALU.mult).then_inc(gam, 1)
                pool.wait_ge(gam, b + 1)
                nc.gpsimd.tensor_tensor(outp, NRM[:, k, :], rows[:, shift_row, :], ALU.add).then_inc(done, 1)

            def norm1(m):
                at_least(pool, e["zt_ready"], m)
                at_least(pool, e["zb_ready"], m)
                weigh_norm(0, m, 0, 1, Z1[:, :], e["z1_ready"])
                pool.wait_ge(e["z1_ready"], m + 1)
                at_least(pool, e["w_ready"], m)
                nc.gpsimd.tensor_tensor(ZB[:, :], Z1[:, :], rows[:, 2, :], ALU.add).then_inc(e["zb_ready"], 1)

            def norm2(b, p):
                at_least(pool, stored[p], 8 * (b - p))
                weigh_norm(1, b, 3, 4, OUT[p][:, :], e["out_ready"])

            def step(t, p, front=True, mid=True, end=True):
                if front:
                    terms(t + 1, 1 - p)
                if end:
                    norm2(t - 1, 1 - p)
                if mid:
                    norm1(t)

            def step_fetch(t, p):
                step(t, p)
                fetch(t + 2, p)

            pool.wait_ge(w_in, 16 * NW)
            pool.wait_ge(e["seg_ready"], 1)
            fetch(0, 0)
            step(-1, 1, mid=False, end=False)
            fetch(1, 1)
            step(0, 0, end=False)
            fetch(2, 0)
            step_fetch(1, 1)
            step_fetch(2, 0)
            by_pairs(pool, 3, B - 3, step_fetch)
            step_fetch(B - 3, 1)
            step(B - 2, 0)
            step(B - 1, 1, front=False)
            step(B, 0, front=False, mid=False)


def build(nc, d, out):
    with ExitStack() as ctx:
        def sb(name, shape, dt=F32):
            return ctx.enter_context(nc.sbuf_tensor(name, shape, dt))

        ps = ctx.enter_context(nc.psum_tensor("ps", [128, 8, BANK], F32))
        bd = nc.dram_tensor("bd_scratch", [B, S, NH * CW1], F32, kind="Internal").ap()
        ident = sb("ident", [128, 128])
        ones = sb("ones", [128, 128])
        halfneg = sb("halfneg", [128, 2])
        x1T = sb("x1T", [128, B, S])
        c_in = ctx.enter_context(nc.semaphore("c_in"))
        with nc.Block() as block:
            @block.sync
            def _(sp):
                sp.dma_start(ident[:, :], d["ident"]).then_inc(c_in, 16)
                sp.wait_ge(c_in, 16)

            @block.vector
            def _(dve):
                nc.vector.memset(ones[:, :], 1.0)
                nc.vector.memset(halfneg[:, :], -0.5)
        layer0(nc, d, x1T, ident, ps, halfneg)
        t = {"MT": sb("MT", [128, NH, H]), "DW": sb("DW", [128, NH]), "DC": sb("DC", [128, NH]), "ctxT": sb("ctxT", [128, B, C])}
        with nc.sbuf_tensor("GM", [128, NH, J], F32) as GM, nc.sbuf_tensor("WT", [128, NH, J], F32) as WT, \
                nc.sbuf_tensor("U", [128, NH, CW1], F32) as U:
            t.update(GM=GM, WT=WT, U=U)
            prepare1(nc, d, t, ident, ones, ps)
            position_terms(nc, t, bd, x1T, ps)
        layer1(nc, d, t, bd, out, x1T, ident, ps, halfneg)


def layouts(i):
    import numpy as np
    a = {k: np.asarray(v) for k, v in i.items()}
    L0, L1 = "L0_xattn_", "L1_xattn_"
    order = [8 * (s // 8) + 4 * (s % 2) + (s % 8) // 2 for s in range(NH)]
    d = {}
    d["x"] = a["x"]
    d["xT"] = a["x"].transpose(0, 2, 1)
    d["ctx"] = a["ctx_1024"]
    d["ctxT"] = a["ctx_1024"].transpose(2, 0, 1)
    d["mask"] = a["mask_Bx1xSxS2_ff0"].reshape(B, S, C)
    d["cmask"] = a["mask_1x1xSxS2_ff0"].reshape(S, C)
    d["seg"] = a["mask_1xSxS2_bk1"].reshape(S, C)
    d["wq0"] = a[L0 + "Wq"].reshape(H, NH, D)[:, order].reshape(H, NH * D)
    d["wkv0"] = np.concatenate([a[L0 + "Wk"], a[L0 + "Wv"]], axis=1)
    d["wo0"] = a[L0 + "Wo"].reshape(CC, 128, H).transpose(1, 0, 2)
    d["wgu"] = np.concatenate([a[L0 + "Wgate"], a[L0 + "Wup"]], axis=1)
    d["wd"] = a[L0 + "Wdown"].reshape(FC, 128, H).transpose(1, 0, 2)
    d["lns"] = np.stack([a[L0 + "ln1_w"], a[L0 + "ln2_w"]], axis=1)
    d["wqT"] = a[L1 + "Wq"].reshape(H, CC, 128).transpose(2, 1, 0)
    d["wkT"] = a[L1 + "Wk"].reshape(H, CC, 128).transpose(2, 1, 0)
    d["wr1"] = a[L1 + "Wr"].reshape(H, NH * D)
    d["pos"] = a[L1 + "position_encoding"][0, 1:J + 1].T
    small = [a[L1 + "content_bias"], a[L1 + "position_bias"], a[L1 + "segment_bias"],
             a[L1 + "segment_encoding"][0], a[L1 + "segment_encoding"][1]]
    d["small"] = np.stack([s.reshape(CC, 128).T for s in small], axis=1)
    d["wv1"] = a[L1 + "Wv"].reshape(H, NH * D)
    d["wo1"] = a[L1 + "Wo"].reshape(H, CC, 128).transpose(2, 1, 0)
    d["w1"] = a[L1 + "W1"]
    d["w2"] = a[L1 + "W2"].reshape(FC, 128, H).transpose(1, 0, 2)
    d["b1"] = a[L1 + "b1"].reshape(FC, 128).T
    d["rows"] = np.stack([a[L1 + n] for n in ("ln1_gamma", "ln1_beta", "b2", "ln2_gamma", "ln2_beta")])
    inv = (1.0 / 10000.0 ** (np.arange(0, D, 2, dtype=np.float32) / np.float32(D))).astype(np.float32)
    ang = np.arange(S, dtype=np.float32)[:, None] * inv[None, :]
    cos, sin = np.cos(ang), np.sin(ang)
    row = np.concatenate([cos, cos, -sin, sin], axis=1).astype(np.float32)
    d["rope"] = np.stack([row, row], axis=1)
    d["ident"] = np.eye(128, dtype=np.float32)
    return {k: np.ascontiguousarray(v) for k, v in d.items()}


def kernel(**inputs):
    import numpy as np
    import concourse.bacc as bacc
    from concourse.bass_utils import run_bass_kernel_spmd

    nc = bacc.Bacc("TRN2", target_bir_lowering=False, num_devices=1)
    arrays, d = {}, {}
    for name, a in layouts(inputs).items():
        arrays[f"in_{name}_dram"] = a
        d[name] = nc.dram_tensor(f"in_{name}_dram", a.shape, mybir.dt.from_np(a.dtype), kind="ExternalInput").ap()
    out = nc.dram_tensor("out_0_dram", (B, S, H), F32, kind="ExternalOutput").ap()
    build(nc, d, out)
    r = run_bass_kernel_spmd(nc, [arrays], core_ids=[0])
    return r.results[0]["out_0_dram"]
```

```python
from contextlib import ExitStack

import concourse.bass as bass
from concourse import mybir

F32 = mybir.dt.float32
U8 = mybir.dt.uint8
ALU = mybir.AluOpType
ACT = mybir.ActivationFunctionType
AX = mybir.AxisListType

B, S, C, H = 64, 128, 77, 128
NH, D = 16, 64
CC = NH // 2
GKV = 4
FF = 512
FC = FF // 128
J = S + C - 1
CW1 = C + 1
BANKS = [(0, 6), (6, 11), (11, 16)]
Z_HEADS = [(0, 3), (3, 6), (6, 9), (9, 12), (12, 15), (15, 16)]
BANK = 512
S_BANKS = (6, 7, 0, 1)
SCALE = 1.0 / 8.0
EPS0, EPS1 = 1e-6, 1e-12
LATER_SHAPES = {"wr1": [128, NH * D], "pos": [128, J], "small": [128, 5, CC], "wqT": [128, CC, H], "wkT": [128, CC, H],
                "ctxT": [128, B, C], "wv1": [128, NH * D], "w1": [128, FF], "b1": [128, FC], "seg": [128, C],
                "cmask": [128, C], "wo1": [128, CC, H], "w2": [128, FC, H], "rows": [128, 5, H]}
LATER = len(LATER_SHAPES)


def at_least(eng, sem, value):
    if isinstance(value, int) and value <= 0:
        return
    eng.wait_ge(sem, value)


def upto_last(count):
    return min(count, B) if isinstance(count, int) else count


def dma_after(sp, sem, value):
    if isinstance(value, int):
        at_least(sp, sem, value)
    else:
        sp.wait_ge(sem, value)
        sp.nop(nofuse=True)


def by_pairs(eng, first, end, step):
    with eng.Fori(first // 2, end // 2) as half:
        for k in range(2):
            step(2 * half + (first % 2 + k), (first + k) % 2)


def active(b):
    return not isinstance(b, int) or 0 <= b < B


def steady_and_last(eng, step):
    for t in range(3):
        step(t, t % 2)
    by_pairs(eng, 3, B - 3, step)
    for t in range(B - 3, B + 2):
        step(t, t % 2)


def bcast_mid(ap, n):
    return ap.unsqueeze(1).to_broadcast([ap.shape[0], n, ap.shape[1]])


def bcast_last(ap, n):
    return ap.unsqueeze(2).to_broadcast([ap.shape[0], ap.shape[1], n])


def layer0(nc, d, x1T, ident, ps, halfneg, load_later):
    with ExitStack() as ctx:
        def sb(name, shape, dt=F32):
            return ctx.enter_context(nc.sbuf_tensor("l0_" + name, shape, dt))

        def sem(name):
            return ctx.enter_context(nc.semaphore("l0_" + name))

        wq = sb("wq", [128, NH * D])
        wkv = sb("wkv", [128, 2 * GKV * D])
        wo = sb("wo", [128, CC, H])
        wgu = sb("wgu", [128, 2 * FF])
        wd = sb("wd", [128, FC, H])
        lns = sb("lns", [128, 2])
        rope_q = sb("rope_q", [128, 2 * D])
        rope_k = sb("rope_k", [C, 2 * D])
        XC = [sb(f"XC{p}", [128, 2, H]) for p in range(2)]
        XT = [sb(f"XT{p}", [128, S]) for p in range(2)]
        CT = [sb(f"CT{p}", [128, C]) for p in range(2)]
        MK = [sb(f"MK{p}", [128, C]) for p in range(2)]
        XR = [sb(f"XR{p}", [128, H]) for p in range(2)]
        sq = sb("sq", [128, 2, H])
        ss = sb("ss", [128, 2])
        ms = sb("ms", [128, 2])
        rstd = [sb(f"rstd{p}", [128, 2]) for p in range(2)]
        KS = sb("KS", [C, GKV * D])
        KA = sb("KA", [C, GKV * D])
        KB = sb("KB", [C, GKV * D])
        VA = [sb(f"VA{p}", [C, GKV, D]) for p in range(2)]
        QE = sb("QE", [128, NH * D])
        QA = sb("QA", [128, NH, D])
        QB = sb("QB", [128, NH, D])
        QT = sb("QT", [128, CC, S])
        KT = sb("KT", [128, 2, 2, C])
        P = sb("P", [128, NH, C])
        MX = sb("MX", [128, NH])
        PT = sb("PT", [C, NH, S])
        RS = sb("RS", [128, NH])
        AT = sb("AT", [128, CC, S])
        XP = [sb(f"XP{p}", [128, H]) for p in range(2)]
        sq2 = sb("sq2", [128, H])
        ss2 = sb("ss2", [128, 1])
        ms2 = sb("ms2", [128, 1])
        rs2 = sb("rs2", [128, 1])
        HN = sb("HN", [128, H])
        HNT = sb("HNT", [128, S])
        TH = sb("TH", [128, FF])
        SG = sb("SG", [128, FF])
        HT = sb("HT", [128, FC, S])

        w_first, w_rest = sem("w_first"), sem("w_rest")
        x_in = [sem(f"x_in{p}") for p in range(2)]
        mk_in = [sem(f"mk_in{p}") for p in range(2)]
        xr_in = [sem(f"xr_in{p}") for p in range(2)]
        w_scaled = sem("w_scaled")
        pads = sem("pads")
        squared, summed, mean_ready, rstd_ready = (sem(n) for n in ("squared", "summed", "mean_ready", "rstd_ready"))
        q_ready, q_out, kv_ready, kv_out = (sem(n) for n in ("q_ready", "q_out", "kv_ready", "kv_out"))
        q_sin, q_cos, q_roped, k_parts, k_roped = (sem(n) for n in ("q_sin", "q_cos", "q_roped", "k_parts", "k_roped"))
        qt_ready, kt_ready, qt_out, kt_out = sem("qt_ready"), sem("kt_ready"), sem("qt_out"), sem("kt_out")
        s_ready, s_masked, s_max, s_centred, p_ready = (sem(n) for n in ("s_ready", "s_masked", "s_max", "s_centred", "p_ready"))
        pt_ready, pt_out = sem("pt_ready"), sem("pt_out")
        sum_ready, sum_inv, p_normed = sem("sum_ready"), sem("sum_inv"), sem("p_normed")
        pv_ready, at_out, wo_ready, xp_ready = sem("pv_ready"), sem("at_out"), sem("wo_ready"), sem("xp_ready")
        sq2_ready, mean2_ready, rstd2_ready, hn_ready = (sem(n) for n in ("sq2_ready", "mean2_ready", "rstd2_ready", "hn_ready"))
        hnt_ready, hnt_out, gate_ready, up_ready = (sem(n) for n in ("hnt_ready", "hnt_out", "gate_ready", "up_ready"))
        tanh_ready, silu_ready, ht_ready = sem("tanh_ready"), sem("silu_ready"), sem("ht_ready")
        down_ready, x1t_out = sem("down_ready"), sem("x1t_out")
        block = ctx.enter_context(nc.Block())


        @block.sync
        def _(sp):
            def load(b, p):
                dma_after(sp, squared, b - 1)
                dma_after(sp, q_ready, 2 * (b - 1))
                dma_after(sp, kv_ready, b - 1)
                sp.dma_start(XC[p][:, 0, :], d["x"][b, :, :]).then_inc(x_in[p], 16)
                sp.dma_start(XC[p][0:C, 1, :], d["ctx"][b, :, :]).then_inc(x_in[p], 16)
                sp.dma_start(XT[p][:, :], d["xT"][b, :, :]).then_inc(x_in[p], 16)
                sp.dma_start(CT[p][:, :], d["ctxT"][:, b, :]).then_inc(x_in[p], 16)

            def load_mask(b, p):
                dma_after(sp, s_masked, 2 * (b - 1))
                sp.dma_start(MK[p][:, :], d["mask"][b, :, :]).then_inc(mk_in[p], 16)

            def load_residual(b, p):
                dma_after(sp, xp_ready, b - 1)
                sp.dma_start(XR[p][:, :], d["x"][b, :, :]).then_inc(xr_in[p], 16)

            sp.wait_ge(pads, 1)
            load(0, 0)
            for t, n in ((lns, "lns"), (wq, "wq0"), (wkv, "wkv0")):
                sp.dma_start(t[:, :], d[n]).then_inc(w_first, 16)
            sp.dma_start(rope_q[:, :], d["rope"][:, 0, :]).then_inc(w_first, 16)
            sp.dma_start(rope_k[:, :], d["rope"][0:C, 1, :]).then_inc(w_first, 16)
            load(1, 1)
            load_mask(0, 0)
            load_mask(1, 1)
            sp.dma_start(wo[:, :, :], d["wo0"]).then_inc(w_rest, 16)
            sp.dma_start(wgu[:, :], d["wgu"]).then_inc(w_rest, 16)
            sp.dma_start(wd[:, :, :], d["wd"]).then_inc(w_rest, 16)
            load_residual(0, 0)

            def both(b, p):
                load(b, p)
                load_mask(b, p)
                load_residual(b - 1, 1 - p)
            both(2, 0)
            both(3, 1)
            by_pairs(sp, 4, B, both)
            load_residual(B - 1, 1)

        @block.tensor
        def _(pe):
            def project(f, p):
                pe.wait_ge(x_in[p], 32 * (f - p) + 64)
                at_least(pe, s_masked, 2 * f)
                for k in range(2):
                    nc.tensor.matmul(ps[:, k, :], XT[p][:, :], wq[:, k * 512:(k + 1) * 512], start=True, stop=True) \
                        .then_inc(q_ready, 1)

            def project_kv(f, p):
                nc.tensor.matmul(ps[0:C, 2, :], CT[p][:, :], wkv[:, :], start=True, stop=True).then_inc(kv_ready, 1)

            def transpose_probs(m):
                for g, bank in enumerate((6, 7, 0, 1)):
                    if g % 2 == 0:
                        pe.wait_ge(p_normed, 2 * m + g // 2 + 1)
                    if g == 2:
                        pe.wait_ge(q_out, 2 * upto_last(m + 2))
                    for n in range(4 * g, 4 * g + 4):
                        mm = nc.tensor.transpose(ps[0:C, bank, (n % 4) * S:(n % 4 + 1) * S], P[:, n, :], ident[:, :])
                    mm.then_inc(pt_ready, 1)

            def weigh_values(m, p, k):
                pe.wait_ge(pt_out, 4 * m + 2 + 2 * k)
                for u in range(2):
                    g = 2 * k + u
                    mm = nc.tensor.matmul(ps[64 * u:64 * u + 64, 6 + k, :], VA[p][:, g, :],
                                          PT[:, 8 * k + u:8 * k + 8:2, :], start=True, stop=True)
                mm.then_inc(pv_ready, 1)

            def transpose_k(f):
                pe.wait_ge(kv_out, f + 1)
                pe.wait_ge(k_roped, f + 1)
                for a in range(2):
                    mm = nc.tensor.transpose(ps[:, 2, a * C:(a + 1) * C], KA[:, a * 128:(a + 1) * 128], ident[0:C, 0:C])
                mm.then_inc(kt_ready, 1)

            def transpose_q(f, k):
                pe.wait_ge(q_roped, f + 1)
                for c in range(4 * k, 4 * k + 4):
                    mm = nc.tensor.transpose(ps[:, k, (c % 4) * S:(c % 4 + 1) * S],
                                             QA[:, 2 * c:2 * c + 2, :].rearrange("q u d -> q (u d)"), ident[:, :])
                mm.then_inc(qt_ready, 1)

            def scores(f):
                pe.wait_ge(kt_out, f + 1)
                at_least(pe, at_out, 2 * f)
                for k in range(2):
                    pe.wait_ge(qt_out, 2 * f + k + 1)
                    for c in range(4 * k, 4 * k + 4):
                        mm = nc.tensor.matmul(ps[:, S_BANKS[c // 2], (c % 2) * 2 * C:(c % 2 + 1) * 2 * C], QT[:, c, :],
                                              KT[:, k, :, :].rearrange("p u c -> p (u c)"), start=True, stop=True)
                    mm.then_inc(s_ready, 1)

            def project_out(m):
                pe.wait_ge(at_out, 2 * (m + 1))
                at_least(pe, hnt_out, m)
                for c in range(CC):
                    mm = nc.tensor.matmul(ps[:, 5, 0:H], AT[:, c, :], wo[:, c, :], start=(c == 0), stop=(c == CC - 1))
                mm.then_inc(wo_ready, 1)

            def transpose_normed(e):
                pe.wait_ge(hn_ready, e + 1)
                nc.tensor.transpose(ps[:, 5, 0:S], HN[:, :], ident[:, :]).then_inc(hnt_ready, 1)

            def gate(e):
                pe.wait_ge(hnt_out, e + 1)
                at_least(pe, x1t_out, e)
                for k in range(FC):
                    mm = nc.tensor.matmul(ps[:, 3, k * S:(k + 1) * S], wgu[:, k * 128:(k + 1) * 128], HNT[:, :],
                                          start=True, stop=True)
                mm.then_inc(gate_ready, 1)

            def up(e):
                for k in range(FC):
                    mm = nc.tensor.matmul(ps[:, 4, k * S:(k + 1) * S], wgu[:, FF + k * 128:FF + (k + 1) * 128], HNT[:, :],
                                          start=True, stop=True)
                mm.then_inc(up_ready, 1)

            def down(e, p):
                pe.wait_ge(ht_ready, e + 1)
                for k in range(FC):
                    nc.tensor.matmul(ps[:, 3, 0:S], wd[:, k, :], HT[:, k, :], start=(k == 0), stop=False)
                nc.tensor.matmul(ps[:, 3, 0:S], XP[p][:, :], ident[:, :], start=False, stop=True).then_inc(down_ready, 1)

            def step(t, p):
                if active(t):
                    transpose_probs(t)
                    weigh_values(t, p, 0)
                    weigh_values(t, p, 1)
                if active(t + 1):
                    transpose_k(t + 1)
                    transpose_q(t + 1, 0)
                if active(t - 2):
                    down(t - 2, p)
                if active(t + 1):
                    transpose_q(t + 1, 1)
                if active(t - 1):
                    transpose_normed(t - 1)
                if active(t + 1):
                    scores(t + 1)
                if active(t - 1):
                    gate(t - 1)
                if active(t + 2):
                    project(t + 2, p)
                if active(t - 1):
                    up(t - 1)
                if active(t + 2):
                    project_kv(t + 2, p)
                if active(t):
                    project_out(t)

            pe.wait_ge(w_first, 16 * 5)
            pe.wait_ge(w_scaled, 1)
            for t in range(-3, 0):
                step(t, t % 2)
            pe.wait_ge(w_rest, 16 * 3)
            pe.wait_ge(w_scaled, 2)
            steady_and_last(pe, step)

        @block.scalar
        def _(act):
            def probs_evict(m):
                at_least(act, pv_ready, 2 * m)
                for g, bank in enumerate((6, 7, 0, 1)):
                    act.wait_ge(pt_ready, 4 * m + g + 1)
                    nc.scalar.copy(PT[:, 4 * g:4 * g + 4, :], ps[0:C, bank, :].rearrange("c (n q) -> c n q", n=4)).then_inc(pt_out, 1)

            def attn_evict(m):
                at_least(act, wo_ready, m)
                for k in range(2):
                    act.wait_ge(pv_ready, 2 * m + k + 1)
                    nc.scalar.copy(AT[:, 4 * k:4 * k + 4, :], ps[:, 6 + k, :].rearrange("c (n q) -> c n q", n=4)).then_inc(at_out, 1)

            def k_evict(f):
                at_least(act, s_ready, 2 * f)
                act.wait_ge(kt_ready, f + 1)
                for u in range(2):
                    h = slice(64 * u, 64 * u + 64)
                    last = nc.scalar.copy(KT[h, :, u, :], ps[h, 2, 0:2 * C].rearrange("p (a c) -> p a c", a=2))
                last.then_inc(kt_out, 1)

            def qt_evict(f, k):
                act.wait_ge(qt_ready, 2 * f + k + 1)
                nc.scalar.copy(QT[:, 4 * k:4 * k + 4, :], ps[:, k, :].rearrange("c (n q) -> c n q", n=4)).then_inc(qt_out, 1)

            def x1_evict(e):
                act.wait_ge(down_ready, e + 1)
                nc.scalar.copy(x1T[:, e, :], ps[:, 3, 0:S]).then_inc(x1t_out, 1)

            def normed_evict(e):
                act.wait_ge(hnt_ready, e + 1)
                at_least(act, up_ready, e)
                nc.scalar.copy(HNT[:, :], ps[:, 5, 0:S]).then_inc(hnt_out, 1)

            def tanh(e):
                act.wait_ge(gate_ready, e + 1)
                at_least(act, silu_ready, e)
                nc.scalar.activation(TH[:, :], ps[:, 3, :], ACT.Tanh, scale=0.5).then_inc(tanh_ready, 1)

            def exps(f, k):
                act.wait_ge(s_centred, 2 * f + k + 1)
                nc.scalar.activation(P[:, 8 * k:8 * k + 8, :], P[:, 8 * k:8 * k + 8, :], ACT.Exp).then_inc(p_ready, 1)

            def q_evict(f, p, k):
                if k == 0:
                    act.wait_ge(rstd_ready, f + 1)
                    at_least(act, q_sin, f)
                    at_least(act, q_cos, f)
                act.wait_ge(q_ready, 2 * f + k + 1)
                nc.scalar.activation(QE[:, 512 * k:512 * k + 512], ps[:, k, :], ACT.Copy, scale=rstd[p][:, 0:1]).then_inc(q_out, 1)

            def kv_evict(f, p):
                act.wait_ge(kv_ready, f + 1)
                at_least(act, k_parts, f)
                at_least(act, pv_ready, 2 * (f - 1))
                nc.scalar.activation(KS[:, :], ps[0:C, 2, 0:GKV * D], ACT.Copy, scale=rstd[p][0:C, 1:2])
                nc.scalar.activation(VA[p][:, :, :], ps[0:C, 2, GKV * D:].rearrange("c (g d) -> c g d", g=GKV),
                                     ACT.Copy, scale=rstd[p][0:C, 1:2]).then_inc(kv_out, 1)

            def step(t, p):
                if active(t):
                    probs_evict(t)
                    attn_evict(t)
                if active(t + 1):
                    k_evict(t + 1)
                    qt_evict(t + 1, 0)
                if active(t - 2):
                    x1_evict(t - 2)
                if active(t + 1):
                    qt_evict(t + 1, 1)
                if active(t - 1):
                    normed_evict(t - 1)
                    tanh(t - 1)
                if active(t + 1):
                    exps(t + 1, 0)
                if active(t + 2):
                    q_evict(t + 2, p, 0)
                if active(t + 1):
                    exps(t + 1, 1)
                if active(t + 2):
                    q_evict(t + 2, p, 1)
                if active(t + 2):
                    kv_evict(t + 2, p)

            act.wait_ge(pads, 2)
            for t in range(-3, 0):
                step(t, t % 2)
            load_later(nc.scalar)
            steady_and_last(act, step)

        @block.vector
        def _(dve):
            def mask_max(f, p):
                at_least(dve, pt_ready, 4 * f)
                at_least(dve, s_centred, 2 * f)
                dve.wait_ge(mk_in[p], 8 * (f - p) + 16)
                for k in range(2):
                    dve.wait_ge(s_ready, 2 * f + k + 1)
                    b0 = S_BANKS[2 * k]
                    sc = ps[:, b0:b0 + 2, 0:4 * C].rearrange("p k (n c) -> p k n c", c=C)
                    mk = MK[p][:, :].unsqueeze(1).unsqueeze(1).to_broadcast([128, 2, 4, C])
                    nc.vector.tensor_tensor(P[:, 8 * k:8 * k + 8, :].rearrange("p (k n) c -> p k n c", k=2), sc, mk,
                                            ALU.add).then_inc(s_masked, 1)
                    dve.wait_ge(s_masked, 2 * f + k + 1)
                    nc.vector.tensor_reduce(MX[:, 8 * k:8 * k + 8], P[:, 8 * k:8 * k + 8, :], AX.X, ALU.max).then_inc(s_max, 1)

            def normalise(f):
                for k in range(2):
                    a, z = 8 * k, 8 * k + 8
                    dve.wait_ge(p_ready, 2 * f + k + 1)
                    at_least(dve, p_normed, 2 * f)
                    nc.vector.tensor_reduce(RS[:, a:z], P[:, a:z, :], AX.X, ALU.add).then_inc(sum_ready, 1)
                    dve.wait_ge(sum_ready, 2 * f + k + 1)
                    nc.vector.reciprocal(RS[:, a:z], RS[:, a:z]).then_inc(sum_inv, 1)
                    dve.wait_ge(sum_inv, 2 * f + k + 1)
                    nc.vector.tensor_tensor(P[:, a:z, :], P[:, a:z, :], bcast_last(RS[:, a:z], C), ALU.mult).then_inc(p_normed, 1)

            def rope(f):
                dve.wait_ge(q_out, 2 * (f + 1))
                at_least(dve, q_roped, f)
                q = QE[:, :].rearrange("p (n d) -> p n d", d=D)
                nc.vector.tensor_tensor(QB[:, :, 0:D // 2], q[:, :, D // 2:], bcast_mid(rope_q[:, D:D + D // 2], NH), ALU.mult)
                nc.vector.tensor_tensor(QB[:, :, D // 2:], q[:, :, 0:D // 2], bcast_mid(rope_q[:, D + D // 2:], NH),
                                        ALU.mult).then_inc(q_sin, 1)
                dve.wait_ge(q_sin, f + 1)
                dve.wait_ge(q_cos, f + 1)
                nc.vector.tensor_tensor(QA[:, :, :], QA[:, :, :], QB[:, :, :], ALU.add).then_inc(q_roped, 1)

            def silu(e):
                dve.wait_ge(tanh_ready, e + 1)
                at_least(dve, ht_ready, e)
                nc.vector.scalar_tensor_tensor(SG[:, :], TH[:, :], 1.0, ps[:, 3, :], ALU.add, ALU.mult).then_inc(silu_ready, 1)
                dve.wait_ge(silu_ready, e + 1)
                dve.wait_ge(up_ready, e + 1)
                at_least(dve, down_ready, e)
                nc.vector.tensor_tensor(HT[:, :, :].rearrange("p k q -> p (k q)"), SG[:, :], ps[:, 4, :], ALU.mult).then_inc(ht_ready, 1)

            def residual(m, p):
                dve.wait_ge(wo_ready, m + 1)
                dve.wait_ge(xr_in[p], 8 * (m - p) + 16)
                at_least(dve, down_ready, m - 1)
                nc.vector.tensor_tensor(XP[p][:, :], ps[:, 5, 0:H], XR[p][:, :], ALU.add).then_inc(xp_ready, 1)
                dve.wait_ge(xp_ready, m + 1)
                nc.vector.tensor_tensor(sq2[:, :], XP[p][:, :], XP[p][:, :], ALU.mult).then_inc(sq2_ready, 1)
                dve.wait_ge(sq2_ready, 2 * m + 1)
                nc.vector.tensor_reduce(ss2[:, :], sq2[:, :], AX.X, ALU.add).then_inc(sq2_ready, 1)
                dve.wait_ge(sq2_ready, 2 * m + 2)
                nc.vector.tensor_scalar(ms2[:, :], ss2[:, :], 1.0 / H, EPS0, ALU.mult, ALU.add).then_inc(mean2_ready, 1)

            def normed(m, p):
                dve.wait_ge(rstd2_ready, m + 1)
                at_least(dve, hnt_ready, m)
                nc.vector.tensor_scalar(HN[:, :], XP[p][:, :], rs2[:, 0:1], None, ALU.mult).then_inc(hn_ready, 1)

            def mean_squares(f, p):
                dve.wait_ge(x_in[p], 32 * (f - p) + 64)
                at_least(dve, summed, f)
                nc.vector.tensor_tensor(sq[:, :, :], XC[p][:, :, :], XC[p][:, :, :], ALU.mult).then_inc(squared, 1)
                dve.wait_ge(squared, f + 1)
                nc.vector.tensor_reduce(ss[:, :], sq[:, :, :], AX.X, ALU.add).then_inc(summed, 1)
                dve.wait_ge(summed, f + 1)
                at_least(dve, rstd_ready, f)
                nc.vector.tensor_scalar(ms[:, :], ss[:, :], 1.0 / H, EPS0, ALU.mult, ALU.add).then_inc(mean_ready, 1)

            def step(t, p):
                if active(t + 1):
                    mask_max(t + 1, 1 - p)
                    normalise(t + 1)
                if active(t + 2):
                    rope(t + 2)
                if active(t - 1):
                    silu(t - 1)
                if active(t):
                    residual(t, p)
                if active(t + 3):
                    mean_squares(t + 3, 1 - p)
                if active(t):
                    normed(t, p)

            for p in range(2):
                last = nc.vector.memset(XC[p][:, :, :], 0.0)
            last.then_inc(pads, 1)
            nc.vector.memset(KT[:, :, :, :], 0.0).then_inc(pads, 1)
            step(-3, 1)
            dve.wait_ge(w_first, 16 * 5)
            nc.vector.tensor_scalar(wq[:, :], wq[:, :], lns[:, 0:1], None, ALU.mult)
            nc.vector.tensor_scalar(wkv[:, :], wkv[:, :], lns[:, 0:1], None, ALU.mult)
            nc.vector.tensor_scalar(rope_q[:, :], rope_q[:, :], SCALE, None, ALU.mult).then_inc(w_scaled, 1)
            dve.wait_ge(w_scaled, 1)
            step(-2, 0)
            step(-1, 1)
            dve.wait_ge(w_rest, 16 * 3)
            nc.vector.tensor_scalar(wgu[:, :], wgu[:, :], lns[:, 1:2], None, ALU.mult)
            nc.vector.tensor_scalar(wd[:, :, :], wd[:, :, :], 0.5, None, ALU.mult).then_inc(w_scaled, 1)
            steady_and_last(dve, step)

        @block.gpsimd
        def _(pool):
            def centre(f):
                for k in range(2):
                    pool.wait_ge(s_max, 2 * f + k + 1)
                    nc.gpsimd.tensor_tensor(P[:, 8 * k:8 * k + 8, :], P[:, 8 * k:8 * k + 8, :],
                                            bcast_last(MX[:, 8 * k:8 * k + 8], C), ALU.subtract).then_inc(s_centred, 1)

            def rope_cos(f):
                pool.wait_ge(q_out, 2 * (f + 1))
                at_least(pool, qt_ready, 2 * f)
                nc.gpsimd.tensor_tensor(QA[:, :, :], QE[:, :].rearrange("p (n d) -> p n d", d=D), bcast_mid(rope_q[:, 0:D], NH),
                                        ALU.mult).then_inc(q_cos, 1)

            def rope_keys(f):
                pool.wait_ge(kv_out, f + 1)
                at_least(pool, kt_ready, f)
                at_least(pool, k_roped, f)
                k = KS[:, :].rearrange("c (g d) -> c g d", d=D)
                ka = KA[:, :].rearrange("c (g d) -> c g d", d=D)
                kb = KB[:, :].rearrange("c (g d) -> c g d", d=D)
                h = D // 2
                nc.gpsimd.tensor_tensor(ka, k, bcast_mid(rope_k[:, 0:D], GKV), ALU.mult)
                nc.gpsimd.tensor_tensor(kb[:, :, 0:h], k[:, :, h:], bcast_mid(rope_k[:, D:D + h], GKV), ALU.mult)
                nc.gpsimd.tensor_tensor(kb[:, :, h:], k[:, :, 0:h], bcast_mid(rope_k[:, D + h:], GKV), ALU.mult).then_inc(k_parts, 1)
                pool.wait_ge(k_parts, f + 1)
                nc.gpsimd.tensor_tensor(KA[:, :], KA[:, :], KB[:, :], ALU.add).then_inc(k_roped, 1)

            def rstd_x(f, p):
                pool.wait_ge(mean_ready, f + 1)
                at_least(pool, kv_out, f - 1)
                at_least(pool, q_out, 2 * (f - 1))
                nc.gpsimd.tensor_tensor(rstd[p][:, :], ms[:, :], halfneg[:, 0:2], ALU.pow).then_inc(rstd_ready, 1)

            def rstd_mlp(m):
                pool.wait_ge(mean2_ready, m + 1)
                at_least(pool, hn_ready, m)
                nc.gpsimd.tensor_tensor(rs2[:, :], ms2[:, :], halfneg[:, 0:1], ALU.pow).then_inc(rstd2_ready, 1)

            def step(t, p):
                if active(t + 1):
                    centre(t + 1)
                if active(t + 2):
                    rope_cos(t + 2)
                    rope_keys(t + 2)
                if active(t):
                    rstd_mlp(t)
                if active(t + 3):
                    rstd_x(t + 3, 1 - p)

            step(-3, 1)
            pool.wait_ge(w_first, 16 * 5)
            pool.wait_ge(w_scaled, 1)
            step(-2, 0)
            step(-1, 1)
            steady_and_last(pool, step)


def prepare1(nc, d, t, ident, ones, ps):
    MT, GM, WT, U, DW, DC, ctxT = t["MT"], t["GM"], t["WT"], t["U"], t["DW"], t["DC"], t["ctxT"]
    with ExitStack() as ctx:
        def sb(name, shape, dt=F32):
            return ctx.enter_context(nc.sbuf_tensor("pr_" + name, shape, dt))

        def sem(name):
            return ctx.enter_context(nc.semaphore("pr_" + name))

        wqT, wkT, wr, pos, small, w_in = (t[n] for n in ("wqT", "wkT", "wr1", "pos", "small", "later_in"))
        rT = sb("rT", [128, CC, J])
        rS = sb("rS", [128, CC, J])
        dse = sb("dse", [128, CC])
        pr = sb("pr", [128, 2, CC])
        bc = sb("bc", [128, NH])
        cw = sb("cw", [128, NH])
        cb, pb, sbias, se0, se1 = (small[:, k, :] for k in range(5))
        r_ready, r_out, rs_out, small_out = (sem(n) for n in ("r_ready", "r_out", "rs_out", "small_out"))
        step_ready, step_out, dse_out, u_ready, u_out, consts = (sem(n) for n in ("step_ready", "step_out", "dse_out", "u_ready", "u_out", "consts"))
        block = ctx.enter_context(nc.Block())

        @block.tensor
        def _(pe):
            pe.wait_ge(w_in, 16 * LATER)
            for c in range(CC):
                nc.tensor.matmul(ps[:, c, 0:J], wr[:, c * 128:(c + 1) * 128], pos[:, :], start=True, stop=True).then_inc(r_ready, 1)
            pe.wait_ge(small_out, 1)
            s = 0
            for n in range(NH):
                if s < 8:
                    pe.wait_ge(rs_out, s + 1)
                    pe.wait_ge(r_out, s + 1)
                else:
                    pe.wait_ge(step_out, s - 7)
                o = 64 * (n % 2)
                nc.tensor.matmul(ps[:, s % 8, 0:J], wqT[o:o + 64, n // 2, :], rS[o:o + 64, n // 2, :],
                                 start=True, stop=True).then_inc(step_ready, 1)
                s += 1
            pe.wait_ge(r_out, 2 * CC)
            for n in range(NH):
                pe.wait_ge(step_out, s - 7)
                o = 64 * (n % 2)
                nc.tensor.matmul(ps[:, s % 8, 0:J], ones[o:o + 64, :], rT[o:o + 64, n // 2, :],
                                 start=True, stop=True).then_inc(step_ready, 1)
                s += 1
            for g in range(4):
                pe.wait_ge(step_out, s - 7)
                for k in range(4):
                    o, c = 64 * (g % 2), 4 * (g // 2) + k
                    mm = nc.tensor.matmul(ps[:, s % 8, k * H:(k + 1) * H], wkT[o:o + 64, c, :], wqT[o:o + 64, c, :],
                                          start=True, stop=True)
                mm.then_inc(step_ready, 1)
                s += 1
            pe.wait_ge(small_out, 2)
            for u in range(2):
                o = 64 * u
                pe.wait_ge(step_out, s - 7)
                for c in range(CC):
                    mm = nc.tensor.matmul(ps[:, s % 8, c:c + 1], wkT[o:o + 64, c, :], cb[o:o + 64, c:c + 1], start=True, stop=True)
                mm.then_inc(step_ready, 1)
                s += 1
            for u in range(2):
                o = 64 * u
                pe.wait_ge(step_out, s - 7)
                for c in range(CC):
                    mm = nc.tensor.matmul(ps[:, s % 8, c:c + 1], wqT[o:o + 64, c, :], dse[o:o + 64, c:c + 1], start=True, stop=True)
                mm.then_inc(step_ready, 1)
                s += 1
            for u in range(2):
                o = 64 * u
                pe.wait_ge(step_out, s - 7)
                for k in range(2):
                    mm = nc.tensor.matmul(ps[:, s % 8, k * CC:(k + 1) * CC], ones[o:o + 64, :], pr[o:o + 64, k, :],
                                          start=True, stop=True)
                mm.then_inc(step_ready, 1)
                s += 1
            pe.wait_ge(step_out, s)
            for c in range(CW1):
                o = ps[:, c // 26, (c % 26) * NH:(c % 26 + 1) * NH]
                if c > 0:
                    mm = nc.tensor.matmul(o[0:64, :], ctxT[:, :, c - 1], cw[:, :], start=True, stop=True)
                if c < C:
                    nc.tensor.matmul(o[64:128, :], ctxT[:, :, c], cw[:, :], start=True, stop=True)
            mm.then_inc(u_ready, 1)

        @block.vector
        def _(dve):
            dve.wait_ge(w_in, 16 * LATER)
            nc.vector.memset(U[:, :, :], 0.0).then_inc(dse_out, 0 + 1)
            nc.vector.tensor_tensor(dse[:, :], se1, se0, ALU.subtract).then_inc(small_out, 1)
            dve.wait_ge(small_out, 1)
            nc.vector.tensor_tensor(pr[:, 0, :], sbias, se0, ALU.mult)
            nc.vector.tensor_tensor(pr[:, 1, :], sbias, dse[:, :], ALU.mult).then_inc(small_out, 1)
            for c in range(CC):
                dve.wait_ge(r_ready, c + 1)
                nc.vector.tensor_scalar(rS[:, c, :], ps[:, c, 0:J], se0[:, c:c + 1], None, ALU.add).then_inc(rs_out, 1)
                nc.vector.tensor_copy(rT[:, c, :], ps[:, c, 0:J]).then_inc(r_out, 1)
            for c in range(CC):
                dve.wait_ge(r_out, c + 1)
                nc.vector.tensor_scalar(rT[:, c, :], rT[:, c, :], pb[:, c:c + 1], None, ALU.mult).then_inc(r_out, 1)
            s = 0
            for table in (GM, WT):
                for n in range(NH):
                    dve.wait_ge(step_ready, s + 1)
                    nc.vector.tensor_scalar(table[:, n, :], ps[:, s % 8, 0:J], SCALE, None, ALU.mult).then_inc(step_out, 1)
                    s += 1
            for g in range(4):
                dve.wait_ge(step_ready, s + 1)
                first = 8 * (g // 2) + g % 2
                nc.vector.tensor_scalar(MT[:, first:first + 7:2, :], ps[:, s % 8, :].rearrange("p (n h) -> p n h", n=4), SCALE, None,
                                        ALU.mult).then_inc(step_out, 1)
                s += 1
            for table in (cw, DW):
                for u in range(2):
                    dve.wait_ge(step_ready, s + 1)
                    nc.vector.tensor_scalar(table[:, u:NH:2], ps[:, s % 8, 0:CC], SCALE, None, ALU.mult).then_inc(step_out, 1)
                    s += 1
            for u in range(2):
                dve.wait_ge(step_ready, s + 1)
                nc.vector.tensor_scalar(bc[:, u:NH:2], ps[:, s % 8, 0:CC], SCALE, None, ALU.mult)
                nc.vector.tensor_scalar(DC[:, u:NH:2], ps[:, s % 8, CC:2 * CC], SCALE, None, ALU.mult).then_inc(step_out, 1)
                s += 1
            dve.wait_ge(step_out, s)
            nc.vector.tensor_tensor(WT[:, :, :], WT[:, :, :], bcast_last(bc[:, :], J), ALU.add).then_inc(consts, 1)
            dve.wait_ge(u_ready, 1)
            dve.wait_ge(dse_out, 1)
            for lo, hi, first, last in ((64, 128, 0, C), (0, 64, 1, CW1)):
                for k in range(3):
                    a, z = max(first, 26 * k), min(last, 26 * k + 26)
                    nc.vector.tensor_copy(U[lo:hi, :, a:z], ps[lo:hi, k, (a - 26 * k) * NH:(z - 26 * k) * NH]
                                          .rearrange("p (c n) -> p n c", n=NH)).then_inc(u_out, 1)


def position_terms(nc, t, bd, x1T, ps):
    GM, WT, U = t["GM"], t["WT"], t["U"]
    with ExitStack() as ctx:
        def sb(name, shape, dt=F32):
            return ctx.enter_context(nc.sbuf_tensor("pt_" + name, shape, dt))

        def sem(name):
            return ctx.enter_context(nc.semaphore("pt_" + name))

        xq = [sb(f"xq{p}", [128, 2, B]) for p in range(2)]
        ev = [sb(f"ev{j}", [128, NH, CW1]) for j in range(4)]
        xq_ready, g_ready, w_added, u_added, u_added_v = (sem(n) for n in ("xq_ready", "g_ready", "w_added", "u_added", "u_added_v"))
        stored = [sem(f"stored{j}") for j in range(4)]
        POOL_HEADS = BANKS[1][1]
        block = ctx.enter_context(nc.Block())

        def loop(eng, step):
            for j in range(4):
                step(j, j)
            with eng.Fori(1, S // 8) as four:
                for j in range(4):
                    step(4 * four + j, j)

        @block.scalar
        def _(act):
            def step(k, j):
                at_least(act, g_ready, 3 * (k - 1))
                nc.scalar.copy(xq[j % 2][:, :, :], x1T[:, :, bass.ds(2 * k, 2)].rearrange("p b s -> p s b")).then_inc(xq_ready, 1)
            loop(act, step)

        @block.tensor
        def _(pe):
            def step(k, j):
                pe.wait_ge(xq_ready, k + 1)
                at_least(pe, w_added, 3 * (k - 1))
                for g, (a, z) in enumerate(BANKS):
                    nc.tensor.matmul(ps[:, 3 * (j % 2) + g, 0:(z - a) * CW1], xq[j % 2][:, :, :].rearrange("p s b -> p (s b)"),
                                     GM[:, a:z, bass.ds(S - 2 - 2 * k, CW1)], start=True, stop=True).then_inc(g_ready, 1)
            loop(pe, step)

        @block.vector
        def _(dve):
            def step(k, j):
                at_least(dve, stored[j], 8 * (k - j))
                for g, (a, z) in enumerate(BANKS):
                    dve.wait_ge(g_ready, 3 * k + g + 1)
                    nc.vector.tensor_tensor(ev[j][:, a:z, :], ps[:, 3 * (j % 2) + g, 0:(z - a) * CW1].rearrange("p (n c) -> p n c", c=CW1),
                                            WT[:, a:z, bass.ds(S - 2 - 2 * k, CW1)], ALU.add).then_inc(w_added, 1)
                dve.wait_ge(w_added, 3 * k + 3)
                nc.vector.tensor_tensor(ev[j][:, POOL_HEADS:, :], ev[j][:, POOL_HEADS:, :], U[:, POOL_HEADS:, :], ALU.add) \
                    .then_inc(u_added_v, 1)
            loop(dve, step)

        @block.gpsimd
        def _(pool):
            def step(k, j):
                pool.wait_ge(w_added, 3 * k + 2)
                nc.gpsimd.tensor_tensor(ev[j][:, 0:POOL_HEADS, :], ev[j][:, 0:POOL_HEADS, :], U[:, 0:POOL_HEADS, :], ALU.add) \
                    .then_inc(u_added, 1)
            loop(pool, step)

        @block.sync
        def _(sp):
            def step(k, j):
                dma_after(sp, u_added, k + 1)
                dma_after(sp, u_added_v, k + 1)
                for s in range(2):
                    sp.dma_start(bd[:, 2 * k + s, :], ev[j][64 * s:64 * s + 64, :, :].rearrange("b n c -> b (n c)")).then_inc(stored[j], 16)
            loop(sp, step)
            for j in range(4):
                sp.wait_ge(stored[j], 32 * (S // 8))


def layer1(nc, d, t, bd, out, x1T, ident, ps, halfneg):
    MT, DW, DC, ctxT = t["MT"], t["DW"], t["DC"], t["ctxT"]
    with ExitStack() as ctx:
        def sb(name, shape, dt=F32):
            return ctx.enter_context(nc.sbuf_tensor("l1_" + name, shape, dt))

        def sem(name):
            return ctx.enter_context(nc.semaphore("l1_" + name))

        wv, wo, w1, w2, b1, rows, seg8, nm, w_in = (t[n] for n in ("wv1", "wo1", "w1", "w2", "b1", "rows", "seg", "cmask", "later_in"))
        seg = sb("seg", [128, C])
        XT = [sb(f"XT{p}", [128, S]) for p in range(2)]
        CT = [sb(f"CT{p}", [128, C]) for p in range(2)]
        BD = [sb(f"BD{p}", [128, NH, CW1]) for p in range(2)]
        DS = sb("DS", [128, NH])
        T = sb("T", [128, NH, C])
        Z = sb("Z", [128, NH, 2, C])
        X1 = [sb(f"X1{p}", [128, H]) for p in range(2)]
        VA = [sb(f"VA{p}", [C, NH, D]) for p in range(2)]
        P = sb("P", [128, NH, C])
        MX = sb("MX", [128, NH])
        PT = sb("PT", [C, NH, S])
        RS = sb("RS", [128, NH])
        AT = sb("AT", [128, CC, S])
        Y = sb("Y", [128, 2, H])
        st = sb("st", [128, 2, 6])
        mv = sb("mv", [128, 2, 2])
        ve = sb("ve", [128, 2])
        rs = sb("rs", [128, 2])
        NRM = sb("NRM", [128, 2, H])
        Z1 = sb("Z1", [128, H])
        ZB = [sb(f"ZB{p}", [128, H]) for p in range(2)]
        ZT = sb("ZT", [128, S])
        HT = sb("HT", [128, FC, S])
        OUT = [sb(f"OUT{p}", [128, H]) for p in range(2)]

        bd_in = [sem(f"bd_in{p}") for p in range(2)]
        stored = [sem(f"stored{p}") for p in range(2)]
        names = ("seg_ready xt_ready dd_ready ds_ready t_seg bd_masked t_ready z_ready z_out v_ready v_out s_ready s_added s_max "
                 "s_centred p_ready pt_ready pt_out sum_ready sum_inv p_normed pv_ready at_out wo_ready "
                 "y_ready stat1 var1 rstd1 nrm1 z1_ready zb_ready zt_ready zt_out h_ready ht_out down_ready "
                 "w_ready stat2 var2 rstd2 nrm2 out_ready").split()
        e = {n: sem(n) for n in names}
        block = ctx.enter_context(nc.Block())


        @block.sync
        def _(sp):
            def load(b, p):
                dma_after(sp, e["t_ready"], b - 1)
                v = bd[b, :, :].rearrange("(k s) e -> s k e", s=2)
                for s in range(2):
                    w = NH * CW1 - 1
                    sp.dma_start(BD[p][s:128:2, :, :].rearrange("q n c -> q (n c)")[:, 0:w], v[s, :, 1 - s:1 - s + w]).then_inc(bd_in[p], 16)

            load(0, 0)
            load(1, 1)
            def store(b, p):
                dma_after(sp, e["out_ready"], b + 1)
                sp.dma_start(out[b, :, :], OUT[p][:, :]).then_inc(stored[p], 16)

            def step(b, p):
                load(b, p)
                store(b - 5, 1 - p)
            for b in range(2, 5):
                load(b, b % 2)
            step(5, 1)
            by_pairs(sp, 6, B, step)
            for b in range(B - 5, B):
                store(b, b % 2)
            for p in range(2):
                sp.wait_ge(stored[p], 16 * (B // 2))

        @block.tensor
        def _(pe):
            def rows_and_segments(f, p):
                at_least(pe, e["zt_out"], f - 1)
                at_least(pe, e["ds_ready"], f + 1)
                if active(f):
                    mm = nc.tensor.transpose(ps[:, 3, 128:256], XT[p][:, :], ident[:, :])
                if active(f + 1):
                    pe.wait_ge(e["xt_ready"], f + 2)
                    mm = nc.tensor.matmul(ps[:, 3, 0:NH], XT[1 - p][:, :], DW[:, :], start=True, stop=True)
                mm.then_inc(e["dd_ready"], 1)

            def fold_context(f, part):
                if part == 0:
                    at_least(pe, e["s_added"], 3 * f)
                for k in range(3):
                    if part == 1:
                        pe.wait_ge(e["z_out"], 3 * f + k + 1)
                    a, z = Z_HEADS[3 * part + k]
                    for n in range(a, z):
                        w = 2 * C
                        mm = nc.tensor.matmul(ps[:, k, (n - a) * w:(n - a + 1) * w], MT[:, n, :],
                                              ctxT[:, bass.ds(f, 2), :].rearrange("p b c -> p (b c)"), start=True, stop=True)
                    mm.then_inc(e["z_ready"], 1)

            def scores(f, p):
                if p == 0:
                    pe.wait_ge(e["z_out"], 3 * f + 6)
                else:
                    pe.wait_ge(e["s_added"], 3 * f)
                for k, (a, z) in enumerate(BANKS):
                    nc.tensor.matmul(ps[:, k, 0:(z - a) * C], XT[p][:, :], Z[:, a:z, p, :],
                                     start=True, stop=True).then_inc(e["s_ready"], 1)

            def values(f, p):
                at_least(pe, e["at_out"], 2 * f)
                for k in range(2):
                    nc.tensor.matmul(ps[0:C, 4 + k, :], CT[p][:, :], wv[:, k * 512:(k + 1) * 512], start=True, stop=True) \
                        .then_inc(e["v_ready"], 1)

            def transpose_probs(m):
                pe.wait_ge(e["ds_ready"], m + 2)
                for g, bank in enumerate((3, 4, 5, 3)):
                    pe.wait_ge(e["p_normed"], 3 * m + min(g + 1, 3))
                    if g == 1:
                        pe.wait_ge(e["v_out"], 2 * (m + 1))
                    if g == 3:
                        pe.wait_ge(e["pt_out"], 4 * m + 1)
                    for n in range(4 * g, 4 * g + 4):
                        mm = nc.tensor.transpose(ps[0:C, bank, (n % 4) * S:(n % 4 + 1) * S], P[:, n, :], ident[:, :])
                    mm.then_inc(e["pt_ready"], 1)

            def weigh_values(m, p, k):
                pe.wait_ge(e["pt_out"], 4 * m + 2 + 2 * k)
                for c in range(4 * k, 4 * k + 4):
                    for u in range(2):
                        mm = nc.tensor.matmul(ps[64 * u:64 * u + 64, 4 + k, (c % 4) * S:(c % 4 + 1) * S], VA[p][:, 2 * c + u, :],
                                              PT[:, 2 * c + u, :], start=True, stop=True)
                mm.then_inc(e["pv_ready"], 1)

            def project_out(m):
                pe.wait_ge(e["at_out"], 2 * (m + 1))
                at_least(pe, e["w_ready"], m - 1)
                for c in range(CC):
                    mm = nc.tensor.matmul(ps[:, 7, 0:H], AT[:, c, :], wo[:, c, :], start=(c == 0), stop=(c == CC - 1))
                mm.then_inc(e["wo_ready"], 1)

            def transpose_normed(b):
                pe.wait_ge(e["z1_ready"], b + 1)
                nc.tensor.transpose(ps[:, 3, 0:S], Z1[:, :], ident[:, :]).then_inc(e["zt_ready"], 1)

            def up(b):
                pe.wait_ge(e["zt_out"], b + 1)
                at_least(pe, e["ht_out"], b)
                for k in range(FC):
                    mm = nc.tensor.matmul(ps[:, 6, k * S:(k + 1) * S], w1[:, k * 128:(k + 1) * 128], ZT[:, :], start=True, stop=True)
                mm.then_inc(e["h_ready"], 1)

            def down(b):
                pe.wait_ge(e["ht_out"], b + 1)
                pe.wait_ge(e["y_ready"], upto_last(b + 2))
                at_least(pe, e["w_ready"], b)
                for k in range(FC):
                    mm = nc.tensor.matmul(ps[:, 7, 0:H], HT[:, k, :], w2[:, k, :], start=(k == 0), stop=(k == FC - 1))
                mm.then_inc(e["down_ready"], 1)

            def step(t, p):
                if active(t):
                    transpose_probs(t)
                if p == 1 and active(t + 1):
                    fold_context(t + 1, 1)
                if active(t):
                    weigh_values(t, p, 0)
                    weigh_values(t, p, 1)
                if active(t - 1):
                    transpose_normed(t - 1)
                if active(t - 2):
                    down(t - 2)
                if active(t + 1):
                    scores(t + 1, 1 - p)
                if active(t + 1) or active(t + 2):
                    rows_and_segments(t + 1, 1 - p)
                if active(t - 1):
                    up(t - 1)
                if active(t + 1):
                    values(t + 1, 1 - p)
                if active(t):
                    project_out(t)
                if p == 0 and active(t + 2):
                    fold_context(t + 2, 0)

            pe.wait_ge(w_in, 16 * LATER)
            for t in range(-3, 0):
                step(t, t % 2)
            steady_and_last(pe, step)

        @block.scalar
        def _(act):
            def fetch(f, p):
                if not isinstance(f, int) or f >= 2:
                    act.wait_ge(e["dd_ready"], f)
                    act.wait_ge(e["v_ready"], 2 * (f - 1))
                nc.scalar.copy(XT[p][:, :], x1T[:, f, :])
                nc.scalar.copy(CT[p][:, :], ctxT[:, f, :]).then_inc(e["xt_ready"], 1)

            def fold_evict(f, part):
                if part == 0:
                    at_least(act, e["s_ready"], 3 * f)
                for k in range(3 * part, 3 * part + 3):
                    a, z = Z_HEADS[k]
                    act.wait_ge(e["z_ready"], 3 * f + k + 1)
                    nc.scalar.copy(Z[:, a:z, :, :].rearrange("p n b c -> p (n b c)"), ps[:, k % 3, 0:(z - a) * 2 * C]) \
                        .then_inc(e["z_out"], 1)

            def probs_evict(m):
                at_least(act, e["pv_ready"], 2 * m)
                for g, bank in enumerate((3, 4, 5, 3)):
                    act.wait_ge(e["pt_ready"], 4 * m + g + 1)
                    nc.scalar.copy(PT[:, 4 * g:4 * g + 4, :], ps[0:C, bank, :].rearrange("c (n q) -> c n q", n=4)).then_inc(e["pt_out"], 1)

            def attn_evict(m):
                at_least(act, e["wo_ready"], m)
                for k in range(2):
                    act.wait_ge(e["pv_ready"], 2 * m + k + 1)
                    nc.scalar.copy(AT[:, 4 * k:4 * k + 4, :], ps[:, 4 + k, :].rearrange("c (n q) -> c n q", n=4)).then_inc(e["at_out"], 1)

            def normed_evict(b):
                act.wait_ge(e["zt_ready"], b + 1)
                at_least(act, e["h_ready"], b)
                nc.scalar.copy(ZT[:, :], ps[:, 3, 0:S]).then_inc(e["zt_out"], 1)

            def exps(f):
                for k, (a, z) in enumerate(BANKS):
                    act.wait_ge(e["s_centred"], 3 * f + k + 1)
                    nc.scalar.activation(P[:, a:z, :], P[:, a:z, :], ACT.Exp).then_inc(e["p_ready"], 1)

            def relu(b):
                act.wait_ge(e["h_ready"], b + 1)
                at_least(act, e["down_ready"], b)
                for k in range(FC):
                    last = nc.scalar.activation(HT[:, k, :], ps[:, 6, k * S:(k + 1) * S], ACT.Relu, bias=b1[:, k:k + 1])
                last.then_inc(e["ht_out"], 1)

            def values_evict(f, p):
                at_least(act, e["pv_ready"], 2 * (f - 1))
                for k in range(2):
                    act.wait_ge(e["v_ready"], 2 * f + k + 1)
                    nc.scalar.copy(VA[p][:, 8 * k:8 * k + 8, :], ps[0:C, 4 + k, :].rearrange("c (n d) -> c n d", d=D)).then_inc(e["v_out"], 1)

            def step(t, p):
                if active(t):
                    probs_evict(t)
                if p == 1 and active(t + 1):
                    fold_evict(t + 1, 1)
                if active(t):
                    attn_evict(t)
                if active(t - 1):
                    normed_evict(t - 1)
                if active(t + 1):
                    exps(t + 1)
                if active(t - 1):
                    relu(t - 1)
                if active(t + 1):
                    values_evict(t + 1, 1 - p)
                if active(t + 3):
                    fetch(t + 3, 1 - p)
                if p == 0 and active(t + 2):
                    fold_evict(t + 2, 0)

            act.wait_ge(w_in, 16 * LATER)
            for t in range(-3, 0):
                step(t, t % 2)
            steady_and_last(act, step)

        @block.vector
        def _(dve):
            def add_positions(f, p):
                dve.wait_ge(e["t_seg"], f + 1)
                dve.wait_ge(e["bd_masked"], f + 1)
                nc.vector.tensor_tensor(T[:, :, :], T[:, :, :], BD[p][:, :, 0:C], ALU.add).then_inc(e["t_ready"], 1)

            def add_max(f):
                at_least(dve, e["pt_ready"], 4 * f)
                at_least(dve, e["s_centred"], 3 * f)
                dve.wait_ge(e["t_ready"], f + 1)
                for k, (a, z) in enumerate(BANKS):
                    dve.wait_ge(e["s_ready"], 3 * f + k + 1)
                    nc.vector.tensor_tensor(P[:, a:z, :], ps[:, k, 0:(z - a) * C].rearrange("p (n c) -> p n c", c=C),
                                            T[:, a:z, :], ALU.add).then_inc(e["s_added"], 1)
                    dve.wait_ge(e["s_added"], 3 * f + k + 1)
                    nc.vector.tensor_reduce(MX[:, a:z], P[:, a:z, :], AX.X, ALU.max).then_inc(e["s_max"], 1)

            def rows_and_segments(f, p):
                dve.wait_ge(e["dd_ready"], f + 2)
                if active(f + 1):
                    at_least(dve, e["t_seg"], f + 1)
                    last = nc.vector.tensor_tensor(DS[:, :], ps[:, 3, 0:NH], DC[:, :], ALU.add)
                if active(f):
                    at_least(dve, e["y_ready"], f - 1)
                    last = nc.vector.tensor_copy(X1[p][:, :], ps[:, 3, 128:256])
                last.then_inc(e["ds_ready"], 1)

            def normalise(f):
                for k, (a, z) in enumerate(BANKS):
                    dve.wait_ge(e["p_ready"], 3 * f + k + 1)
                    at_least(dve, e["p_normed"], 3 * f)
                    nc.vector.tensor_reduce(RS[:, a:z], P[:, a:z, :], AX.X, ALU.add).then_inc(e["sum_ready"], 1)
                    dve.wait_ge(e["sum_ready"], 3 * f + k + 1)
                    nc.vector.reciprocal(RS[:, a:z], RS[:, a:z]).then_inc(e["sum_inv"], 1)
                    dve.wait_ge(e["sum_inv"], 3 * f + k + 1)
                    nc.vector.tensor_tensor(P[:, a:z, :], P[:, a:z, :], bcast_last(RS[:, a:z], C), ALU.mult) \
                        .then_inc(e["p_normed"], 1)

            def mlp_residual(b, p):
                dve.wait_ge(e["down_ready"], b + 1)
                dve.wait_ge(e["zb_ready"], b + 1)
                nc.vector.tensor_tensor(Y[:, 1, :], ps[:, 7, 0:H], ZB[p][:, :], ALU.add).then_inc(e["w_ready"], 1)

            def attn_residual(m, p):
                dve.wait_ge(e["wo_ready"], m + 1)
                nc.vector.tensor_tensor(Y[:, 0, :], ps[:, 7, 0:H], X1[p][:, :], ALU.add).then_inc(e["y_ready"], 1)

            def norms(m, p):
                which = [(k, b) for k, b in ((0, m), (1, m - 2)) if active(b)]
                stat, var, rstd, nrm = ([e[f"{n}{k + 1}"] for k in range(2)] for n in ("stat", "var", "rstd", "nrm"))
                for k, b in which:
                    dve.wait_ge((e["y_ready"], e["w_ready"])[k], b + 1)
                    at_least(dve, stat[k], 2 * b)
                    nc.vector.bn_stats(st[:, k, :], Y[:, k, :]).then_inc(stat[k], 1)
                for k, b in which:
                    dve.wait_ge(stat[k], 2 * b + 1)
                    dve.nop(nofuse=True)
                    nc.vector.bn_aggr(mv[:, k, :], st[:, k, :]).then_inc(stat[k], 1)
                for k, b in which:
                    dve.wait_ge(stat[k], 2 * b + 2)
                    nc.vector.tensor_scalar(ve[:, k:k + 1], mv[:, k, 1:2], EPS1, None, ALU.add).then_inc(var[k], 1)
                for k, b in which:
                    nc.vector.scalar_tensor_tensor(NRM[:, k, :], Y[:, k, :], mv[:, k, 0:1], rows[:, 3 * k, :],
                                                   ALU.subtract, ALU.mult).then_inc(nrm[k], 1)
                for k, b in which:
                    if k == 0:
                        at_least(dve, e["zt_ready"], b)
                        at_least(dve, e["zb_ready"], b)
                        to, done = Z1, e["z1_ready"]
                    else:
                        at_least(dve, stored[p], 8 * (b - p))
                        to, done = OUT[p], e["out_ready"]
                    dve.wait_ge(nrm[k], b + 1)
                    dve.wait_ge(rstd[k], b + 1)
                    nc.vector.scalar_tensor_tensor(to[:, :], NRM[:, k, :], rs[:, k:k + 1], rows[:, 3 * k + 1, :],
                                                   ALU.mult, ALU.add).then_inc(done, 1)

            def step(t, p):
                if active(t + 1):
                    add_max(t + 1)
                if active(t - 2):
                    mlp_residual(t - 2, p)
                if active(t + 1) or active(t + 2):
                    rows_and_segments(t + 1, 1 - p)
                if active(t + 1):
                    normalise(t + 1)
                if active(t):
                    attn_residual(t, p)
                norms(t, p)
                if active(t + 2):
                    add_positions(t + 2, p)

            dve.wait_ge(w_in, 16 * LATER)
            nc.vector.tensor_copy(seg[:, :], seg8[:, :])
            nc.vector.tensor_scalar(nm[:, :], nm[:, :], -1e30, None, ALU.mult).then_inc(e["seg_ready"], 1)
            for t in range(-3, 0):
                step(t, t % 2)
            steady_and_last(dve, step)

        @block.gpsimd
        def _(pool):
            def centre(f):
                for k, (a, z) in enumerate(BANKS):
                    pool.wait_ge(e["s_max"], 3 * f + k + 1)
                    nc.gpsimd.tensor_tensor(P[:, a:z, :], P[:, a:z, :], bcast_last(MX[:, a:z], C), ALU.subtract) \
                        .then_inc(e["s_centred"], 1)

            def segments(f):
                pool.wait_ge(e["ds_ready"], f + 1)
                at_least(pool, e["s_added"], 3 * f)
                nc.gpsimd.tensor_tensor(T[:, :, :], bcast_mid(seg[:, :], NH), bcast_last(DS[:, :], C), ALU.mult).then_inc(e["t_seg"], 1)

            def masked_positions(f, p):
                pool.wait_ge(bd_in[p], 16 * (f - p) + 32)
                nc.gpsimd.tensor_tensor(BD[p][:, :, 0:C], BD[p][:, :, 0:C], bcast_mid(nm[:, :], NH), ALU.add).then_inc(e["bd_masked"], 1)

            def rstd(k, b):
                pool.wait_ge(e[f"var{k + 1}"], b + 1)
                nc.gpsimd.tensor_tensor(rs[:, k:k + 1], ve[:, k:k + 1], halfneg[:, 0:1], ALU.pow).then_inc(e[f"rstd{k + 1}"], 1)

            def residual_bias(m, p):
                pool.wait_ge(e["z1_ready"], m + 1)
                at_least(pool, e["w_ready"], m - 1)
                nc.gpsimd.tensor_tensor(ZB[p][:, :], Z1[:, :], rows[:, 2, :], ALU.add).then_inc(e["zb_ready"], 1)

            def step(t, p):
                if active(t + 1):
                    centre(t + 1)
                if active(t + 2):
                    segments(t + 2)
                if active(t):
                    rstd(0, t)
                if active(t - 2):
                    rstd(1, t - 2)
                if active(t):
                    residual_bias(t, p)
                if active(t + 3):
                    masked_positions(t + 3, 1 - p)

            pool.wait_ge(w_in, 16 * LATER)
            pool.wait_ge(e["seg_ready"], 1)
            for t in range(-3, 0):
                step(t, t % 2)
            steady_and_last(pool, step)


def build(nc, d, out):
    with ExitStack() as ctx:
        def sb(name, shape, dt=F32):
            return ctx.enter_context(nc.sbuf_tensor(name, shape, dt))

        ps = ctx.enter_context(nc.psum_tensor("ps", [128, 8, BANK], F32))
        bd = nc.dram_tensor("bd_scratch", [B, S, NH * CW1], F32, kind="Internal").ap()
        ident = sb("ident", [128, 128])
        ones = sb("ones", [128, 128])
        halfneg = sb("halfneg", [128, 2])
        x1T = sb("x1T", [128, B, S])
        c_in = ctx.enter_context(nc.semaphore("c_in"))
        with nc.Block() as block:
            @block.sync
            def _(sp):
                sp.dma_start(ident[:, :], d["ident"]).then_inc(c_in, 16)
                sp.wait_ge(c_in, 16)

            @block.vector
            def _(dve):
                nc.vector.memset(ones[:, :], 1.0)
                nc.vector.memset(halfneg[:, :], -0.5)
        t = {n: sb(n, shape, U8 if n == "seg" else F32) for n, shape in LATER_SHAPES.items()}
        t["later_in"] = ctx.enter_context(nc.semaphore("later_in"))

        def load_later(eng):
            for n, shape in LATER_SHAPES.items():
                eng.dma_start(t[n][tuple(slice(None) for _ in shape)], d[n].partition_broadcast(128) if n == "rows" else d[n]) \
                    .then_inc(t["later_in"], 16)

        layer0(nc, d, x1T, ident, ps, halfneg, load_later)
        t.update(MT=sb("MT", [128, NH, H]), DW=sb("DW", [128, NH]), DC=sb("DC", [128, NH]))
        with nc.sbuf_tensor("GM", [128, NH, J], F32) as GM, nc.sbuf_tensor("WT", [128, NH, J], F32) as WT, \
                nc.sbuf_tensor("U", [128, NH, CW1], F32) as U:
            t.update(GM=GM, WT=WT, U=U)
            prepare1(nc, d, t, ident, ones, ps)
            position_terms(nc, t, bd, x1T, ps)
        layer1(nc, d, t, bd, out, x1T, ident, ps, halfneg)


def layouts(i):
    import numpy as np
    a = {k: np.asarray(v) for k, v in i.items()}
    L0, L1 = "L0_xattn_", "L1_xattn_"
    order = [8 * (s // 8) + 4 * (s % 2) + (s % 8) // 2 for s in range(NH)]
    d = {}
    d["x"] = a["x"]
    d["xT"] = a["x"].transpose(0, 2, 1)
    d["ctx"] = a["ctx_1024"]
    d["ctxT"] = a["ctx_1024"].transpose(2, 0, 1)
    d["mask"] = a["mask_Bx1xSxS2_ff0"].reshape(B, S, C)
    d["cmask"] = a["mask_1x1xSxS2_ff0"].reshape(S, C)
    d["seg"] = a["mask_1xSxS2_bk1"].reshape(S, C)
    d["wq0"] = a[L0 + "Wq"].reshape(H, NH, D)[:, order].reshape(H, NH * D)
    d["wkv0"] = np.concatenate([a[L0 + "Wk"], a[L0 + "Wv"]], axis=1)
    d["wo0"] = a[L0 + "Wo"].reshape(NH, D, H)[order].reshape(CC, 128, H).transpose(1, 0, 2)
    d["wgu"] = np.concatenate([a[L0 + "Wgate"], a[L0 + "Wup"]], axis=1)
    d["wd"] = a[L0 + "Wdown"].reshape(FC, 128, H).transpose(1, 0, 2)
    d["lns"] = np.stack([a[L0 + "ln1_w"], a[L0 + "ln2_w"]], axis=1)
    d["wqT"] = a[L1 + "Wq"].reshape(H, CC, 128).transpose(2, 1, 0)
    d["wkT"] = a[L1 + "Wk"].reshape(H, CC, 128).transpose(2, 1, 0)
    d["wr1"] = a[L1 + "Wr"].reshape(H, NH * D)
    d["pos"] = a[L1 + "position_encoding"][0, 1:J + 1].T
    small = [a[L1 + "content_bias"], a[L1 + "position_bias"], a[L1 + "segment_bias"],
             a[L1 + "segment_encoding"][0], a[L1 + "segment_encoding"][1]]
    d["small"] = np.stack([s.reshape(CC, 128).T for s in small], axis=1)
    d["wv1"] = a[L1 + "Wv"].reshape(H, NH * D)
    d["wo1"] = a[L1 + "Wo"].reshape(H, CC, 128).transpose(2, 1, 0)
    d["w1"] = a[L1 + "W1"]
    d["w2"] = a[L1 + "W2"].reshape(FC, 128, H).transpose(1, 0, 2)
    d["b1"] = a[L1 + "b1"].reshape(FC, 128).T
    d["rows"] = np.stack([a[L1 + n] for n in ("ln1_gamma", "ln1_beta", "b2", "ln2_gamma", "ln2_beta")])
    inv = (1.0 / 10000.0 ** (np.arange(0, D, 2, dtype=np.float32) / np.float32(D))).astype(np.float32)
    ang = np.arange(S, dtype=np.float32)[:, None] * inv[None, :]
    cos, sin = np.cos(ang), np.sin(ang)
    row = np.concatenate([cos, cos, -sin, sin], axis=1).astype(np.float32)
    d["rope"] = np.stack([row, row], axis=1)
    d["ident"] = np.eye(128, dtype=np.float32)
    return {k: np.ascontiguousarray(v) for k, v in d.items()}


def kernel(**inputs):
    import numpy as np
    import concourse.bacc as bacc
    from concourse.bass_utils import run_bass_kernel_spmd

    nc = bacc.Bacc("TRN2", target_bir_lowering=False, num_devices=1)
    arrays, d = {}, {}
    for name, a in layouts(inputs).items():
        arrays[f"in_{name}_dram"] = a
        d[name] = nc.dram_tensor(f"in_{name}_dram", a.shape, mybir.dt.from_np(a.dtype), kind="ExternalInput").ap()
    out = nc.dram_tensor("out_0_dram", (B, S, H), F32, kind="ExternalOutput").ap()
    build(nc, d, out)
    r = run_bass_kernel_spmd(nc, [arrays], core_ids=[0])
    return r.results[0]["out_0_dram"]
```

```python
from contextlib import ExitStack

import concourse.bass as bass
from concourse import mybir

F32 = mybir.dt.float32
F32R = mybir.dt.float32r
U8 = mybir.dt.uint8
ALU = mybir.AluOpType
ACT = mybir.ActivationFunctionType
AX = mybir.AxisListType

B, S, C, H = 64, 128, 77, 128
NH, D = 16, 64
CC = NH // 2
GKV = 4
FF = 512
FC = FF // 128
J = S + C - 1
CW1 = C + 1
BANKS = [(0, 6), (6, 11), (11, 16)]
Z_HEADS = [(0, 3), (3, 6), (6, 9), (9, 12), (12, 15), (15, 16)]
BANK = 512
S_BANKS = (6, 7, 0, 1)
SCALE = 1.0 / 8.0
EPS0, EPS1 = 1e-6, 1e-12
LATER_SHAPES = {"wr1": [128, NH * D], "pos": [128, J], "small": [128, 5, CC], "wqT": [128, CC, H], "wkT": [128, CC, H],
                "ctxT": [128, B, C], "wv1": [128, NH * D], "w1": [128, FF], "b1": [128, FC], "seg": [128, C],
                "cmask": [128, C], "wo1": [128, CC, H], "w2": [128, FC, H], "rows": [128, 5, H]}
LATER = len(LATER_SHAPES)


def at_least(eng, sem, value):
    if isinstance(value, int) and value <= 0:
        return
    eng.wait_ge(sem, value)


def upto_last(count):
    return min(count, B) if isinstance(count, int) else count


def dma_after(sp, sem, value):
    if isinstance(value, int):
        at_least(sp, sem, value)
    else:
        sp.wait_ge(sem, value)
        sp.nop(nofuse=True)


def by_pairs(eng, first, end, step):
    with eng.Fori(first // 2, end // 2) as half:
        for k in range(2):
            step(2 * half + (first % 2 + k), (first + k) % 2)


def active(b):
    return not isinstance(b, int) or 0 <= b < B


def steady_and_last(eng, step):
    for t in range(3):
        step(t, t % 2)
    by_pairs(eng, 3, B - 3, step)
    for t in range(B - 3, B + 2):
        step(t, t % 2)


def product_of_parts(nc, out, stationary, moving):
    (sh, sl), (mh, ml) = stationary, moving
    nc.tensor.matmul(out, sh, ml, start=True, stop=False)
    nc.tensor.matmul(out, sl, mh, start=False, stop=False)
    return nc.tensor.matmul(out, sh, mh, start=False, stop=True)


def steady_and_last_by_fours(eng, step):
    for t in range(5):
        step(t, t % 4)
    with eng.Fori(1, (B - 4) // 4) as four:
        for k in range(1, 5):
            step(4 * four + k, k % 4)
    for t in range(B - 3, B + 2):
        step(t, t % 4)


def bcast_mid(ap, n):
    return ap.unsqueeze(1).to_broadcast([ap.shape[0], n, ap.shape[1]])


def bcast_last(ap, n):
    return ap.unsqueeze(2).to_broadcast([ap.shape[0], ap.shape[1], n])


def layer0(nc, d, x1T, ident, ps, halfneg, load_later):
    with ExitStack() as ctx:
        def sb(name, shape, dt=F32):
            return ctx.enter_context(nc.sbuf_tensor("l0_" + name, shape, dt))

        def sem(name):
            return ctx.enter_context(nc.semaphore("l0_" + name))

        wq = sb("wq", [128, NH * D])
        wkv = sb("wkv", [128, 2 * GKV * D])
        wo = sb("wo", [128, CC, H])
        wgu = sb("wgu", [128, 2 * FF])
        wd = sb("wd", [128, FC, H])
        lns = sb("lns", [128, 2])
        rope_q = sb("rope_q", [128, 2 * D])
        rope_k = sb("rope_k", [C, 2 * D])
        XC = [sb(f"XC{p}", [128, 2, H]) for p in range(2)]
        XT = [sb(f"XT{p}", [128, S]) for p in range(2)]
        CT = [sb(f"CT{p}", [128, C]) for p in range(2)]
        XS = [[sb(f"XS{p}{n}", [128, S], F32R) for n in "hl"] for p in range(2)]
        CS = [[sb(f"CS{p}{n}", [128, C], F32R) for n in "hl"] for p in range(2)]
        wqs = [sb(f"wq{n}", [128, NH * D], F32R) for n in "hl"]
        wkvs = [sb(f"wkv{n}", [128, 2 * GKV * D], F32R) for n in "hl"]
        MK = [sb(f"MK{p}", [128, C]) for p in range(2)]
        XR = [sb(f"XR{p}", [128, H]) for p in range(2)]
        sq = sb("sq", [128, 2, H])
        ss = sb("ss", [128, 2])
        ms = sb("ms", [128, 2])
        rstd = [sb(f"rstd{p}", [128, 2]) for p in range(2)]
        KS = sb("KS", [C, GKV * D])
        KA = sb("KA", [C, GKV * D])
        KB = sb("KB", [C, GKV * D])
        VA = [sb(f"VA{p}", [C, GKV, D]) for p in range(2)]
        QE = sb("QE", [128, NH * D])
        QA = sb("QA", [128, NH, D])
        QB = sb("QB", [128, NH, D])
        QT = sb("QT", [128, CC, S])
        KT = sb("KT", [128, 2, 2, C])
        P = sb("P", [128, NH, C])
        MX = sb("MX", [128, NH])
        PT = sb("PT", [C, NH, S])
        RS = sb("RS", [128, NH])
        AT = sb("AT", [128, CC, S])
        XP = [sb(f"XP{p}", [128, H]) for p in range(2)]
        sq2 = sb("sq2", [128, H])
        ss2 = sb("ss2", [128, 1])
        ms2 = sb("ms2", [128, 1])
        rs2 = sb("rs2", [128, 1])
        HN = sb("HN", [128, H])
        HNT = sb("HNT", [128, S])
        TH = sb("TH", [128, FF])
        SG = sb("SG", [128, FF])
        HT = sb("HT", [128, FC, S])

        w_first, w_rest = sem("w_first"), sem("w_rest")
        x_in = [sem(f"x_in{p}") for p in range(2)]
        mk_in = [sem(f"mk_in{p}") for p in range(2)]
        xr_in = [sem(f"xr_in{p}") for p in range(2)]
        w_scaled, w_high, w_split = sem("w_scaled"), sem("w_high"), sem("w_split")
        x_high, x_split = sem("x_high"), sem("x_split")
        pads = sem("pads")
        squared, summed, mean_ready, rstd_ready = (sem(n) for n in ("squared", "summed", "mean_ready", "rstd_ready"))
        q_ready, q_out, kv_ready, kv_out = (sem(n) for n in ("q_ready", "q_out", "kv_ready", "kv_out"))
        q_sin, q_cos, q_roped, k_parts, k_roped = (sem(n) for n in ("q_sin", "q_cos", "q_roped", "k_parts", "k_roped"))
        qt_ready, kt_ready, qt_out, kt_out = sem("qt_ready"), sem("kt_ready"), sem("qt_out"), sem("kt_out")
        s_ready, s_masked, s_max, s_centred, p_ready = (sem(n) for n in ("s_ready", "s_masked", "s_max", "s_centred", "p_ready"))
        pt_ready, pt_out = sem("pt_ready"), sem("pt_out")
        sum_ready, sum_inv, p_normed = sem("sum_ready"), sem("sum_inv"), sem("p_normed")
        pv_ready, at_out, wo_ready, xp_ready = sem("pv_ready"), sem("at_out"), sem("wo_ready"), sem("xp_ready")
        sq2_ready, mean2_ready, rstd2_ready, hn_ready = (sem(n) for n in ("sq2_ready", "mean2_ready", "rstd2_ready", "hn_ready"))
        hnt_ready, hnt_out, gate_ready, up_ready = (sem(n) for n in ("hnt_ready", "hnt_out", "gate_ready", "up_ready"))
        tanh_ready, silu_ready, ht_ready = sem("tanh_ready"), sem("silu_ready"), sem("ht_ready")
        down_ready, x1t_out = sem("down_ready"), sem("x1t_out")
        block = ctx.enter_context(nc.Block())


        @block.sync
        def _(sp):
            def load(b, p):
                dma_after(sp, squared, b - 1)
                dma_after(sp, x_split, b - 1)
                sp.dma_start(XC[p][:, 0, :], d["x"][b, :, :]).then_inc(x_in[p], 16)
                sp.dma_start(XC[p][0:C, 1, :], d["ctx"][b, :, :]).then_inc(x_in[p], 16)
                sp.dma_start(XT[p][:, :], d["xT"][b, :, :]).then_inc(x_in[p], 16)
                sp.dma_start(CT[p][:, :], d["ctxT"][:, b, :]).then_inc(x_in[p], 16)

            def load_mask(b, p):
                dma_after(sp, s_masked, 2 * (b - 1))
                sp.dma_start(MK[p][:, :], d["mask"][b, :, :]).then_inc(mk_in[p], 16)

            def load_residual(b, p):
                dma_after(sp, xp_ready, b - 1)
                sp.dma_start(XR[p][:, :], d["x"][b, :, :]).then_inc(xr_in[p], 16)

            sp.wait_ge(pads, 1)
            load(0, 0)
            for t, n in ((lns, "lns"), (wq, "wq0"), (wkv, "wkv0")):
                sp.dma_start(t[:, :], d[n]).then_inc(w_first, 16)
            sp.dma_start(rope_q[:, :], d["rope"][:, 0, :]).then_inc(w_first, 16)
            sp.dma_start(rope_k[:, :], d["rope"][0:C, 1, :]).then_inc(w_first, 16)
            load(1, 1)
            load_mask(0, 0)
            load_mask(1, 1)
            sp.dma_start(wo[:, :, :], d["wo0"]).then_inc(w_rest, 16)
            sp.dma_start(wgu[:, :], d["wgu"]).then_inc(w_rest, 16)
            sp.dma_start(wd[:, :, :], d["wd"]).then_inc(w_rest, 16)
            load_residual(0, 0)

            def both(b, p):
                load(b, p)
                load_mask(b, p)
                load_residual(b - 1, 1 - p)
            both(2, 0)
            both(3, 1)
            by_pairs(sp, 4, B, both)
            load_residual(B - 1, 1)

        @block.tensor
        def _(pe):
            def project(f, p):
                pe.wait_ge(x_split, f + 1)
                at_least(pe, s_masked, 2 * f)
                for k in range(2):
                    product_of_parts(nc, ps[:, k, :], [a[:, :] for a in XS[p]], [w[:, k * 512:(k + 1) * 512] for w in wqs]) \
                        .then_inc(q_ready, 1)

            def project_kv(f, p):
                pe.wait_ge(x_split, f + 1)
                product_of_parts(nc, ps[0:C, 2, :], [a[:, :] for a in CS[p]], [w[:, :] for w in wkvs]).then_inc(kv_ready, 1)

            def transpose_probs(m):
                for g, bank in enumerate((6, 7, 0, 1)):
                    if g % 2 == 0:
                        pe.wait_ge(p_normed, 2 * m + g // 2 + 1)
                    if g == 2:
                        pe.wait_ge(q_out, 2 * upto_last(m + 2))
                    for n in range(4 * g, 4 * g + 4):
                        mm = nc.tensor.transpose(ps[0:C, bank, (n % 4) * S:(n % 4 + 1) * S], P[:, n, :], ident[:, :])
                    mm.then_inc(pt_ready, 1)

            def weigh_values(m, p, k):
                pe.wait_ge(pt_out, 4 * m + 2 + 2 * k)
                for u in range(2):
                    g = 2 * k + u
                    mm = nc.tensor.matmul(ps[64 * u:64 * u + 64, 6 + k, :], VA[p][:, g, :],
                                          PT[:, 8 * k + u:8 * k + 8:2, :], start=True, stop=True)
                mm.then_inc(pv_ready, 1)

            def transpose_k(f):
                pe.wait_ge(kv_out, f + 1)
                pe.wait_ge(k_roped, f + 1)
                for a in range(2):
                    mm = nc.tensor.transpose(ps[:, 2, a * C:(a + 1) * C], KA[:, a * 128:(a + 1) * 128], ident[0:C, 0:C])
                mm.then_inc(kt_ready, 1)

            def transpose_q(f, k):
                pe.wait_ge(q_roped, f + 1)
                for c in range(4 * k, 4 * k + 4):
                    mm = nc.tensor.transpose(ps[:, k, (c % 4) * S:(c % 4 + 1) * S],
                                             QA[:, 2 * c:2 * c + 2, :].rearrange("q u d -> q (u d)"), ident[:, :])
                mm.then_inc(qt_ready, 1)

            def scores(f, k):
                if k == 0:
                    pe.wait_ge(kt_out, f + 1)
                    at_least(pe, at_out, 2 * f)
                pe.wait_ge(qt_out, 2 * f + k + 1)
                for c in range(4 * k, 4 * k + 4):
                    mm = nc.tensor.matmul(ps[:, S_BANKS[c // 2], (c % 2) * 2 * C:(c % 2 + 1) * 2 * C], QT[:, c, :],
                                          KT[:, k, :, :].rearrange("p u c -> p (u c)"), start=True, stop=True)
                mm.then_inc(s_ready, 1)

            def project_out(m):
                pe.wait_ge(at_out, 2 * (m + 1))
                at_least(pe, hnt_out, m)
                for c in range(CC):
                    mm = nc.tensor.matmul(ps[:, 5, 0:H], AT[:, c, :], wo[:, c, :], start=(c == 0), stop=(c == CC - 1))
                mm.then_inc(wo_ready, 1)

            def transpose_normed(e):
                pe.wait_ge(hn_ready, e + 1)
                nc.tensor.transpose(ps[:, 5, 0:S], HN[:, :], ident[:, :]).then_inc(hnt_ready, 1)

            def gate(e):
                pe.wait_ge(hnt_out, e + 1)
                at_least(pe, x1t_out, e)
                for k in range(FC):
                    mm = nc.tensor.matmul(ps[:, 3, k * S:(k + 1) * S], wgu[:, k * 128:(k + 1) * 128], HNT[:, :],
                                          start=True, stop=True)
                mm.then_inc(gate_ready, 1)

            def up(e):
                for k in range(FC):
                    mm = nc.tensor.matmul(ps[:, 4, k * S:(k + 1) * S], wgu[:, FF + k * 128:FF + (k + 1) * 128], HNT[:, :],
                                          start=True, stop=True)
                mm.then_inc(up_ready, 1)

            def down(e, p):
                pe.wait_ge(ht_ready, e + 1)
                for k in range(FC):
                    nc.tensor.matmul(ps[:, 3, 0:S], wd[:, k, :], HT[:, k, :], start=(k == 0), stop=False)
                nc.tensor.matmul(ps[:, 3, 0:S], XP[p][:, :], ident[:, :], start=False, stop=True).then_inc(down_ready, 1)

            def step(t, p):
                if active(t):
                    transpose_probs(t)
                    weigh_values(t, p, 0)
                    weigh_values(t, p, 1)
                if active(t + 1):
                    transpose_k(t + 1)
                if active(t - 2):
                    down(t - 2, p)
                if active(t + 1):
                    transpose_q(t + 1, 0)
                    transpose_q(t + 1, 1)
                if active(t + 1):
                    scores(t + 1, 0)
                if active(t - 1):
                    transpose_normed(t - 1)
                if active(t + 1):
                    scores(t + 1, 1)
                if active(t - 1):
                    gate(t - 1)
                    up(t - 1)
                if active(t + 2):
                    project_kv(t + 2, p)
                    project(t + 2, p)
                if active(t):
                    project_out(t)

            pe.wait_ge(w_first, 16 * 5)
            pe.wait_ge(w_split, 1)
            for t in range(-3, 0):
                step(t, t % 2)
            pe.wait_ge(w_rest, 16 * 3)
            pe.wait_ge(w_scaled, 2)
            steady_and_last(pe, step)

        @block.scalar
        def _(act):
            def split_high(f, p):
                act.wait_ge(x_in[p], 32 * (f - p) + 64)
                at_least(act, q_ready, 2 * (f - 1))
                at_least(act, kv_ready, f - 1)
                nc.scalar.copy(XS[p][0][:, :], XT[p][:, :])
                nc.scalar.copy(CS[p][0][:, :], CT[p][:, :]).then_inc(x_high, 1)

            def probs_evict(m):
                at_least(act, pv_ready, 2 * m)
                for g, bank in enumerate((6, 7, 0, 1)):
                    act.wait_ge(pt_ready, 4 * m + g + 1)
                    nc.scalar.copy(PT[:, 4 * g:4 * g + 4, :], ps[0:C, bank, :].rearrange("c (n q) -> c n q", n=4)).then_inc(pt_out, 1)

            def attn_evict(m):
                at_least(act, wo_ready, m)
                for k in range(2):
                    act.wait_ge(pv_ready, 2 * m + k + 1)
                    nc.scalar.copy(AT[:, 4 * k:4 * k + 4, :], ps[:, 6 + k, :].rearrange("c (n q) -> c n q", n=4)).then_inc(at_out, 1)

            def k_evict(f):
                at_least(act, s_ready, 2 * f)
                act.wait_ge(kt_ready, f + 1)
                for u in range(2):
                    h = slice(64 * u, 64 * u + 64)
                    last = nc.scalar.copy(KT[h, :, u, :], ps[h, 2, 0:2 * C].rearrange("p (a c) -> p a c", a=2))
                last.then_inc(kt_out, 1)

            def qt_evict(f, k):
                act.wait_ge(qt_ready, 2 * f + k + 1)
                nc.scalar.copy(QT[:, 4 * k:4 * k + 4, :], ps[:, k, :].rearrange("c (n q) -> c n q", n=4)).then_inc(qt_out, 1)

            def x1_evict(e):
                act.wait_ge(down_ready, e + 1)
                nc.scalar.copy(x1T[:, e, :], ps[:, 3, 0:S]).then_inc(x1t_out, 1)

            def normed(e, p):
                act.wait_ge(rstd2_ready, e + 1)
                at_least(act, hnt_ready, e)
                nc.scalar.activation(HN[:, :], XP[p][:, :], ACT.Copy, scale=rs2[:, 0:1]).then_inc(hn_ready, 1)

            def normed_evict(e):
                act.wait_ge(hnt_ready, e + 1)
                at_least(act, up_ready, e)
                nc.scalar.copy(HNT[:, :], ps[:, 5, 0:S]).then_inc(hnt_out, 1)

            def tanh(e):
                act.wait_ge(gate_ready, e + 1)
                at_least(act, silu_ready, e)
                nc.scalar.activation(TH[:, :], ps[:, 3, :], ACT.Tanh, scale=0.5).then_inc(tanh_ready, 1)

            def exps(f, k):
                act.wait_ge(s_centred, 2 * f + k + 1)
                nc.scalar.activation(P[:, 8 * k:8 * k + 8, :], P[:, 8 * k:8 * k + 8, :], ACT.Exp).then_inc(p_ready, 1)

            def q_evict(f, p, k):
                if k == 0:
                    at_least(act, q_sin, f)
                    at_least(act, q_cos, f)
                act.wait_ge(q_ready, 2 * f + k + 1)
                nc.scalar.activation(QE[:, 512 * k:512 * k + 512], ps[:, k, :], ACT.Copy, scale=rstd[p][:, 0:1]).then_inc(q_out, 1)

            def kv_evict(f, p):
                act.wait_ge(rstd_ready, f + 1)
                act.wait_ge(kv_ready, f + 1)
                at_least(act, k_parts, f)
                at_least(act, pv_ready, 2 * (f - 1))
                nc.scalar.activation(KS[:, :], ps[0:C, 2, 0:GKV * D], ACT.Copy, scale=rstd[p][0:C, 1:2])
                nc.scalar.activation(VA[p][:, :, :], ps[0:C, 2, GKV * D:].rearrange("c (g d) -> c g d", g=GKV),
                                     ACT.Copy, scale=rstd[p][0:C, 1:2]).then_inc(kv_out, 1)

            def step(t, p):
                if active(t):
                    probs_evict(t)
                    attn_evict(t)
                if active(t + 1):
                    k_evict(t + 1)
                if active(t - 2):
                    x1_evict(t - 2)
                if active(t + 1):
                    qt_evict(t + 1, 0)
                    qt_evict(t + 1, 1)
                if active(t - 1):
                    normed(t - 1, 1 - p)
                    normed_evict(t - 1)
                    tanh(t - 1)
                if active(t + 1):
                    exps(t + 1, 0)
                if active(t + 2):
                    kv_evict(t + 2, p)
                if active(t + 1):
                    exps(t + 1, 1)
                if active(t + 2):
                    q_evict(t + 2, p, 0)
                    q_evict(t + 2, p, 1)
                if active(t + 3):
                    split_high(t + 3, 1 - p)

            act.wait_ge(pads, 2)
            step(-3, 1)
            act.wait_ge(w_scaled, 1)
            nc.scalar.copy(wqs[0][:, :], wq[:, :])
            nc.scalar.copy(wkvs[0][:, :], wkv[:, :]).then_inc(w_high, 1)
            for t in range(-2, 0):
                step(t, t % 2)
            load_later(nc.scalar)
            steady_and_last(act, step)

        @block.vector
        def _(dve):
            def mask_max(f, p):
                at_least(dve, pt_ready, 4 * f)
                at_least(dve, s_centred, 2 * f)
                dve.wait_ge(mk_in[p], 8 * (f - p) + 16)
                for k in range(2):
                    dve.wait_ge(s_ready, 2 * f + k + 1)
                    b0 = S_BANKS[2 * k]
                    sc = ps[:, b0:b0 + 2, 0:4 * C].rearrange("p k (n c) -> p k n c", c=C)
                    mk = MK[p][:, :].unsqueeze(1).unsqueeze(1).to_broadcast([128, 2, 4, C])
                    nc.vector.tensor_tensor(P[:, 8 * k:8 * k + 8, :].rearrange("p (k n) c -> p k n c", k=2), sc, mk,
                                            ALU.add).then_inc(s_masked, 1)
                    dve.wait_ge(s_masked, 2 * f + k + 1)
                    nc.vector.tensor_reduce(MX[:, 8 * k:8 * k + 8], P[:, 8 * k:8 * k + 8, :], AX.X, ALU.max).then_inc(s_max, 1)

            def normalise(f):
                for k in range(2):
                    a, z = 8 * k, 8 * k + 8
                    dve.wait_ge(p_ready, 2 * f + k + 1)
                    at_least(dve, p_normed, 2 * f)
                    nc.vector.tensor_reduce(RS[:, a:z], P[:, a:z, :], AX.X, ALU.add).then_inc(sum_ready, 1)
                    dve.wait_ge(sum_ready, 2 * f + k + 1)
                    nc.vector.reciprocal(RS[:, a:z], RS[:, a:z]).then_inc(sum_inv, 1)
                    dve.wait_ge(sum_inv, 2 * f + k + 1)
                    nc.vector.tensor_tensor(P[:, a:z, :], P[:, a:z, :], bcast_last(RS[:, a:z], C), ALU.mult).then_inc(p_normed, 1)

            def rope(f):
                dve.wait_ge(q_out, 2 * (f + 1))
                at_least(dve, q_roped, f)
                q = QE[:, :].rearrange("p (n d) -> p n d", d=D)
                nc.vector.tensor_tensor(QB[:, :, 0:D // 2], q[:, :, D // 2:], bcast_mid(rope_q[:, D:D + D // 2], NH), ALU.mult)
                nc.vector.tensor_tensor(QB[:, :, D // 2:], q[:, :, 0:D // 2], bcast_mid(rope_q[:, D + D // 2:], NH),
                                        ALU.mult).then_inc(q_sin, 1)
                dve.wait_ge(q_sin, f + 1)
                dve.wait_ge(q_cos, f + 1)
                nc.vector.tensor_tensor(QA[:, :, :], QA[:, :, :], QB[:, :, :], ALU.add).then_inc(q_roped, 1)

            def silu(e):
                dve.wait_ge(tanh_ready, e + 1)
                at_least(dve, ht_ready, e)
                nc.vector.scalar_tensor_tensor(SG[:, :], TH[:, :], 1.0, ps[:, 3, :], ALU.add, ALU.mult).then_inc(silu_ready, 1)
                dve.wait_ge(silu_ready, e + 1)
                dve.wait_ge(up_ready, e + 1)
                at_least(dve, down_ready, e)
                nc.vector.tensor_tensor(HT[:, :, :].rearrange("p k q -> p (k q)"), SG[:, :], ps[:, 4, :], ALU.mult).then_inc(ht_ready, 1)

            def residual(m, p):
                dve.wait_ge(wo_ready, m + 1)
                dve.wait_ge(xr_in[p], 8 * (m - p) + 16)
                at_least(dve, down_ready, m - 1)
                nc.vector.tensor_tensor(XP[p][:, :], ps[:, 5, 0:H], XR[p][:, :], ALU.add).then_inc(xp_ready, 1)
                dve.wait_ge(xp_ready, m + 1)
                nc.vector.tensor_tensor(sq2[:, :], XP[p][:, :], XP[p][:, :], ALU.mult).then_inc(sq2_ready, 1)
                dve.wait_ge(sq2_ready, 2 * m + 1)
                nc.vector.tensor_reduce(ss2[:, :], sq2[:, :], AX.X, ALU.add).then_inc(sq2_ready, 1)
                dve.wait_ge(sq2_ready, 2 * m + 2)
                nc.vector.tensor_scalar(ms2[:, :], ss2[:, :], 1.0 / H, EPS0, ALU.mult, ALU.add).then_inc(mean2_ready, 1)

            def mean_squares(f, p):
                dve.wait_ge(x_in[p], 32 * (f - p) + 64)
                at_least(dve, summed, f)
                nc.vector.tensor_tensor(sq[:, :, :], XC[p][:, :, :], XC[p][:, :, :], ALU.mult).then_inc(squared, 1)
                dve.wait_ge(squared, f + 1)
                nc.vector.tensor_reduce(ss[:, :], sq[:, :, :], AX.X, ALU.add).then_inc(summed, 1)
                dve.wait_ge(summed, f + 1)
                at_least(dve, rstd_ready, f)
                nc.vector.tensor_scalar(ms[:, :], ss[:, :], 1.0 / H, EPS0, ALU.mult, ALU.add).then_inc(mean_ready, 1)

            def step(t, p):
                if active(t + 1):
                    mask_max(t + 1, 1 - p)
                    normalise(t + 1)
                if active(t - 1):
                    silu(t - 1)
                if active(t + 2):
                    rope(t + 2)
                if active(t):
                    residual(t, p)
                if active(t + 3):
                    mean_squares(t + 3, 1 - p)

            for p in range(2):
                last = nc.vector.memset(XC[p][:, :, :], 0.0)
            last.then_inc(pads, 1)
            nc.vector.memset(KT[:, :, :, :], 0.0).then_inc(pads, 1)
            step(-3, 1)
            dve.wait_ge(w_first, 16 * 5)
            nc.vector.tensor_scalar(wq[:, :], wq[:, :], lns[:, 0:1], None, ALU.mult)
            nc.vector.tensor_scalar(wkv[:, :], wkv[:, :], lns[:, 0:1], None, ALU.mult)
            nc.vector.tensor_scalar(rope_q[:, :], rope_q[:, :], SCALE, None, ALU.mult).then_inc(w_scaled, 1)
            dve.wait_ge(w_high, 1)
            nc.vector.tensor_tensor(wqs[1][:, :], wq[:, :], wqs[0][:, :], ALU.subtract)
            nc.vector.tensor_tensor(wkvs[1][:, :], wkv[:, :], wkvs[0][:, :], ALU.subtract).then_inc(w_split, 1)
            step(-2, 0)
            step(-1, 1)
            dve.wait_ge(w_rest, 16 * 3)
            nc.vector.tensor_scalar(wgu[:, :], wgu[:, :], lns[:, 1:2], None, ALU.mult)
            nc.vector.tensor_scalar(wd[:, :, :], wd[:, :, :], 0.5, None, ALU.mult).then_inc(w_scaled, 1)
            steady_and_last(dve, step)

        @block.gpsimd
        def _(pool):
            def centre(f):
                for k in range(2):
                    pool.wait_ge(s_max, 2 * f + k + 1)
                    nc.gpsimd.tensor_tensor(P[:, 8 * k:8 * k + 8, :], P[:, 8 * k:8 * k + 8, :],
                                            bcast_last(MX[:, 8 * k:8 * k + 8], C), ALU.subtract).then_inc(s_centred, 1)

            def rope_cos(f):
                pool.wait_ge(q_out, 2 * (f + 1))
                at_least(pool, qt_ready, 2 * f)
                nc.gpsimd.tensor_tensor(QA[:, :, :], QE[:, :].rearrange("p (n d) -> p n d", d=D), bcast_mid(rope_q[:, 0:D], NH),
                                        ALU.mult).then_inc(q_cos, 1)

            def rope_keys(f):
                pool.wait_ge(kv_out, f + 1)
                at_least(pool, kt_ready, f)
                at_least(pool, k_roped, f)
                k = KS[:, :].rearrange("c (g d) -> c g d", d=D)
                ka = KA[:, :].rearrange("c (g d) -> c g d", d=D)
                kb = KB[:, :].rearrange("c (g d) -> c g d", d=D)
                h = D // 2
                nc.gpsimd.tensor_tensor(ka, k, bcast_mid(rope_k[:, 0:D], GKV), ALU.mult)
                nc.gpsimd.tensor_tensor(kb[:, :, 0:h], k[:, :, h:], bcast_mid(rope_k[:, D:D + h], GKV), ALU.mult)
                nc.gpsimd.tensor_tensor(kb[:, :, h:], k[:, :, 0:h], bcast_mid(rope_k[:, D + h:], GKV), ALU.mult).then_inc(k_parts, 1)
                pool.wait_ge(k_parts, f + 1)
                nc.gpsimd.tensor_tensor(KA[:, :], KA[:, :], KB[:, :], ALU.add).then_inc(k_roped, 1)

            def rstd_x(f, p):
                pool.wait_ge(mean_ready, f + 1)
                at_least(pool, kv_out, f - 1)
                at_least(pool, q_out, 2 * (f - 1))
                nc.gpsimd.tensor_tensor(rstd[p][:, :], ms[:, :], halfneg[:, 0:2], ALU.pow).then_inc(rstd_ready, 1)

            def split_low(f, p):
                pool.wait_ge(x_high, f + 1)
                nc.gpsimd.tensor_tensor(XS[p][1][:, :], XT[p][:, :], XS[p][0][:, :], ALU.subtract)
                nc.gpsimd.tensor_tensor(CS[p][1][:, :], CT[p][:, :], CS[p][0][:, :], ALU.subtract).then_inc(x_split, 1)

            def rstd_mlp(m):
                pool.wait_ge(mean2_ready, m + 1)
                at_least(pool, hn_ready, m)
                nc.gpsimd.tensor_tensor(rs2[:, :], ms2[:, :], halfneg[:, 0:1], ALU.pow).then_inc(rstd2_ready, 1)

            def step(t, p):
                if active(t + 1):
                    centre(t + 1)
                if active(t + 2):
                    rope_keys(t + 2)
                    rope_cos(t + 2)
                if active(t):
                    rstd_mlp(t)
                if active(t + 3):
                    rstd_x(t + 3, 1 - p)
                    split_low(t + 3, 1 - p)

            step(-3, 1)
            pool.wait_ge(w_first, 16 * 5)
            pool.wait_ge(w_scaled, 1)
            step(-2, 0)
            step(-1, 1)
            steady_and_last(pool, step)


def prepare1(nc, d, t, ident, ones, ps):
    MT, GM, WT, U, DW, DC, ctxT = (t[n] for n in ("MT", "GM", "WT", "U", "DW", "DC", "ctxT"))
    with ExitStack() as ctx:
        def sb(name, shape, dt=F32):
            return ctx.enter_context(nc.sbuf_tensor("pr_" + name, shape, dt))

        def sem(name):
            return ctx.enter_context(nc.semaphore("pr_" + name))

        wqT, wkT, wr, pos, small, w_in = (t[n] for n in ("wqT", "wkT", "wr1", "pos", "small", "later_in"))
        cb, pb, sbias, se0, se1 = (small[:, k, :] for k in range(5))
        RB = sb("RB", [128, CC, 2, J + 1])
        PB = sb("PB", [128, CC, 2, J + 2])
        WB = sb("WB", [128, CC, 2, H + 1])
        dse = sb("dse", [128, CC])
        zeroed, dse_ready, rb_ready, pb_ready, wb_ready = (sem(n) for n in ("zeroed", "dse_ready", "rb_ready", "pb_ready", "wb_ready"))
        r_ready, r_out, rp_out, g_ready, g_out = (sem(n) for n in ("r_ready", "r_out", "rp_out", "g_ready", "g_out"))
        w_ready, w_out, m_ready, m_out, u_ready, consts = (sem(n) for n in ("w_ready", "w_out", "m_ready", "m_out", "u_ready", "consts"))
        halves = [(u, slice(64 * u, 64 * u + 64)) for u in range(2)]
        block = ctx.enter_context(nc.Block())

        @block.tensor
        def _(pe):
            pe.wait_ge(w_in, 16 * LATER)
            for c in range(CC):
                nc.tensor.matmul(ps[:, c, 0:J], wr[:, c * 128:(c + 1) * 128], pos[:, :], start=True, stop=True).then_inc(r_ready, 1)
            pe.wait_ge(rb_ready, 1)
            for c in range(CC):
                pe.wait_ge(r_out, c + 1)
                pe.wait_ge(rp_out, c + 1)
                nc.tensor.matmul(ps[:, c, 0:2 * (J + 1)], wqT[:, c, :], RB[:, c, :, :].rearrange("p u j -> p (u j)"),
                                 start=True, stop=True).then_inc(g_ready, 1)
            pe.wait_ge(pb_ready, 1)
            for c in range(CC):
                pe.wait_ge(g_out, c + 1)
                nc.tensor.matmul(ps[:, c, 0:2 * (J + 2)], ones[:, :], PB[:, c, :, :].rearrange("p u j -> p (u j)"),
                                 start=True, stop=True).then_inc(w_ready, 1)
            pe.wait_ge(wb_ready, 1)
            for c in range(CC):
                pe.wait_ge(w_out, c + 1)
                nc.tensor.matmul(ps[:, c, 0:2 * (H + 1)], wkT[:, c, :], WB[:, c, :, :].rearrange("p u h -> p (u h)"),
                                 start=True, stop=True).then_inc(m_ready, 1)
            pe.wait_ge(m_out, CC)
            for c in range(CW1):
                o = ps[:, c // 26, (c % 26) * NH:(c % 26 + 1) * NH]
                if c > 0:
                    mm = nc.tensor.matmul(o[0:64, :], ctxT[:, :, c - 1], MT[:, :, H], start=True, stop=True)
                if c < C:
                    mm = nc.tensor.matmul(o[64:128, :], ctxT[:, :, c], MT[:, :, H], start=True, stop=True)
                if c % 26 == 25:
                    mm.then_inc(u_ready, 1)

        @block.scalar
        def _(act):
            act.wait_ge(w_in, 16 * LATER)
            act.wait_ge(zeroed, 1)
            for c in range(CC):
                act.wait_ge(r_out, c + 1)
                for u, h in halves:
                    last = nc.scalar.activation(PB[h, c, u, 0:J], ps[h, c, 0:J], ACT.Copy, scale=pb[h, c:c + 1])
                last.then_inc(rp_out, 1)
            for c in range(CC):
                act.wait_ge(w_ready, c + 1)
                nc.scalar.activation(WT[:, 2 * c:2 * c + 2, :], ps[:, c, 0:2 * (J + 2)].rearrange("p (u j) -> p u j", u=2),
                                     ACT.Copy, scale=SCALE).then_inc(w_out, 1)

        @block.vector
        def _(dve):
            nc.vector.memset(RB[:, :, :, :], 0.0).then_inc(consts, 1)
            dve.wait_ge(w_in, 16 * LATER)
            nc.vector.tensor_tensor(dse[:, :], se1, se0, ALU.subtract).then_inc(dse_ready, 1)
            dve.wait_ge(dse_ready, 1)
            dve.wait_ge(consts, 1)
            for u, h in halves:
                last = nc.vector.tensor_copy(RB[h, :, u, J], dse[h, :])
            last.then_inc(rb_ready, 1)
            for c in range(CC):
                dve.wait_ge(r_ready, c + 1)
                for u, h in halves:
                    last = nc.vector.tensor_scalar(RB[h, c, u, 0:J], ps[h, c, 0:J], se0[h, c:c + 1], None, ALU.add)
                last.then_inc(r_out, 1)
            for c in range(CC):
                dve.wait_ge(g_ready, c + 1)
                nc.vector.tensor_scalar(GM[:, 2 * c:2 * c + 2, :], ps[:, c, 0:2 * (J + 1)].rearrange("p (u j) -> p u j", u=2),
                                        SCALE, None, ALU.mult).then_inc(g_out, 1)
            for c in range(CC):
                dve.wait_ge(m_ready, c + 1)
                nc.vector.tensor_scalar(MT[:, 2 * c:2 * c + 2, :], ps[:, c, 0:2 * (H + 1)].rearrange("p (u h) -> p u h", u=2),
                                        SCALE, None, ALU.mult).then_inc(m_out, 1)
            dve.wait_ge(g_out, CC)
            dve.wait_ge(w_out, CC)
            nc.vector.tensor_copy(DW[:, :], GM[:, :, J])
            nc.vector.tensor_copy(DC[:, :], WT[:, :, J + 1])
            nc.vector.tensor_tensor(WT[:, :, 0:J], WT[:, :, 0:J], bcast_last(WT[:, :, J], J), ALU.add).then_inc(consts, 1)
            dve.wait_ge(zeroed, 2)
            for k in range(3):
                dve.wait_ge(u_ready, k + 1)
                for lo, hi, first, last in ((64, 128, 0, C), (0, 64, 1, CW1)):
                    a, z = max(first, 26 * k), min(last, 26 * k + 26)
                    nc.vector.tensor_copy(U[lo:hi, :, a:z], ps[lo:hi, k, (a - 26 * k) * NH:(z - 26 * k) * NH]
                                          .rearrange("p (c n) -> p n c", n=NH)).then_inc(consts, 1)

        @block.gpsimd
        def _(pool):
            nc.gpsimd.memset(PB[:, :, :, :], 0.0).then_inc(zeroed, 1)
            nc.gpsimd.memset(WB[:, :, :, :], 0.0)
            nc.gpsimd.memset(U[:, :, :], 0.0).then_inc(zeroed, 1)
            pool.wait_ge(zeroed, 2)
            pool.wait_ge(w_in, 16 * LATER)
            pool.wait_ge(dse_ready, 1)
            for u, h in halves:
                nc.gpsimd.tensor_tensor(PB[h, :, u, J], sbias[h, :], se0[h, :], ALU.mult)
                last = nc.gpsimd.tensor_tensor(PB[h, :, u, J + 1], sbias[h, :], dse[h, :], ALU.mult)
            last.then_inc(pb_ready, 1)
            for u, h in halves:
                nc.gpsimd.tensor_copy(WB[h, :, u, 0:H], wqT[h, :, :])
                last = nc.gpsimd.tensor_copy(WB[h, :, u, H], cb[h, :])
            last.then_inc(wb_ready, 1)


def position_terms(nc, t, bd, x1T, ps):
    GM, WT, U = t["GM"], t["WT"], t["U"]
    with ExitStack() as ctx:
        def sb(name, shape, dt=F32):
            return ctx.enter_context(nc.sbuf_tensor("pt_" + name, shape, dt))

        def sem(name):
            return ctx.enter_context(nc.semaphore("pt_" + name))

        xq = [sb(f"xq{p}", [128, 2, B]) for p in range(2)]
        ev = [sb(f"ev{j}", [128, NH, CW1]) for j in range(4)]
        xq_ready, g_ready, w_added, u_added, u_added_v = (sem(n) for n in ("xq_ready", "g_ready", "w_added", "u_added", "u_added_v"))
        stored = [sem(f"stored{j}") for j in range(4)]
        POOL_HEADS = BANKS[1][1]
        block = ctx.enter_context(nc.Block())

        def loop(eng, step):
            for j in range(4):
                step(j, j)
            with eng.Fori(1, S // 8) as four:
                for j in range(4):
                    step(4 * four + j, j)

        @block.scalar
        def _(act):
            def step(k, j):
                at_least(act, g_ready, 3 * (k - 1))
                nc.scalar.copy(xq[j % 2][:, :, :], x1T[:, :, bass.ds(2 * k, 2)].rearrange("p b s -> p s b")).then_inc(xq_ready, 1)
            loop(act, step)

        @block.tensor
        def _(pe):
            def step(k, j):
                pe.wait_ge(xq_ready, k + 1)
                at_least(pe, w_added, 3 * (k - 1))
                for g, (a, z) in enumerate(BANKS):
                    nc.tensor.matmul(ps[:, 3 * (j % 2) + g, 0:(z - a) * CW1], xq[j % 2][:, :, :].rearrange("p s b -> p (s b)"),
                                     GM[:, a:z, bass.ds(S - 2 - 2 * k, CW1)], start=True, stop=True).then_inc(g_ready, 1)
            loop(pe, step)

        @block.vector
        def _(dve):
            def step(k, j):
                at_least(dve, stored[j], 8 * (k - j))
                for g, (a, z) in enumerate(BANKS):
                    dve.wait_ge(g_ready, 3 * k + g + 1)
                    nc.vector.tensor_tensor(ev[j][:, a:z, :], ps[:, 3 * (j % 2) + g, 0:(z - a) * CW1].rearrange("p (n c) -> p n c", c=CW1),
                                            WT[:, a:z, bass.ds(S - 2 - 2 * k, CW1)], ALU.add).then_inc(w_added, 1)
                dve.wait_ge(w_added, 3 * k + 3)
                nc.vector.tensor_tensor(ev[j][:, POOL_HEADS:, :], ev[j][:, POOL_HEADS:, :], U[:, POOL_HEADS:, :], ALU.add) \
                    .then_inc(u_added_v, 1)
            loop(dve, step)

        @block.gpsimd
        def _(pool):
            def step(k, j):
                pool.wait_ge(w_added, 3 * k + 2)
                nc.gpsimd.tensor_tensor(ev[j][:, 0:POOL_HEADS, :], ev[j][:, 0:POOL_HEADS, :], U[:, 0:POOL_HEADS, :], ALU.add) \
                    .then_inc(u_added, 1)
            loop(pool, step)

        @block.sync
        def _(sp):
            def step(k, j):
                dma_after(sp, u_added, k + 1)
                dma_after(sp, u_added_v, k + 1)
                for s in range(2):
                    sp.dma_start(bd[:, 2 * k + s, :], ev[j][64 * s:64 * s + 64, :, :].rearrange("b n c -> b (n c)")).then_inc(stored[j], 16)
            loop(sp, step)
            for j in range(4):
                sp.wait_ge(stored[j], 32 * (S // 8))


def layer1(nc, d, t, bd, out, x1T, ident, ps, halfneg):
    MT, DW, DC, ctxT = t["MT"], t["DW"], t["DC"], t["ctxT"]
    with ExitStack() as ctx:
        def sb(name, shape, dt=F32):
            return ctx.enter_context(nc.sbuf_tensor("l1_" + name, shape, dt))

        def sem(name):
            return ctx.enter_context(nc.semaphore("l1_" + name))

        wv, wo, w1, w2, b1, rows, seg8, nm, w_in = (t[n] for n in ("wv1", "wo1", "w1", "w2", "b1", "rows", "seg", "cmask", "later_in"))
        seg = sb("seg", [128, C])
        XT = [sb(f"XT{p}", [128, S]) for p in range(2)]
        CS = [[sb(f"CS{p}{n}", [128, C], F32R) for n in "hl"] for p in range(2)]
        wvs = [sb(f"wv{n}", [128, NH * D], F32R) for n in "hl"]
        BD = [sb(f"BD{p}", [128, NH, CW1]) for p in range(2)]
        DS = sb("DS", [128, NH])
        T = sb("T", [128, NH, C])
        Z = [sb(f"folded{q}", [128, NH, 2, C]) for q in range(2)]
        X1 = [sb(f"X1{p}", [128, H]) for p in range(2)]
        VA = [sb(f"VA{p}", [C, NH, D]) for p in range(2)]
        P = sb("P", [128, NH, C])
        MX = sb("MX", [128, NH])
        PT = sb("PT", [C, NH, S])
        RS = sb("RS", [128, NH])
        AT = sb("AT", [128, CC, S])
        Y = sb("Y", [128, 2, H])
        st = sb("st", [128, 2, 6])
        mv = sb("mv", [128, 2, 2])
        ve = sb("ve", [128, 2])
        rs = sb("rs", [128, 2])
        NRM = sb("NRM", [128, 2, H])
        Z1 = sb("Z1", [128, H])
        ZB = [sb(f"ZB{p}", [128, H]) for p in range(2)]
        ZT = sb("ZT", [128, S])
        HT = sb("HT", [128, FC, S])
        OUT = [sb(f"OUT{p}", [128, H]) for p in range(2)]

        bd_in = [sem(f"bd_in{p}") for p in range(2)]
        stored = [sem(f"stored{p}") for p in range(2)]
        names = ("w_high w_split c_split seg_ready xt_ready dd_ready ds_ready t_seg bd_masked t_ready z_ready z_out v_ready v_out s_ready s_added s_max "
                 "s_centred p_ready pt_ready pt_out sum_ready sum_inv p_normed pv_ready at_out wo_ready "
                 "y_ready stat1 var1 rstd1 nrm1 z1_ready zb_ready zt_ready zt_out h_ready ht_out down_ready "
                 "w_ready stat2 var2 rstd2 nrm2 out_ready").split()
        e = {n: sem(n) for n in names}
        block = ctx.enter_context(nc.Block())


        @block.sync
        def _(sp):
            def load(b, p):
                dma_after(sp, e["t_ready"], b - 1)
                v = bd[b, :, :].rearrange("(k s) e -> s k e", s=2)
                for s in range(2):
                    w = NH * CW1 - 1
                    sp.dma_start(BD[p][s:128:2, :, :].rearrange("q n c -> q (n c)")[:, 0:w], v[s, :, 1 - s:1 - s + w]).then_inc(bd_in[p], 16)

            load(0, 0)
            load(1, 1)
            def store(b, p):
                dma_after(sp, e["out_ready"], b + 1)
                sp.dma_start(out[b, :, :], OUT[p][:, :]).then_inc(stored[p], 16)

            def step(b, p):
                load(b, p)
                store(b - 5, 1 - p)
            for b in range(2, 5):
                load(b, b % 2)
            step(5, 1)
            by_pairs(sp, 6, B, step)
            for b in range(B - 5, B):
                store(b, b % 2)
            for p in range(2):
                sp.wait_ge(stored[p], 16 * (B // 2))

        @block.tensor
        def _(pe):
            def rows_and_segments(f, p):
                at_least(pe, e["zt_out"], f - 1)
                at_least(pe, e["ds_ready"], f + 1)
                if active(f):
                    mm = nc.tensor.transpose(ps[:, 3, 128:256], XT[p][:, :], ident[:, :])
                if active(f + 1):
                    pe.wait_ge(e["xt_ready"], f + 2)
                    mm = nc.tensor.matmul(ps[:, 3, 0:NH], XT[1 - p][:, :], DW[:, :], start=True, stop=True)
                mm.then_inc(e["dd_ready"], 1)

            def fold_context(f, part):
                at_least(pe, e["s_added"], 3 * (f - 1 + part))
                if part == 1:
                    pe.wait_ge(e["z_out"], 3 * f + 3)
                for k in range(3):
                    a, z = Z_HEADS[3 * part + k]
                    for n in range(a, z):
                        w = 2 * C
                        mm = nc.tensor.matmul(ps[:, k, (n - a) * w:(n - a + 1) * w], MT[:, n, 0:H],
                                              ctxT[:, bass.ds(f, 2), :].rearrange("p b c -> p (b c)"), start=True, stop=True)
                    mm.then_inc(e["z_ready"], 1)

            def scores(f, p, q):
                if p == 0 or active(f + 1):
                    pe.wait_ge(e["z_out"], 3 * f + 6)
                else:
                    pe.wait_ge(e["s_added"], 3 * f)
                for k, (a, z) in enumerate(BANKS):
                    nc.tensor.matmul(ps[:, k, 0:(z - a) * C], XT[p][:, :], Z[q][:, a:z, p, :],
                                     start=True, stop=True).then_inc(e["s_ready"], 1)

            def values(f, p):
                at_least(pe, e["at_out"], 2 * f)
                pe.wait_ge(e["c_split"], f + 1)
                for k in range(2):
                    product_of_parts(nc, ps[0:C, 4 + k, :], [a[:, :] for a in CS[p]], [w[:, k * 512:(k + 1) * 512] for w in wvs]) \
                        .then_inc(e["v_ready"], 1)

            def transpose_probs(m):
                pe.wait_ge(e["ds_ready"], m + 2)
                for g, bank in enumerate((3, 4, 5, 3)):
                    pe.wait_ge(e["p_normed"], 3 * m + min(g + 1, 3))
                    if g == 1:
                        pe.wait_ge(e["v_out"], 2 * (m + 1))
                    if g == 3:
                        pe.wait_ge(e["pt_out"], 4 * m + 1)
                    for n in range(4 * g, 4 * g + 4):
                        mm = nc.tensor.transpose(ps[0:C, bank, (n % 4) * S:(n % 4 + 1) * S], P[:, n, :], ident[:, :])
                    mm.then_inc(e["pt_ready"], 1)

            def weigh_values(m, p, k):
                pe.wait_ge(e["pt_out"], 4 * m + 2 + 2 * k)
                for c in range(4 * k, 4 * k + 4):
                    for u in range(2):
                        mm = nc.tensor.matmul(ps[64 * u:64 * u + 64, 4 + k, (c % 4) * S:(c % 4 + 1) * S], VA[p][:, 2 * c + u, :],
                                              PT[:, 2 * c + u, :], start=True, stop=True)
                mm.then_inc(e["pv_ready"], 1)

            def project_out(m):
                pe.wait_ge(e["at_out"], 2 * (m + 1))
                at_least(pe, e["w_ready"], m - 1)
                for c in range(CC):
                    mm = nc.tensor.matmul(ps[:, 7, 0:H], AT[:, c, :], wo[:, c, :], start=(c == 0), stop=(c == CC - 1))
                mm.then_inc(e["wo_ready"], 1)

            def transpose_normed(b):
                pe.wait_ge(e["z1_ready"], b + 1)
                nc.tensor.transpose(ps[:, 3, 0:S], Z1[:, :], ident[:, :]).then_inc(e["zt_ready"], 1)

            def up(b):
                pe.wait_ge(e["zt_out"], b + 1)
                at_least(pe, e["ht_out"], b)
                for k in range(FC):
                    mm = nc.tensor.matmul(ps[:, 6, k * S:(k + 1) * S], w1[:, k * 128:(k + 1) * 128], ZT[:, :], start=True, stop=True)
                mm.then_inc(e["h_ready"], 1)

            def down(b):
                pe.wait_ge(e["ht_out"], b + 1)
                pe.wait_ge(e["y_ready"], upto_last(b + 2))
                at_least(pe, e["w_ready"], b)
                for k in range(FC):
                    mm = nc.tensor.matmul(ps[:, 7, 0:H], HT[:, k, :], w2[:, k, :], start=(k == 0), stop=(k == FC - 1))
                mm.then_inc(e["down_ready"], 1)

            def step(t, j):
                p = j % 2
                if active(t):
                    transpose_probs(t)
                if active(t):
                    weigh_values(t, p, 0)
                    weigh_values(t, p, 1)
                if active(t - 1):
                    transpose_normed(t - 1)
                if active(t + 1):
                    scores(t + 1, 1 - p, (j + 1) % 4 // 2)
                if active(t + 1) or active(t + 2):
                    rows_and_segments(t + 1, 1 - p)
                if active(t - 2):
                    down(t - 2)
                if active(t - 1):
                    up(t - 1)
                if active(t + 1):
                    values(t + 1, 1 - p)
                if active(t):
                    project_out(t)
                if p == 1 and active(t + 3):
                    fold_context(t + 3, 0)
                if p == 0 and active(t + 2):
                    fold_context(t + 2, 1)

            pe.wait_ge(w_in, 16 * LATER)
            pe.wait_ge(e["w_split"], 1)
            for t in range(-3, 0):
                step(t, t % 4)
            steady_and_last_by_fours(pe, step)

        @block.scalar
        def _(act):
            def fetch(f, p):
                if not isinstance(f, int) or f >= 2:
                    act.wait_ge(e["dd_ready"], f)
                    act.wait_ge(e["v_ready"], 2 * (f - 1))
                nc.scalar.copy(XT[p][:, :], x1T[:, f, :])
                nc.scalar.copy(CS[p][0][:, :], ctxT[:, f, :]).then_inc(e["xt_ready"], 1)

            def fold_evict(f, part, q):
                if part == 0:
                    at_least(act, e["s_ready"], 3 * (f - 2))
                for k in range(3 * part, 3 * part + 3):
                    a, z = Z_HEADS[k]
                    act.wait_ge(e["z_ready"], 3 * f + k + 1)
                    nc.scalar.copy(Z[q][:, a:z, :, :].rearrange("p n b c -> p (n b c)"), ps[:, k % 3, 0:(z - a) * 2 * C]) \
                        .then_inc(e["z_out"], 1)

            def probs_evict(m):
                at_least(act, e["pv_ready"], 2 * m)
                for g, bank in enumerate((3, 4, 5, 3)):
                    act.wait_ge(e["pt_ready"], 4 * m + g + 1)
                    nc.scalar.copy(PT[:, 4 * g:4 * g + 4, :], ps[0:C, bank, :].rearrange("c (n q) -> c n q", n=4)).then_inc(e["pt_out"], 1)

            def attn_evict(m):
                at_least(act, e["wo_ready"], m)
                for k in range(2):
                    act.wait_ge(e["pv_ready"], 2 * m + k + 1)
                    nc.scalar.copy(AT[:, 4 * k:4 * k + 4, :], ps[:, 4 + k, :].rearrange("c (n q) -> c n q", n=4)).then_inc(e["at_out"], 1)

            def normed_evict(b):
                act.wait_ge(e["zt_ready"], b + 1)
                at_least(act, e["h_ready"], b)
                nc.scalar.copy(ZT[:, :], ps[:, 3, 0:S]).then_inc(e["zt_out"], 1)

            def exps(f):
                for k, (a, z) in enumerate(BANKS):
                    act.wait_ge(e["s_centred"], 3 * f + k + 1)
                    nc.scalar.activation(P[:, a:z, :], P[:, a:z, :], ACT.Exp).then_inc(e["p_ready"], 1)

            def relu(b):
                act.wait_ge(e["h_ready"], b + 1)
                at_least(act, e["down_ready"], b)
                for k in range(FC):
                    last = nc.scalar.activation(HT[:, k, :], ps[:, 6, k * S:(k + 1) * S], ACT.Relu, bias=b1[:, k:k + 1])
                last.then_inc(e["ht_out"], 1)

            def values_evict(f, p):
                at_least(act, e["pv_ready"], 2 * (f - 1))
                for k in range(2):
                    act.wait_ge(e["v_ready"], 2 * f + k + 1)
                    nc.scalar.copy(VA[p][:, 8 * k:8 * k + 8, :], ps[0:C, 4 + k, :].rearrange("c (n d) -> c n d", d=D)).then_inc(e["v_out"], 1)

            def step(t, j):
                p = j % 2
                if active(t):
                    probs_evict(t)
                    attn_evict(t)
                if active(t - 1):
                    normed_evict(t - 1)
                if active(t + 1):
                    exps(t + 1)
                if active(t - 1):
                    relu(t - 1)
                if active(t + 1):
                    values_evict(t + 1, 1 - p)
                if active(t + 3):
                    fetch(t + 3, 1 - p)
                if p == 1 and active(t + 3):
                    fold_evict(t + 3, 0, (j + 3) % 4 // 2)
                if p == 0 and active(t + 2):
                    fold_evict(t + 2, 1, (j + 2) % 4 // 2)

            act.wait_ge(w_in, 16 * LATER)
            nc.scalar.copy(wvs[0][:, :], wv[:, :]).then_inc(e["w_high"], 1)
            for t in range(-3, 0):
                step(t, t % 4)
            steady_and_last_by_fours(act, step)

        @block.vector
        def _(dve):
            def add_positions(f, p):
                dve.wait_ge(e["t_seg"], f + 1)
                dve.wait_ge(e["bd_masked"], f + 1)
                nc.vector.tensor_tensor(T[:, :, :], T[:, :, :], BD[p][:, :, 0:C], ALU.add).then_inc(e["t_ready"], 1)

            def add_max(f):
                at_least(dve, e["pt_ready"], 4 * f)
                at_least(dve, e["s_centred"], 3 * f)
                dve.wait_ge(e["t_ready"], f + 1)
                for k, (a, z) in enumerate(BANKS):
                    dve.wait_ge(e["s_ready"], 3 * f + k + 1)
                    nc.vector.tensor_tensor(P[:, a:z, :], ps[:, k, 0:(z - a) * C].rearrange("p (n c) -> p n c", c=C),
                                            T[:, a:z, :], ALU.add).then_inc(e["s_added"], 1)
                    dve.wait_ge(e["s_added"], 3 * f + k + 1)
                    nc.vector.tensor_reduce(MX[:, a:z], P[:, a:z, :], AX.X, ALU.max).then_inc(e["s_max"], 1)

            def rows_and_segments(f, p):
                dve.wait_ge(e["dd_ready"], f + 2)
                if active(f + 1):
                    at_least(dve, e["t_seg"], f + 1)
                    last = nc.vector.tensor_tensor(DS[:, :], ps[:, 3, 0:NH], DC[:, :], ALU.add)
                if active(f):
                    at_least(dve, e["y_ready"], f - 1)
                    last = nc.vector.tensor_copy(X1[p][:, :], ps[:, 3, 128:256])
                last.then_inc(e["ds_ready"], 1)

            def normalise(f, k):
                a, z = BANKS[k]
                dve.wait_ge(e["p_ready"], 3 * f + k + 1)
                at_least(dve, e["p_normed"], 3 * f)
                nc.vector.tensor_reduce(RS[:, a:z], P[:, a:z, :], AX.X, ALU.add).then_inc(e["sum_ready"], 1)
                dve.wait_ge(e["sum_ready"], 3 * f + k + 1)
                nc.vector.reciprocal(RS[:, a:z], RS[:, a:z]).then_inc(e["sum_inv"], 1)
                dve.wait_ge(e["sum_inv"], 3 * f + k + 1)
                nc.vector.tensor_tensor(P[:, a:z, :], P[:, a:z, :], bcast_last(RS[:, a:z], C), ALU.mult).then_inc(e["p_normed"], 1)

            def mlp_residual(b, p):
                dve.wait_ge(e["down_ready"], b + 1)
                dve.wait_ge(e["zb_ready"], b + 1)
                nc.vector.tensor_tensor(Y[:, 1, :], ps[:, 7, 0:H], ZB[p][:, :], ALU.add).then_inc(e["w_ready"], 1)

            def attn_residual(m, p):
                dve.wait_ge(e["wo_ready"], m + 1)
                nc.vector.tensor_tensor(Y[:, 0, :], ps[:, 7, 0:H], X1[p][:, :], ALU.add).then_inc(e["y_ready"], 1)

            def norms(m, p):
                which = [(k, b) for k, b in ((0, m), (1, m - 2)) if active(b)]
                stat, var, rstd, nrm = ([e[f"{n}{k + 1}"] for k in range(2)] for n in ("stat", "var", "rstd", "nrm"))
                for k, b in which:
                    dve.wait_ge((e["y_ready"], e["w_ready"])[k], b + 1)
                    at_least(dve, stat[k], 2 * b)
                    nc.vector.bn_stats(st[:, k, :], Y[:, k, :]).then_inc(stat[k], 1)
                for k, b in which:
                    dve.wait_ge(stat[k], 2 * b + 1)
                    dve.nop(nofuse=True)
                    nc.vector.bn_aggr(mv[:, k, :], st[:, k, :]).then_inc(stat[k], 1)
                for k, b in which:
                    dve.wait_ge(stat[k], 2 * b + 2)
                    nc.vector.tensor_scalar(ve[:, k:k + 1], mv[:, k, 1:2], EPS1, None, ALU.add).then_inc(var[k], 1)
                for k, b in which:
                    nc.vector.scalar_tensor_tensor(NRM[:, k, :], Y[:, k, :], mv[:, k, 0:1], rows[:, 3 * k, :],
                                                   ALU.subtract, ALU.mult).then_inc(nrm[k], 1)
                for k, b in which:
                    if k == 0:
                        at_least(dve, e["zt_ready"], b)
                        at_least(dve, e["zb_ready"], b)
                        to, done = Z1, e["z1_ready"]
                    else:
                        at_least(dve, stored[p], 8 * (b - p))
                        to, done = OUT[p], e["out_ready"]
                    dve.wait_ge(nrm[k], b + 1)
                    dve.wait_ge(rstd[k], b + 1)
                    nc.vector.scalar_tensor_tensor(to[:, :], NRM[:, k, :], rs[:, k:k + 1], rows[:, 3 * k + 1, :],
                                                   ALU.mult, ALU.add).then_inc(done, 1)

            def step(t, p):
                if active(t + 1):
                    add_max(t + 1)
                if active(t - 2):
                    mlp_residual(t - 2, p)
                if active(t + 1):
                    normalise(t + 1, 0)
                if active(t + 1) or active(t + 2):
                    rows_and_segments(t + 1, 1 - p)
                if active(t + 1):
                    normalise(t + 1, 1)
                    normalise(t + 1, 2)
                if active(t):
                    attn_residual(t, p)
                norms(t, p)
                if active(t + 2):
                    add_positions(t + 2, p)

            dve.wait_ge(w_in, 16 * LATER)
            dve.wait_ge(e["w_high"], 1)
            nc.vector.tensor_tensor(wvs[1][:, :], wv[:, :], wvs[0][:, :], ALU.subtract).then_inc(e["w_split"], 1)
            nc.vector.tensor_copy(seg[:, :], seg8[:, :])
            nc.vector.tensor_scalar(nm[:, :], nm[:, :], -1e30, None, ALU.mult).then_inc(e["seg_ready"], 1)
            for t in range(-3, 0):
                step(t, t % 2)
            steady_and_last(dve, step)

        @block.gpsimd
        def _(pool):
            def centre(f):
                for k, (a, z) in enumerate(BANKS):
                    pool.wait_ge(e["s_max"], 3 * f + k + 1)
                    nc.gpsimd.tensor_tensor(P[:, a:z, :], P[:, a:z, :], bcast_last(MX[:, a:z], C), ALU.subtract) \
                        .then_inc(e["s_centred"], 1)

            def segments(f):
                pool.wait_ge(e["ds_ready"], f + 1)
                at_least(pool, e["s_added"], 3 * f)
                nc.gpsimd.tensor_tensor(T[:, :, :], bcast_mid(seg[:, :], NH), bcast_last(DS[:, :], C), ALU.mult).then_inc(e["t_seg"], 1)

            def masked_positions(f, p):
                pool.wait_ge(bd_in[p], 16 * (f - p) + 32)
                nc.gpsimd.tensor_tensor(BD[p][:, :, 0:C], BD[p][:, :, 0:C], bcast_mid(nm[:, :], NH), ALU.add).then_inc(e["bd_masked"], 1)

            def rstd(k, b):
                pool.wait_ge(e[f"var{k + 1}"], b + 1)
                nc.gpsimd.tensor_tensor(rs[:, k:k + 1], ve[:, k:k + 1], halfneg[:, 0:1], ALU.pow).then_inc(e[f"rstd{k + 1}"], 1)

            def residual_bias(m, p):
                pool.wait_ge(e["z1_ready"], m + 1)
                at_least(pool, e["w_ready"], m - 1)
                nc.gpsimd.tensor_tensor(ZB[p][:, :], Z1[:, :], rows[:, 2, :], ALU.add).then_inc(e["zb_ready"], 1)

            def context_low(f, p):
                pool.wait_ge(e["xt_ready"], f + 1)
                nc.gpsimd.tensor_tensor(CS[p][1][:, :], ctxT[:, f, :], CS[p][0][:, :], ALU.subtract).then_inc(e["c_split"], 1)

            def step(t, p):
                if active(t + 1):
                    centre(t + 1)
                if active(t + 2):
                    segments(t + 2)
                if active(t):
                    rstd(0, t)
                if active(t - 2):
                    rstd(1, t - 2)
                if active(t):
                    residual_bias(t, p)
                if active(t + 3):
                    context_low(t + 3, 1 - p)
                    masked_positions(t + 3, 1 - p)

            pool.wait_ge(w_in, 16 * LATER)
            pool.wait_ge(e["seg_ready"], 1)
            for t in range(-3, 0):
                step(t, t % 2)
            steady_and_last(pool, step)


def build(nc, d, out):
    with ExitStack() as ctx:
        def sb(name, shape, dt=F32):
            return ctx.enter_context(nc.sbuf_tensor(name, shape, dt))

        ps = ctx.enter_context(nc.psum_tensor("ps", [128, 8, BANK], F32))
        bd = nc.dram_tensor("bd_scratch", [B, S, NH * CW1], F32, kind="Internal").ap()
        ident = sb("ident", [128, 128])
        ones = sb("ones", [128, 128])
        halfneg = sb("halfneg", [128, 2])
        x1T = sb("x1T", [128, B, S])
        c_in = ctx.enter_context(nc.semaphore("c_in"))
        with nc.Block() as block:
            @block.sync
            def _(sp):
                sp.dma_start(ident[:, :], d["ident"]).then_inc(c_in, 16)
                sp.wait_ge(c_in, 16)

            @block.vector
            def _(dve):
                nc.vector.memset(ones[:, :], 1.0)
                nc.vector.memset(halfneg[:, :], -0.5)
        t = {n: sb(n, shape, U8 if n == "seg" else F32) for n, shape in LATER_SHAPES.items()}
        t["later_in"] = ctx.enter_context(nc.semaphore("later_in"))

        def load_later(eng):
            for n, shape in LATER_SHAPES.items():
                eng.dma_start(t[n][tuple(slice(None) for _ in shape)], d[n].partition_broadcast(128) if n == "rows" else d[n]) \
                    .then_inc(t["later_in"], 16)

        layer0(nc, d, x1T, ident, ps, halfneg, load_later)
        t.update(MT=sb("MT", [128, NH, H + 1]), DW=sb("DW", [128, NH]), DC=sb("DC", [128, NH]))
        with nc.sbuf_tensor("GM", [128, NH, J + 1], F32) as GM, nc.sbuf_tensor("WT", [128, NH, J + 2], F32) as WT, \
                nc.sbuf_tensor("U", [128, NH, CW1], F32) as U:
            t.update(GM=GM, WT=WT, U=U)
            prepare1(nc, d, t, ident, ones, ps)
            position_terms(nc, t, bd, x1T, ps)
        layer1(nc, d, t, bd, out, x1T, ident, ps, halfneg)


def layouts(i):
    import numpy as np
    a = {k: np.asarray(v) for k, v in i.items()}
    L0, L1 = "L0_xattn_", "L1_xattn_"
    order = [8 * (s // 8) + 4 * (s % 2) + (s % 8) // 2 for s in range(NH)]
    d = {}
    d["x"] = a["x"]
    d["xT"] = a["x"].transpose(0, 2, 1)
    d["ctx"] = a["ctx_1024"]
    d["ctxT"] = a["ctx_1024"].transpose(2, 0, 1)
    d["mask"] = a["mask_Bx1xSxS2_ff0"].reshape(B, S, C)
    d["cmask"] = a["mask_1x1xSxS2_ff0"].reshape(S, C)
    d["seg"] = a["mask_1xSxS2_bk1"].reshape(S, C)
    d["wq0"] = a[L0 + "Wq"].reshape(H, NH, D)[:, order].reshape(H, NH * D)
    d["wkv0"] = np.concatenate([a[L0 + "Wk"], a[L0 + "Wv"]], axis=1)
    d["wo0"] = a[L0 + "Wo"].reshape(NH, D, H)[order].reshape(CC, 128, H).transpose(1, 0, 2)
    d["wgu"] = np.concatenate([a[L0 + "Wgate"], a[L0 + "Wup"]], axis=1)
    d["wd"] = a[L0 + "Wdown"].reshape(FC, 128, H).transpose(1, 0, 2)
    d["lns"] = np.stack([a[L0 + "ln1_w"], a[L0 + "ln2_w"]], axis=1)
    d["wqT"] = a[L1 + "Wq"].reshape(H, CC, 128).transpose(2, 1, 0)
    d["wkT"] = a[L1 + "Wk"].reshape(H, CC, 128).transpose(2, 1, 0)
    d["wr1"] = a[L1 + "Wr"].reshape(H, NH * D)
    d["pos"] = a[L1 + "position_encoding"][0, 1:J + 1].T
    small = [a[L1 + "content_bias"], a[L1 + "position_bias"], a[L1 + "segment_bias"],
             a[L1 + "segment_encoding"][0], a[L1 + "segment_encoding"][1]]
    d["small"] = np.stack([s.reshape(CC, 128).T for s in small], axis=1)
    d["wv1"] = a[L1 + "Wv"].reshape(H, NH * D)
    d["wo1"] = a[L1 + "Wo"].reshape(H, CC, 128).transpose(2, 1, 0)
    d["w1"] = a[L1 + "W1"]
    d["w2"] = a[L1 + "W2"].reshape(FC, 128, H).transpose(1, 0, 2)
    d["b1"] = a[L1 + "b1"].reshape(FC, 128).T
    d["rows"] = np.stack([a[L1 + n] for n in ("ln1_gamma", "ln1_beta", "b2", "ln2_gamma", "ln2_beta")])
    inv = (1.0 / 10000.0 ** (np.arange(0, D, 2, dtype=np.float32) / np.float32(D))).astype(np.float32)
    ang = np.arange(S, dtype=np.float32)[:, None] * inv[None, :]
    cos, sin = np.cos(ang), np.sin(ang)
    row = np.concatenate([cos, cos, -sin, sin], axis=1).astype(np.float32)
    d["rope"] = np.stack([row, row], axis=1)
    d["ident"] = np.eye(128, dtype=np.float32)
    return {k: np.ascontiguousarray(v) for k, v in d.items()}


def kernel(**inputs):
    import numpy as np
    import concourse.bacc as bacc
    from concourse.bass_utils import run_bass_kernel_spmd

    nc = bacc.Bacc("TRN2", target_bir_lowering=False, num_devices=1)
    arrays, d = {}, {}
    for name, a in layouts(inputs).items():
        arrays[f"in_{name}_dram"] = a
        d[name] = nc.dram_tensor(f"in_{name}_dram", a.shape, mybir.dt.from_np(a.dtype), kind="ExternalInput").ap()
    out = nc.dram_tensor("out_0_dram", (B, S, H), F32, kind="ExternalOutput").ap()
    build(nc, d, out)
    r = run_bass_kernel_spmd(nc, [arrays], core_ids=[0])
    return r.results[0]["out_0_dram"]
```
